# Optimizing a Trainium2 kernel written in Bass

```python
import numpy as np
import jax
import jax.numpy as jnp

def _softmax(x, axis=-1):
    return jax.nn.softmax(x, axis=axis)

def _gelu(x):
    return jax.nn.gelu(x, approximate=True)

def _silu(x):
    return jax.nn.silu(x)

def _sigmoid(x):
    return jax.nn.sigmoid(x)

def _layernorm(x, axis=-1, eps=1e-05):
    m = jnp.mean(x, axis=axis, keepdims=True)
    v = jnp.var(x, axis=axis, keepdims=True)
    return (x - m) / jnp.sqrt(v + eps)

def _scatter_add(tgt, idx, src, axis=0):
    return tgt.at[idx].add(src)

def _segment_sum(src, seg, n):
    return jax.ops.segment_sum(src, seg, n)
kernel_name = 'mk_perceiver_d1_seqx_r2_04b63a'

def setup_inputs(seed: int=0):
    np.random.seed(seed)
    _w = jnp.asarray

    def _rec_inputs():
        import jax
        import jax.numpy as jnp
        _rk = jax.random.key(seed)
        x = 7.22e-05 + 1 * jax.random.normal(jax.random.fold_in(_rk, 1), (2, 512, 512), jnp.float32)
        _lenS = 512 - jax.random.randint(jax.random.fold_in(_rk, 7), (2,), 0, max(1, 512 // 4) + 1, jnp.int32)
        _lenS2 = 8192 - jax.random.randint(jax.random.fold_in(_rk, 8), (2,), 0, max(1, 8192 // 4) + 1, jnp.int32)
        _ctx_1024P = jax.random.normal(jax.random.fold_in(_rk, 11), (2, 16, 512), jnp.float32)
        _ctx_1024c = jax.random.dirichlet(jax.random.fold_in(_rk, 511), 0.3 * jnp.ones((16,), jnp.float32), (2, 8192))
        _ctx_1024t = jnp.einsum('bsk,bkd->bsd', _ctx_1024c, _ctx_1024P)
        _ctx_1024t = _ctx_1024t * jax.lax.rsqrt(jnp.mean(jnp.square(_ctx_1024t)) + 1e-12) * 0.953939
        ctx_1024 = -4.77421e-07 + 0.031248 * (_ctx_1024t + 0.3 * jax.random.normal(jax.random.fold_in(_rk, 611), (2, 8192, 512), jnp.float32))
        return (x, ctx_1024)
    x, ctx_1024 = _rec_inputs()

    def _L0_xattn_setup():
        import jax, jax.numpy as jnp
        import numpy as np
        E, T, H, F = (8, 512, 512, 2048)
        key = jax.random.key(seed)
        k1, k2, k3 = jax.random.split(key, 3)
        x = jax.random.normal(k1, (E, T, H), dtype=jnp.float32)
        w1 = jax.random.normal(k2, (E, F, H), dtype=jnp.float32) * (1.0 / np.sqrt(H))
        w2 = jax.random.normal(k3, (E, F, H), dtype=jnp.float32) * (1.0 / np.sqrt(F))
        return {'x': x, 'w1': w1, 'w2': w2}
    _L0_xattn_all = _L0_xattn_setup()
    _L0_xattn_in = {k: v for k, v in _L0_xattn_all.items() if k in ()}
    del _L0_xattn_all

    def _L0_attn_setup():
        import jax, jax.numpy as jnp
        import numpy as np
        import math
        D_MODEL = 512
        N_HEADS = 16
        D_K = D_MODEL // N_HEADS
        BATCH = 4
        SEQ = 1024
        TRAINING_PROGRESS = 0.25
        CONVERGENCE_PHASE = 0.5
        TENSION = abs(1.0 - 1.0)

        def _pos_encoding(seq_len, d, yellow):
            phase_mod = 0.1 * math.sin(2.0 * math.pi * TRAINING_PROGRESS)
            i_even = jnp.arange(0, d, 2, dtype=jnp.float32)
            denom = jnp.power(10000.0, 2.0 * i_even / d) * (1.0 + yellow * phase_mod)
            pos = jnp.arange(seq_len, dtype=jnp.float32)
            ang = pos[:, None] / denom[None, :]
            pe = jnp.zeros((seq_len, d), jnp.float32)
            pe = pe.at[:, 0::2].set(jnp.sin(ang))
            pe = pe.at[:, 1::2].set(jnp.cos(ang))
            return pe
        key = jax.random.key(seed)
        ks = jax.random.split(key, 8)
        x = jax.random.normal(ks[0], (BATCH, SEQ, D_MODEL), dtype=jnp.float32)
        rby = jax.random.uniform(ks[1], (3,), dtype=jnp.float32)
        s = 0.02
        Wq = jax.random.normal(ks[2], (D_MODEL, D_MODEL), dtype=jnp.float32) * s
        Wk = jax.random.normal(ks[3], (D_MODEL, D_MODEL), dtype=jnp.float32) * s
        Wv = jax.random.normal(ks[4], (D_MODEL, D_MODEL), dtype=jnp.float32) * s
        Wo = jax.random.normal(ks[5], (D_MODEL, D_MODEL), dtype=jnp.float32) * s
        bq = jnp.zeros((D_MODEL,), jnp.float32)
        bk = jnp.zeros((D_MODEL,), jnp.float32)
        bv = jnp.zeros((D_MODEL,), jnp.float32)
        bo = jnp.zeros((D_MODEL,), jnp.float32)
        ln_gamma = jnp.ones((D_MODEL,), jnp.float32)
        ln_beta = jnp.zeros((D_MODEL,), jnp.float32)
        return {'x': x, 'rby': rby, 'Wq': Wq, 'bq': bq, 'Wk': Wk, 'bk': bk, 'Wv': Wv, 'bv': bv, 'Wo': Wo, 'bo': bo, 'ln_gamma': ln_gamma, 'ln_beta': ln_beta}
    _L0_attn_all = _L0_attn_setup()
    _L0_attn_in = {k: v for k, v in _L0_attn_all.items() if k in ('rby', 'Wq', 'bq', 'Wk', 'bk', 'Wv', 'bv', 'Wo', 'bo', 'ln_gamma', 'ln_beta')}
    del _L0_attn_all

    def _L0_ffn_setup():
        import jax, jax.numpy as jnp
        import numpy as np
        S, B, H, I, E = (256, 2, 512, 1408, 8)
        key = jax.random.key(seed)
        ks = jax.random.split(key, 5)
        return {'hidden_states': jax.random.normal(ks[0], (S, B, H), dtype=jnp.float32), 'router_w': jax.random.normal(ks[1], (E, H), dtype=jnp.float32) * 0.02, 'gate_w': jax.random.normal(ks[2], (E, I, H), dtype=jnp.float32) * 0.02, 'up_w': jax.random.normal(ks[3], (E, I, H), dtype=jnp.float32) * 0.02, 'down_w': jax.random.normal(ks[4], (E, H, I), dtype=jnp.float32) * 0.02}
    _L0_ffn_all = _L0_ffn_setup()
    _L0_ffn_in = {k: v for k, v in _L0_ffn_all.items() if k in ('router_w', 'gate_w', 'up_w', 'down_w')}
    del _L0_ffn_all
    return {'x': x, 'ctx_1024': ctx_1024, 'L0_attn_rby': _L0_attn_in['rby'], 'L0_attn_Wq': _L0_attn_in['Wq'], 'L0_attn_bq': _L0_attn_in['bq'], 'L0_attn_Wk': _L0_attn_in['Wk'], 'L0_attn_bk': _L0_attn_in['bk'], 'L0_attn_Wv': _L0_attn_in['Wv'], 'L0_attn_bv': _L0_attn_in['bv'], 'L0_attn_Wo': _L0_attn_in['Wo'], 'L0_attn_bo': _L0_attn_in['bo'], 'L0_attn_ln_gamma': _L0_attn_in['ln_gamma'], 'L0_attn_ln_beta': _L0_attn_in['ln_beta'], 'L0_ffn_router_w': _L0_ffn_in['router_w'], 'L0_ffn_gate_w': _L0_ffn_in['gate_w'], 'L0_ffn_up_w': _L0_ffn_in['up_w'], 'L0_ffn_down_w': _L0_ffn_in['down_w']}

def reference(x, ctx_1024, L0_attn_rby, L0_attn_Wq, L0_attn_bq, L0_attn_Wk, L0_attn_bk, L0_attn_Wv, L0_attn_bv, L0_attn_Wo, L0_attn_bo, L0_attn_ln_gamma, L0_attn_ln_beta, L0_ffn_router_w, L0_ffn_gate_w, L0_ffn_up_w, L0_ffn_down_w):
    import jax
    import jax.numpy as jnp

    def _L0_xattn_ref(x, w1, w2):
        import jax, jax.numpy as jnp
        import numpy as np
        E, T, H, F = (8, 512, 512, 2048)
        h = jnp.einsum('eth,efh->etf', x, w1)
        g = jax.nn.gelu(h, approximate=True)
        out = jnp.einsum('etf,efh->eth', g, w2)
        return out

    def _L0_attn_ref(x, rby, Wq, bq, Wk, bk, Wv, bv, Wo, bo, ln_gamma, ln_beta):
        import jax, jax.numpy as jnp
        import numpy as np
        import math
        D_MODEL = 512
        N_HEADS = 16
        D_K = D_MODEL // N_HEADS
        BATCH = 4
        SEQ = 1024
        TRAINING_PROGRESS = 0.25
        CONVERGENCE_PHASE = 0.5
        TENSION = abs(1.0 - 1.0)

        def _pos_encoding(seq_len, d, yellow):
            phase_mod = 0.1 * math.sin(2.0 * math.pi * TRAINING_PROGRESS)
            i_even = jnp.arange(0, d, 2, dtype=jnp.float32)
            denom = jnp.power(10000.0, 2.0 * i_even / d) * (1.0 + yellow * phase_mod)
            pos = jnp.arange(seq_len, dtype=jnp.float32)
            ang = pos[:, None] / denom[None, :]
            pe = jnp.zeros((seq_len, d), jnp.float32)
            pe = pe.at[:, 0::2].set(jnp.sin(ang))
            pe = pe.at[:, 1::2].set(jnp.cos(ang))
            return pe
        B, S, d = x.shape
        red, blue, yellow = (rby[0], rby[1], rby[2])
        x = x + _pos_encoding(S, d, yellow)[None, :, :]

        def proj(W, b):
            return (x @ W.T + b).reshape(B, S, N_HEADS, D_K).transpose(0, 2, 1, 3)
        Q, K, V = (proj(Wq, bq), proj(Wk, bk), proj(Wv, bv))
        scale = jnp.sqrt(D_K * (1.0 + TENSION * red))
        logits = jnp.einsum('bhqd,bhkd->bhqk', Q, K) / scale
        scale_matrix = 1.0 + red * 0.1 + blue * 0.05 + yellow * 0.15
        logits = logits * scale_matrix
        attn = jax.nn.softmax(logits, axis=-1)
        eps_adaptive = 0.1 * math.sin(2.0 * math.pi * CONVERGENCE_PHASE)
        out = jnp.einsum('bhqk,bhkd->bhqd', attn, V) * (1.0 + yellow * eps_adaptive)
        out = out.transpose(0, 2, 1, 3).reshape(B, S, d)
        out = out @ Wo.T + bo
        x = x + out
        mean = jnp.mean(x, axis=-1, keepdims=True)
        var = jnp.var(x, axis=-1, keepdims=True)
        eps_rby = 1e-05 * (1.0 + blue * 0.1)
        gamma_rby = ln_gamma * (1.0 + red * 0.1 + yellow * 0.05)
        normalized = (x - mean) / jnp.sqrt(var + eps_rby)
        return normalized * gamma_rby + ln_beta

    def _L0_ffn_ref(hidden_states, router_w, gate_w, up_w, down_w):
        import jax, jax.numpy as jnp
        import numpy as np
        S, B, H, I, E = (256, 2, 512, 1408, 8)
        router_logits = jnp.einsum('sbh,eh->sbe', hidden_states, router_w)
        routing_indices = jnp.argmax(router_logits, axis=-1)
        out = jnp.zeros_like(hidden_states)
        for e in range(E):
            mask = (routing_indices == e)[..., None]
            xe = jnp.where(mask, hidden_states, 0.0)
            g = jnp.einsum('sbh,ih->sbi', xe, gate_w[e])
            u = jnp.einsum('sbh,ih->sbi', xe, up_w[e])
            ye = jnp.einsum('sbi,hi->sbh', jax.nn.silu(g) * u, down_w[e])
            out = out + jnp.where(mask, ye, 0.0)
        return out
    x = x + _L0_xattn_ref(_layernorm(x, axis=-1), ctx_1024, ctx_1024)
    x = x + _L0_attn_ref(_layernorm(x, axis=-1), L0_attn_rby, L0_attn_Wq, L0_attn_bq, L0_attn_Wk, L0_attn_bk, L0_attn_Wv, L0_attn_bv, L0_attn_Wo, L0_attn_bo, L0_attn_ln_gamma, L0_attn_ln_beta)
    x = x + _L0_ffn_ref(_layernorm(x, axis=-1), L0_ffn_router_w, L0_ffn_gate_w, L0_ffn_up_w, L0_ffn_down_w)
    return x

_drawn_inputs = setup_inputs


def setup_inputs(seed=0):
    import zlib

    import numpy as np

    out = dict(_drawn_inputs(seed))
    spreads = {'L0_attn_bq': (0.0, 0.8),
     'L0_attn_bk': (0.0, 0.8),
     'L0_attn_bv': (0.0, 0.8),
     'L0_attn_bo': (0.0, 0.8),
     'L0_attn_ln_gamma': (1.0, 0.6),
     'L0_attn_ln_beta': (0.0, 0.8)}
    factors = {'L0_attn_rby': 7.862,
     'L0_attn_Wq': 8.0,
     'L0_attn_Wk': 8.0,
     'L0_attn_Wv': 8.0,
     'L0_attn_Wo': 8.0,
     'L0_ffn_router_w': 8.0,
     'L0_ffn_gate_w': 8.0,
     'L0_ffn_up_w': 8.0,
     'L0_ffn_down_w': 8.0}
    for name, (base, spread) in spreads.items():
        noise = np.random.default_rng([zlib.crc32(name.encode()), seed]).standard_normal(out[name].shape)
        drawn = base * np.exp(spread * noise) if base else spread * noise
        out[name] = jnp.asarray(drawn.astype(out[name].dtype))
    for name, factor in factors.items():
        out[name] = (out[name] * factor).astype(out[name].dtype)
    return out
```

```python
import math
import numpy as np
import concourse.bass as bass
from concourse import mybir
from contextlib import ExitStack

F32 = mybir.dt.float32
F32R = mybir.dt.float32r
I32 = mybir.dt.int32
ALU = mybir.AluOpType
ACT = mybir.ActivationFunctionType
AX = mybir.AxisListType

P = 128
B, T, D = 2, 512, 512
KT = D // P
TT = T // P
NT = B * TT
F = 8192
GT = 4
NG = F // (GT * P)
NF = B * F // P
RING = 8
GRING = 4
AHEAD = 4
PE_LAG = 2
LN_EPS = 1e-5

H, DH = 16, 32
HG = P // DH
NGRP = H // HG
GH = HG * B
PHASE_MOD = 0.1 * math.sin(2.0 * math.pi * 0.25)
EPS_ADAPTIVE = 0.1 * math.sin(2.0 * math.pi * 0.5)
E, FF = 8, 1408
FT = FF // P
CH = [4, 4, 3]
assert sum(CH) == FT
NB = (B * T + E * (P - 1)) // P
PIECES = [("g", 0), ("u", 0), ("d", 2), ("g", 1), ("u", 1), ("d", 0), ("g", 2), ("u", 2), ("d", 1)]
EARLY = [pc for pc in PIECES if pc != ("d", 2)]
RAW = 3
assert len(PIECES) % RAW == 0
TWO_PI = 2.0 * math.pi
PI_A = 6.28125
PI_B = float(np.float32(0.0019352436065673828))
PI_C = TWO_PI - PI_A - PI_B
ROUND = 1.5 * 2.0 ** 23
C_POS, C_POW, C_TRI = P, P + TT, P + TT + D // 2
C_ONE = C_TRI + P
C_DEC = C_ONE + P
C_END = C_DEC + E + E + NB

FULL_BODY = ["turn"]
for _s in range(GH):
    FULL_BODY += [(_s + 2, 0), (_s + 2, 1)] + {1: ["Q"], 2: ["K"], 3: ["V"]}.get(_s, [])
LAST_BODY = ["turn"] + [(_s + 2, _p) for _s in range(GH - 2) for _p in range(2)]
PER_BODY = len(FULL_BODY)
assert PER_BODY % 2 == 0
FIRST_USES = {"Q": 1, "K": 2, "V": 3}
BODY0 = 2 * 2 + len(FIRST_USES) + 1


def use(grp, what, last=False):
    if isinstance(what, tuple) and what[0] < 2:
        return (grp - 1) * PER_BODY + (BODY0 + FULL_BODY.index((what[0] + GH, what[1])))
    return grp * PER_BODY + (BODY0 + (LAST_BODY if last else FULL_BODY).index(what))


def slot_of(what, last=False):
    if isinstance(what, tuple) and what[0] < 2:
        return (BODY0 + FULL_BODY.index((what[0] + GH, what[1]))) % 2
    return (BODY0 + (LAST_BODY if last else FULL_BODY).index(what)) % 2


def reads(grp, what, last=False):
    prev = isinstance(what, tuple) and what[0] < 2
    order = FULL_BODY if prev or not last else LAST_BODY
    at = BODY0 + order.index((what[0] + GH, what[1]) if prev else what)
    return (grp - 1 if prev else grp) * (PER_BODY // 2) + (at + at % 2) // 2


FAC_STEPS = 10


def first_reads(u):
    return (u + u % 2) // 2


def build(nc, x, ctx_nat, ctx_tr, consts, rby, w_qkv, b_qkv, w_o, rows, router, ffn0, ffn1, ffn2, out):
    ctx = ExitStack()
    with ctx:
        top = [(nc.sbuf_base + 31) // 32 * 32]

        def place(name, shape, dt, at=None):
            size = int(np.prod(shape[1:])) * 4
            if at is None:
                at = top[0]
                top[0] += (size + 31) // 32 * 32
            t = nc.alloc_sbuf_tensor_at(name, shape, dt, offset=at)
            return t

        def sem(name):
            return ctx.enter_context(nc.semaphore(name))

        z_slots = nc.dram_tensor("z_slots", (NB * P, D), F32).ap()
        y_slots = nc.dram_tensor("y_slots", (NB * P, D), F32).ap()

        ident = place("ident", [P, P], F32)
        zero = place("zero", [P, D], F32)
        tok = place("tok", [P, NT, D], F32)
        stats = place("stats", [P, NT, 6], F32)
        mv = place("mv", [P, NT, 2], F32)
        rstd = place("rstd", [P, NT], F32)
        mv2 = place("mv2", [P, NT, 2], F32)
        rstd2 = place("rstd2", [P, NT], F32)
        mv3 = place("mv3", [P, NT, 2], F32)
        rstd3 = place("rstd3", [P, NT], F32)
        mv4 = place("mv4", [P, NT, 2], F32)
        rstd4 = place("rstd4", [P, NT], F32)
        early_c = top[0]
        rby_all = place("rby_all", [P, 3], F32)
        fac = place("fac", [P, 8], F32)
        cst = place("cst", [P, TT + D // 2], F32)
        b_all = place("b_all", [P, 3, NGRP], F32)
        row_in = place("row_in", [P, 3, D], F32)
        w_raw = place("w_raw", [P, 3, KT, P], F32)
        pe_at = top[0]
        pe_tab = place("pe_tab", [P, TT, D], F32)
        wrap = place("wrap", [P, TT, D // 2], F32, pe_at)
        wrap2 = place("wrap2", [P, TT, D // 2], F32, pe_at + 4096)
        phase = top[0]

        norm = place("norm", [P, 2, D], F32)
        xT_hi = place("xT_hi", [P, KT, NT * P], F32R)
        xT_lo = place("xT_lo", [P, KT, NT * P], F32R)
        nat_raw = place("nat_raw", [P, 2, GT, D], F32)
        tr_raw = place("tr_raw", [P, 2, KT, GT * P], F32)
        cN_hi = place("cN_hi", [P, RING, D], F32R)
        cN_lo = place("cN_lo", [P, RING, D], F32R)
        cT_hi = place("cT_hi", [P, RING, KT, P], F32R)
        cT_lo = place("cT_lo", [P, RING, KT, P], F32R)
        g_full = place("g_full", [P, GRING, T], F32)
        g_hi = place("g_hi", [P, GRING, T], F32R)
        g_lo = place("g_lo", [P, GRING, T], F32R)
        ang = place("ang", [P, TT, D // 2], F32)
        ang2 = place("ang2", [P, TT, D // 2], F32)

        assert top[0] <= nc.sbuf_usable_end, top[0]
        top[0] = phase
        yT_at = top[0]
        yT_hi = place("yT_hi", [P, KT, NT * P], F32R)
        yT_lo = place("yT_lo", [P, KT, NT * P], F32R)
        wo_raw = place("wo_raw", [P, KT, D], F32, yT_at)
        wo_hi = place("wo_hi", [P, KT, D], F32R, yT_at + 8192)
        wo_lo = place("wo_lo", [P, KT, D], F32R, yT_at + 16384)
        w_hi = place("w_hi", [P, 3, KT, P], F32R)
        w_lo = place("w_lo", [P, 3, KT, P], F32R)
        qk_at = top[0]
        qk_hi = place("qk_hi", [P, 2, NT * P], F32R)
        qk_lo = place("qk_lo", [P, 2, NT * P], F32R)
        y_bo = place("y_bo", [P, NT, D], F32, qk_at)
        vT = place("vT", [P, NT * P], F32)
        v_tok = place("v_tok", [P, NT, P], F32)
        stack_at = top[0]
        q_st = place("q_st", [P, HG, NT * P], F32R)
        k_st = place("k_st", [P, HG, NT * P], F32R)
        xa = place("xa", [P, NT, D], F32, stack_at)
        xg = place("xg", [P, NT, D], F32, stack_at + 16384)
        prob_at = top[0]
        prob = place("prob", [P, 2, TT, T], F32)
        o_hi = place("o_hi", [P, 2, KT, P], F32R, prob_at)
        o_lo = place("o_lo", [P, 2, KT, P], F32R, prob_at + 4096)
        probT = place("probT", [P, 2, TT, T], F32)
        ynorm = place("ynorm", [P, 4, D], F32, prob_at + 16384)
        oT = place("oT", [P, KT, NT * P], F32)
        r_all = place("r_all", [P, B, T], F32)
        r_wide = place("r_wide", [P, B * TT, P], F32)
        sums = place("sums", [P, B, TT, HG], F32)
        recip = place("recip", [P, B, TT, HG], F32)
        nmax = place("nmax", [P, 2, TT], F32)
        assert top[0] <= nc.sbuf_usable_end, top[0]

        tri_one = place("tri_one", [P, 2, P], F32, yT_at)
        rcst = place("rcst", [P, 2 * E + NB], F32, yT_at + 1024)
        rw = place("rw", [P, KT, E], F32, yT_at + 1280)
        zT = place("zT", [P, 2, KT, P], F32, yT_at + 2048)
        tmp_at = yT_at + 6144

        def small(name, shape, dt=F32):
            nonlocal tmp_at
            t = place(name, shape, dt, tmp_at)
            tmp_at += (int(np.prod(shape[1:])) * 4 + 31) // 32 * 32
            return t

        logit = small("logit", [P, NT, E])
        best = small("best", [P, NT])
        hot = small("hot", [P, NT, E])
        hot2 = small("hot2", [P, NT, E])
        before = small("before", [P, NT + 1, E])
        count = small("count", [P, E])
        over = small("over", [P, E, E])
        blocks = small("blocks", [P, E])
        base = small("base", [P, E])
        at_b = small("at_b", [P, NB, E])
        blk = small("blk", [P, NB])
        place_f = small("place_f", [P, NT, E])
        slot_f = small("slot_f", [P, NT])
        assert tmp_at <= yT_at + 32768
        slot_i = place("slot_i", [P, NT], I32, early_c)
        blk_i = place("blk_i", [P, NB], I32, early_c + 32)
        c_at = early_c + 128
        used = [c_at]

        def placec(name, shape, dt):
            t = place(name, shape, dt, used[0])
            used[0] += (int(np.prod(shape[1:])) * 4 + 31) // 32 * 32
            assert used[0] <= nc.sbuf_usable_end, (name, used[0])
            return t

        raw = placec("raw", [P, RAW, 4 * D], F32)
        half_hi = {pc: placec(f"{pc[0]}{pc[1]}_hi", [P, KT * CH[pc[1]] * P], F32R) for pc in sorted(PIECES)}
        half_lo = {pc: placec(f"{pc[0]}{pc[1]}_lo", [P, KT * CH[pc[1]] * P], F32R) for pc in sorted(PIECES)}
        zb = placec("zb", [P, D], F32)
        zbT_hi = placec("zbT_hi", [P, KT, P], F32R)
        zbT_lo = placec("zbT_lo", [P, KT, P], F32R)
        sil = placec("sil", [P, 4 * P], F32)
        hid = placec("hid", [P, 4 * P], F32)
        hT_hi = placec("hT_hi", [P, 4, P], F32R)
        hT_lo = placec("hT_lo", [P, 4, P], F32R)
        yb = placec("yb", [P, D], F32)
        res = place("res", [P, NT, D], F32, c_at)

        psum = ctx.enter_context(nc.psum_tensor("psum", [P, 8, 512], F32))
        bank = [psum[:, i, :] for i in range(8)]
        o_bank, h_bank = bank[0:4], bank[4:8]
        pair = [psum[:, 0:2, :], psum[:, 2:4, :]]
        pt_bank, ot_bank = bank[4:6], bank[6:8]
        g_bank, u_bank, turn_bank, y_bank = bank[0:3], bank[3:6], bank[6], bank[7]

        consts_in = sem("consts_in")
        x_in = [sem(f"x_in{b}") for b in range(B)]
        zero_set = sem("zero_set")
        ln_step = sem("ln_step")
        ln_var = sem("ln_var")
        ln_std = sem("ln_std")
        normed = sem("normed")
        norm_turned = sem("norm_turned")
        turn_hi = sem("turn_hi")
        turn_lo = sem("turn_lo")
        nat_in = [sem(f"nat_in{s}") for s in range(2)]
        tr_in = [sem(f"tr_in{s}") for s in range(2)]
        cT_hi_done = sem("cT_hi_done")
        cT_lo_done = sem("cT_lo_done")
        cN_hi_done = sem("cN_hi_done")
        cN_lo_done = sem("cN_lo_done")
        h_done = sem("h_done")
        g_hi_done = sem("g_hi_done")
        g_lo_done = sem("g_lo_done")
        g_free = sem("g_free")
        o_read = sem("o_read")
        stored = sem("stored")
        row_in_done = sem("row_in_done")
        fac_step = sem("fac_step")
        pool_step = sem("pool_step")
        angles = sem("angles")
        wrapped = sem("wrapped")
        encoded = sem("encoded")
        y_ready = sem("y_ready")
        y_normed = sem("y_normed")
        act_step = sem("act_step")
        w_in = sem("w_in")
        w_hi_done = sem("w_hi_done")
        w_lo_done = sem("w_lo_done")
        proj_done = sem("proj_done")
        qk_hi_done = sem("qk_hi_done")
        pair_read = [sem(f"pair_read{i}") for i in range(2)]
        stack_in = [sem(f"stack_in{j}") for j in range(HG)]
        v_turned = sem("v_turned")
        s_done = sem("s_done")
        max_done = sem("max_done")
        tr_done = sem("tr_done")
        pt_read = [sem(f"pt_read{i}") for i in range(2)]
        pv_done = sem("pv_done")
        ot_free = [sem(f"ot_free{b}") for b in range(B)]
        r_step = sem("r_step")
        r_turned = sem("r_turned")
        wo_in = sem("wo_in")
        wo_hi_done = sem("wo_hi_done")
        wo_lo_done = sem("wo_lo_done")
        y_bo_done = sem("y_bo_done")
        o_hi_done = sem("o_hi_done")
        o_lo_done = sem("o_lo_done")
        wo_done = sem("wo_done")
        wo_read = sem("wo_read")
        var3 = sem("var3")
        std3 = sem("std3")
        n3_done = sem("n3_done")
        g3_done = sem("g3_done")
        x3_done = sem("x3_done")
        zeroed = sem("zeroed")
        router_in = sem("router_in")
        var4 = sem("var4")
        std4 = sem("std4")
        z_done = sem("z_done")
        z_turned = sem("z_turned")
        zT_done = sem("zT_done")
        logit_done = sem("logit_done")
        hot_done = sem("hot_done")
        ranked = sem("ranked")
        route_step = sem("route_step")
        routed = sem("routed")
        scattered = sem("scattered")
        raw_in = [sem(f"raw_in{i}") for i in range(RAW)]
        half_hi_done = sem("half_hi_done")
        half_lo_done = sem("half_lo_done")
        zb_in = sem("zb_in")
        zb_turned = sem("zb_turned")
        zb_hi_done = sem("zb_hi_done")
        zb_lo_done = sem("zb_lo_done")
        gate_done = sem("gate_done")
        up_done = sem("up_done")
        silu_done = sem("silu_done")
        hid_done = sem("hid_done")
        hid_turned = sem("hid_turned")
        hT_hi_done = sem("hT_hi_done")
        hT_lo_done = sem("hT_lo_done")
        down_done = sem("down_done")
        y_read = sem("y_read")
        y_stored = sem("y_stored")
        gathered = [sem(f"gathered{t}") for t in range(NT)]
        summed = sem("summed")

        block = ctx.enter_context(nc.Block())

        def piece_no(b, pc):
            if pc == ("d", 2):
                if isinstance(b, int) and b == NB - 1:
                    return b * len(PIECES) + len(EARLY) + 1
                return b * len(PIECES) + (len(EARLY) + PIECES.index(pc) + 1)
            if isinstance(b, int) and b == 0:
                return EARLY.index(pc) + 1
            return b * len(PIECES) + (len(EARLY) - len(PIECES) + PIECES.index(pc) + 1)

        def raw_count(b, n):
            return b * (16 * len(PIECES) // RAW) + 16 * ((len(EARLY) + 1 + n) // RAW + (n % RAW > 0))

        def raw_count_early(n):
            return 16 * ((n + 1) // RAW + ((n + 1) % RAW > 0))

        @block.sync
        def _(sp):
            sp.dma_start(ident[:, :], consts[:, 0:P]).then_inc(consts_in, 16)
            xt = x.rearrange("(t p) d -> p t d", p=P)
            sp.dma_start(cst[:, :], consts[:, C_POS:C_TRI]).then_inc(consts_in, 16)
            sp.dma_start(rby_all[:, :], rby.partition_broadcast(P)).then_inc(consts_in, 16)
            for b in range(B):
                sp.dma_start(tok[:, b * TT:(b + 1) * TT, :], xt[:, b * TT:(b + 1) * TT, :]).then_inc(x_in[b], 16)

            def load_group(g, s):
                sp.dma_start(tr_raw[:, s], ctx_tr[g]).then_inc(tr_in[s], 16)
                sp.dma_start(nat_raw[:, s], ctx_nat[g]).then_inc(nat_in[s], 16)

            for s in range(2):
                load_group(s, s)
            sp.dma_start(w_raw[:, :, :, :], w_qkv[0]).then_inc(w_in, 16)
            sp.dma_start(row_in[:, :, :], rows.partition_broadcast(P)).then_inc(row_in_done, 16)
            sp.dma_start(b_all[:, :, :], b_qkv).then_inc(row_in_done, 16)
            sp.wait_ge(zero_set, 1)
            sp.dma_start(z_slots.rearrange("(b p) d -> p b d", p=P),
                         zero[:, :].unsqueeze(1).to_broadcast([P, NB, D])).then_inc(zeroed, 16)
            with sp.Fori(1, B * NG // 2) as i:
                for s in range(2):
                    sp.wait_ge(cT_lo_done, i * (2 * GT) + (s - 1) * GT)
                    sp.wait_ge(cN_lo_done, i * (2 * GT) + (s - 1) * GT)
                    load_group(i * 2 + s, s)

            def stack(grp, j, seen):
                rows_j = slice(DH * j, DH * j + DH)
                for st, m, halves in ((q_st, 0, (qk_hi, qk_hi, qk_lo, qk_lo)), (k_st, 1, (qk_hi, qk_lo, qk_hi, qk_lo))):
                    for c, half in enumerate(halves):
                        sp.dma_start(st[DH * c:DH * c + DH, j, :].bitcast(F32), half[rows_j, m, :].bitcast(F32)).then_inc(stack_in[j], 16)

            for u in (FIRST_USES["Q"], FIRST_USES["K"]):
                sp.wait_ge(pair_read[u % 2], first_reads(u))
            for j in range(HG):
                stack(0, j, None)
            with sp.Fori(0, NGRP - 1) as grp:
                sp.wait_ge(w_lo_done, grp * 2 + 2)
                sp.dma_start(w_raw[:, :, :, :], w_qkv[grp + 1]).then_inc(w_in, 16)
                sp.wait_ge(pair_read[slot_of("K")], reads(grp, "K"))
                for j in range(HG):
                    sp.wait_ge(s_done, grp * (2 * GH) + (4 * j + 4))
                    stack(grp + 1, j, None)
            sp.wait_ge(proj_done, 3 * NGRP)
            sp.dma_start(wo_raw[:, :, :], w_o).then_inc(wo_in, 16)


            sp.wait_ge(wo_done, NT)
            sp.dma_start(tri_one[:, :, :], consts[:, C_TRI:C_DEC].rearrange("p (a c) -> p a c", a=2))\
                .then_inc(router_in, 16)
            sp.dma_start(rcst[:, :], consts[:, C_DEC:C_END]).then_inc(router_in, 16)
            sp.dma_start(rw[:, :, :], router).then_inc(router_in, 16)

            def load_piece(pc, slot, e):
                size = KT * CH[pc[1]] * P
                sp.dma_start(raw[:, slot, 0:size], (ffn0, ffn1, ffn2)[pc[1]][e, "gud".index(pc[0])])\
                    .then_inc(raw_in[slot], 16)

            sp.wait_ge(routed, 1)
            e0 = sp.value_load(blk_i[0:1, 0:1], min_val=0, max_val=E - 1)
            for n, pc in enumerate(EARLY):
                if n >= RAW:
                    sp.wait_ge(half_lo_done, n - RAW + 1)
                load_piece(pc, (n + 1) % RAW, e0)
                if n == RAW - 1:
                    sp.wait_ge(scattered, 16 * NT)
                    sp.dma_start(zb[:, :], z_slots[0:P, :]).then_inc(zb_in, 16)

            def body(b, first=False, last=False):
                e_now = sp.value_load(blk_i[0:1, bass.ds(b, 1)], min_val=0, max_val=E - 1)
                if not last:
                    e_next = sp.value_load(blk_i[0:1, bass.ds(b + 1, 1)], min_val=0, max_val=E - 1)
                for n, pc in enumerate(PIECES):
                    if not last or pc == ("d", 2):
                        sp.wait_ge(half_lo_done, b * len(PIECES) + (len(EARLY) + n - RAW + 1))
                        load_piece(pc, n % RAW, e_now if pc == ("d", 2) else e_next)
                    if n == 3 and not first:
                        sp.wait_ge(y_read, b)
                        sp.dma_start(y_slots[bass.ds((b - 1) * P, P), :], yb[:, :]).then_inc(y_stored, 16)
                    if n == 5 and not last:
                        sp.wait_ge(zb_turned, b + 1)
                        sp.dma_start(zb[:, :], z_slots[bass.ds((b + 1) * P, P), :]).then_inc(zb_in, 16)

            body(0, first=True)
            with sp.Fori(1, NB - 1) as b:
                body(b)
            body(NB - 1, last=True)
            sp.wait_ge(y_read, NB)
            sp.dma_start(y_slots[(NB - 1) * P:NB * P, :], yb[:, :]).then_inc(y_stored, 16)
            for t in range(NT):
                sp.wait_ge(summed, t + 1)
                sp.dma_start(out[t * P:(t + 1) * P, :], res[:, t]).then_inc(stored, 16)
            sp.wait_ge(stored, 16 * NT)

        @block.scalar
        def _(act):
            for b in range(B):
                act.wait_ge(ln_var, (b + 1))
                act.activation(rstd[:, b * TT:(b + 1) * TT], mv[:, b * TT:(b + 1) * TT, 1], ACT.Sqrt)\
                   .then_inc(ln_std, 1)
            for t in range(NT):
                act.wait_ge(norm_turned, t + 1)
                act.activation(xT_hi[:, :, t * P:(t + 1) * P],
                               h_bank[t % 4].rearrange("p (k t) -> p k t", k=KT), ACT.Copy)\
                   .then_inc(turn_hi, 1)

            def split(n, i, j):
                s = j // GT
                act.wait_ge(tr_in[s], i * 16 + 16)
                act.activation(cT_hi[:, j], tr_raw[:, s, :, (j % GT) * P:(j % GT + 1) * P], ACT.Copy)\
                   .then_inc(cT_hi_done, 1)
                act.wait_ge(nat_in[s], i * 16 + 16)
                act.activation(cN_hi[:, j], nat_raw[:, s, j % GT], ACT.Copy).then_inc(cN_hi_done, 1)

            def gelu(n, j):
                act.wait_ge(h_done, n + 1)
                act.wait_ge(g_free, n + 1)
                act.activation(g_full[:, j % GRING], h_bank[j % 4], ACT.Gelu_apprx_tanh)
                act.activation(g_hi[:, j % GRING], h_bank[j % 4], ACT.Gelu_apprx_tanh).then_inc(g_hi_done, 1)

            for j in range(AHEAD):
                split(j, 0, j)
            with act.Fori(0, NF // RING - 1) as i:
                for j in range(RING):
                    gelu(i * RING + j, j)
                    split(None, i + (j + AHEAD) // RING, (j + AHEAD) % RING)
            for j in range(RING):
                gelu(NF - RING + j, j)
                if j + AHEAD < RING:
                    split(None, NF // RING - 1, j + AHEAD)

            for q in range(2):
                act.wait_ge(wrapped, q + 1)
                act.activation(pe_tab[:, :, q::2], (ang, ang2)[q][:, :, :], ACT.Sin).then_inc(encoded, 1)
            sq = [0]

            def root(to, mv_x, b, ready, n, done, bias=0.0):
                act.wait_ge(ready, n)
                act.activation(to[:, b * TT:(b + 1) * TT], mv_x[:, b * TT:(b + 1) * TT, 1], ACT.Sqrt)\
                   .then_inc(done, 1)

            for b in range(B):
                root(rstd2, mv2, b, ln_var, B + b + 1, ln_std)

            def w_high(grp):
                act.wait_ge(w_in, grp * 16 + 16)
                act.activation(w_hi[:, 0], w_raw[:, 0], ACT.Copy, scale=fac[:, 0:1]).then_inc(w_hi_done, 1)
                act.activation(w_hi[:, 1:3], w_raw[:, 1:3], ACT.Copy).then_inc(w_hi_done, 1)

            act.wait_ge(fac_step, FAC_STEPS)
            w_high(0)
            for t in range(NT):
                act.wait_ge(norm_turned, NT + t + 1)
                act.activation(yT_hi[:, :, t * P:(t + 1) * P],
                               h_bank[t % 4].rearrange("p (k t) -> p k t", k=KT), ACT.Copy)\
                   .then_inc(turn_hi, 1)

            def qk_high(m, grp, pr):
                act.wait_ge(proj_done, grp * 3 + (m + 1))
                for j in range(HG):
                    if not isinstance(grp, int) or grp:
                        act.wait_ge(stack_in[j], grp * 128)
                act.activation(qk_hi[:, m, :], pair[pr].rearrange("p a t -> p (a t)"), ACT.Identity,
                               bias=b_all[:, m, bass.ds(grp, 1)]).then_inc(qk_hi_done, 1)

            def v_out(grp, pr):
                act.wait_ge(proj_done, grp * 3 + 3)
                act.activation(vT[:, :], pair[pr].rearrange("p a t -> p (a t)"), ACT.Identity,
                               bias=b_all[:, 2, bass.ds(grp, 1)]).then_inc(pair_read[pr], 1)

            def exps(n, par, h, p, pr):
                act.wait_ge(max_done, n * 2 + p + 1)
                b, j = h % B, h // B
                for q in (2 * p, 2 * p + 1):
                    e = act.activation(prob[:, par, q, :], pair[pr][:, q % 2, :], ACT.Exp,
                                       bias=nmax[:, par, q:q + 1], accum_out=sums[:, b, q, j:j + 1])
                e.then_inc(pair_read[pr], 1)

            def turned(n, par, q):
                act.wait_ge(tr_done, n * 4 + q + 1)
                act.activation(probT[:, par, :, q * P:(q + 1) * P],
                               pt_bank[q % 2].rearrange("p (k t) -> p k t", k=TT), ACT.Copy)\
                   .then_inc(pt_read[q % 2], 1)

            qk_high(0, 0, 1)
            qk_high(1, 0, 0)
            v_out(0, 1)
            exps(0, 0, 0, 0, 0)
            exps(0, 0, 0, 1, 1)
            exps(1, 1, 1, 0, 0)
            turned(0, 0, 1)
            exps(1, 1, 1, 1, 1)
            turned(0, 0, 3)

            def body(grp, last):
                if not last:
                    w_high(grp + 1)
                act.wait_ge(v_turned, grp + 1)
                pr = slot_of("turn", last)
                act.activation(v_tok[:, :, :], pair[pr].rearrange("p a (k d) -> p (a k) d", d=P), ACT.Copy)\
                   .then_inc(pair_read[pr], 1)
                for s in range(GH):
                    n = grp * GH + s
                    for p in range(2):
                        if (s + 2, p) in (LAST_BODY if last else FULL_BODY):
                            exps(n + 2, s % 2, (s + 2) % GH, p, slot_of((s + 2, p), last))
                        if s == GH - 1 and p == 0:
                            act.wait_ge(r_turned, grp + 1)
                            for b in range(B):
                                act.activation(r_all[:, b, :], pt_bank[b], ACT.Copy).then_inc(pt_read[b], 1)
                        if not (last and s == GH - 1):
                            turned(n + 1, (s + 1) % 2, 2 * p + 1)
                    if not last and s in (1, 2):
                        qk_high(s - 1, grp + 1, slot_of("QK"[s - 1]))
                    if not last and s == 3:
                        v_out(grp + 1, slot_of("V"))

            with act.Fori(0, NGRP - 1) as grp:
                body(grp, False)
            act.wait_ge(wo_in, 16)
            act.activation(wo_hi[:, :, :], wo_raw[:, :, :], ACT.Copy).then_inc(wo_hi_done, 1)
            body(NGRP - 1, True)

            for t in range(NT):
                if t == 0:
                    for b in range(B):
                        act.wait_ge(ot_free[b], NGRP + 1)
                if t >= 2:
                    act.wait_ge(wo_done, t - 1)
                act.activation(o_hi[:, t % 2], oT[:, :, t * P:(t + 1) * P], ACT.Copy).then_inc(o_hi_done, 1)
            for b in range(B):
                act.wait_ge(var3, b + 1)
                act.activation(rstd3[:, b * TT:(b + 1) * TT], mv3[:, b * TT:(b + 1) * TT, 1], ACT.Sqrt,
                               bias=fac[:, 2:3]).then_inc(std3, 1)

            for b in range(B):
                root(rstd4, mv4, b, var4, b + 1, std4)
            for t in range(NT):
                act.wait_ge(z_turned, t + 1)
                if t >= 2:
                    act.wait_ge(logit_done, t - 1)
                act.activation(zT[:, t % 2], h_bank[t % 4].rearrange("p (k t) -> p k t", k=KT), ACT.Copy)\
                   .then_inc(zT_done, 1)
            act.sem_inc(y_stored, 16)

            def high(pc, slot, count):
                size = KT * CH[pc[1]] * P
                act.wait_ge(raw_in[slot], count)
                act.activation(half_hi[pc][:, :], raw[:, slot, 0:size], ACT.Copy).then_inc(half_hi_done, 1)

            def zb_high(b):
                act.wait_ge(zb_turned, b + 1)
                act.activation(zbT_hi[:, :, :], turn_bank.rearrange("p (k t) -> p k t", k=KT), ACT.Copy)\
                   .then_inc(zb_hi_done, 1)

            def hid_high(q, c):
                act.wait_ge(hid_turned, q + 1)
                act.activation(hT_hi[:, 0:CH[c]], turn_bank[:, 0:CH[c] * P].rearrange("p (i t) -> p i t", t=P),
                               ACT.Copy).then_inc(hT_hi_done, 1)

            def y_out(b):
                act.wait_ge(down_done, b * 3 + 3)
                act.wait_ge(y_stored, b * 16 + 16)
                act.activation(yb[:, :], y_bank, ACT.Copy).then_inc(y_read, 1)

            act.wait_ge(scattered, 16 * NT)
            for n, pc in enumerate(EARLY):
                high(pc, (n + 1) % RAW, raw_count_early(n))
                if n == 1:
                    zb_high(0)

            def body(b, first=False, last=False):
                for c in range(3):
                    act.wait_ge(gate_done, b * 3 + (c + 1))
                    if not (first and c == 0):
                        act.wait_ge(hid_done, b * 3 + c)
                    act.activation(sil[:, 0:CH[c] * P], g_bank[c][:, 0:CH[c] * P], ACT.Silu).then_inc(silu_done, 1)
                    if not (first and c == 0):
                        hid_high(b * 3 + (c - 1), (c - 1) % 3)
                    for n in range(3 * c, 3 * c + 3):
                        pc = PIECES[n]
                        if pc[0] == "u" and not last:
                            act.wait_ge(up_done, b * 3 + (c + 1))
                        if pc[0] == "d" and (c or not first):
                            act.wait_ge(down_done, b * 3 + c)
                        if pc == ("d", 2) and not first:
                            y_out(b - 1)
                        if pc == ("u", 2) and not last:
                            zb_high(b + 1)
                        if not last or pc == ("d", 2):
                            high(pc, n % RAW, raw_count(b, n))

            body(0, first=True)
            with act.Fori(1, NB - 1) as b:
                body(b)
            body(NB - 1, last=True)
            hid_high(3 * NB - 1, 2)
            y_out(NB - 1)

        @block.gpsimd
        def _(pool):
            steps = [0]

            def link(ins):
                steps[0] += 1
                ins.then_inc(pool_step, 1)
                pool.wait_ge(pool_step, steps[0])

            pool.wait_ge(angles, 1)
            for q, (to, turn) in enumerate(((ang2, 0.25), (ang, 0.0))):
                link(nc.gpsimd.tensor_scalar(wrap[:, :, :], ang[:, :, :], 1.0 / TWO_PI, turn, ALU.mult, ALU.add))
                link(nc.gpsimd.tensor_scalar(wrap[:, :, :], wrap[:, :, :], ROUND, None, ALU.add))
                link(nc.gpsimd.tensor_scalar(wrap[:, :, :], wrap[:, :, :], ROUND, None, ALU.subtract))
                for n, part in enumerate((PI_A, PI_B, PI_C)):
                    link(nc.gpsimd.tensor_scalar(wrap2[:, :, :], wrap[:, :, :], part, None, ALU.mult))
                    link(nc.gpsimd.tensor_tensor(to[:, :, :], (ang if n == 0 else to)[:, :, :], wrap2[:, :, :],
                                                 ALU.subtract))
                if turn:
                    link(nc.gpsimd.tensor_scalar(to[:, :, :], to[:, :, :], turn * TWO_PI, None, ALU.add))
                lim = float(np.nextafter(np.float32(math.pi), np.float32(0)))
                link(nc.gpsimd.tensor_scalar(to[:, :, :], to[:, :, :], lim, -lim, ALU.min, ALU.max))
            nc.gpsimd.tensor_scalar(to[:, 0, 0:1], to[:, 0, 0:1], 1.0, None, ALU.mult).then_inc(wrapped, 2)

            pool.wait_ge(row_in_done, 32)
            pool.wait_ge(fac_step, FAC_STEPS)
            link(nc.gpsimd.tensor_scalar(row_in[:, 1], row_in[:, 1], fac[:, 3:4], None, ALU.mult))

            pool.wait_ge(encoded, 2)
            for t in range(NT):
                pool.wait_ge(y_normed, t + 1)
                nc.gpsimd.tensor_tensor(ynorm[:, t % 4], ynorm[:, t % 4], pe_tab[:, t % TT], ALU.add)\
                    .then_inc(y_ready, 1)
            pool.wait_ge(proj_done, 3 * NGRP)
            for j in range(HG):
                pool.wait_ge(stack_in[j], 128 * NGRP)
            for t in range(NT):
                link(nc.gpsimd.tensor_scalar(y_bo[:, t], tok[:, t], mv2[:, t, 0:1], rstd2[:, t:t + 1],
                                             ALU.subtract, ALU.mult))
                link(nc.gpsimd.tensor_tensor(y_bo[:, t], y_bo[:, t], pe_tab[:, t % TT], ALU.add))
                nc.gpsimd.tensor_tensor(tok[:, t], tok[:, t], row_in[:, 2], ALU.add)
                nc.gpsimd.tensor_tensor(y_bo[:, t], y_bo[:, t], row_in[:, 0], ALU.add).then_inc(y_bo_done, 1)
            for t in range(NT):
                pool.wait_ge(n3_done, t + 1)
                nc.gpsimd.tensor_tensor(xg[:, t], xg[:, t], row_in[:, 1], ALU.mult).then_inc(g3_done, 1)

            pool.wait_ge(zeroed, 16)
            pool.wait_ge(routed, 2)
            pool.wait_ge(z_done, NT)
            for t in range(NT):
                nc.gpsimd.indirect_dma_start(
                    out=z_slots, out_offset=bass.IndirectOffsetOnAxis(ap=slot_i[:, t:t + 1], axis=0),
                    in_=xg[:, t], in_offset=None).then_inc(scattered, 16)
            pool.wait_ge(y_stored, 16 * NB + 16)
            for t in range(NT):
                nc.gpsimd.indirect_dma_start(
                    out=res[:, t], out_offset=None, in_=y_slots,
                    in_offset=bass.IndirectOffsetOnAxis(ap=slot_i[:, t:t + 1], axis=0)).then_inc(gathered[t], 16)

        @block.vector
        def _(dve):
            steps = [0]

            def link(ins):
                steps[0] += 1
                ins.then_inc(ln_step, 1)
                dve.wait_ge(ln_step, steps[0])

            nc.vector.memset(zero[:, :], 0.0).then_inc(zero_set, 1)

            dve.wait_ge(consts_in, 48)
            facs = [0]

            def fac_link(ins):
                facs[0] += 1
                ins.then_inc(fac_step, 1)
                dve.wait_ge(fac_step, facs[0])

            red, blue, yellow = (rby_all[:, c:c + 1] for c in range(3))
            ts = nc.vector.tensor_scalar
            fac_link(ts(fac[:, 5:6], red, 0.1, 1.0, ALU.mult, ALU.add))
            fac_link(nc.vector.scalar_tensor_tensor(fac[:, 0:1], blue, 0.05, fac[:, 5:6], ALU.mult, ALU.add))
            fac_link(nc.vector.scalar_tensor_tensor(fac[:, 6:7], yellow, 0.15, fac[:, 0:1], ALU.mult, ALU.add))
            fac_link(ts(fac[:, 0:1], fac[:, 6:7], DH ** -0.5, None, ALU.mult))
            fac_link(ts(fac[:, 1:2], yellow, EPS_ADAPTIVE, 1.0, ALU.mult, ALU.add))
            fac_link(ts(fac[:, 2:3], blue, 0.1 * LN_EPS, LN_EPS, ALU.mult, ALU.add))
            fac_link(nc.vector.scalar_tensor_tensor(fac[:, 3:4], yellow, 0.05, fac[:, 5:6], ALU.mult, ALU.add))
            fac_link(ts(fac[:, 4:5], yellow, PHASE_MOD, 1.0, ALU.mult, ALU.add))
            fac_link(ts(cst[:, TT:], cst[:, TT:], fac[:, 4:5], None, ALU.mult))
            fac_link(nc.vector.reciprocal(cst[:, TT:], cst[:, TT:]))
            assert facs[0] == FAC_STEPS
            nc.vector.tensor_tensor(ang[:, :, :], cst[:, 0:TT].unsqueeze(2).to_broadcast([P, TT, D // 2]),
                                    cst[:, TT:].unsqueeze(1).to_broadcast([P, TT, D // 2]), ALU.mult)\
                .then_inc(angles, 1)

            def layer_stats(b, mv=mv, src=tok, done=ln_var, eps=LN_EPS):
                for t in range(b * TT, (b + 1) * TT):
                    link(nc.vector.bn_stats(stats[:, t], src[:, t]))
                    link(nc.vector.bn_aggr(mv[:, t], stats[:, t]))
                nc.vector.tensor_scalar(mv[:, b * TT:(b + 1) * TT, 1], mv[:, b * TT:(b + 1) * TT, 1],
                                        eps, None, ALU.add).then_inc(done, 1)

            def layer_scale(b, n_std):
                dve.wait_ge(ln_std, n_std)
                link(nc.vector.reciprocal(rstd[:, b * TT:(b + 1) * TT], rstd[:, b * TT:(b + 1) * TT]))

            for b in range(B):
                dve.wait_ge(x_in[b], 16)
                layer_stats(b)
            for b in range(B):
                layer_scale(b, b + 1)
            for t in range(NT):
                if t >= 2:
                    dve.wait_ge(norm_turned, t - 1)
                nc.vector.tensor_scalar(norm[:, t % 2], tok[:, t], mv[:, t, 0:1], rstd[:, t:t + 1],
                                        ALU.subtract, ALU.mult).then_inc(normed, 1)
                dve.wait_ge(turn_hi, t + 1)
                nc.vector.tensor_tensor(xT_lo[:, :, t * P:(t + 1) * P],
                                        h_bank[t % 4].rearrange("p (k t) -> p k t", k=KT),
                                        xT_hi[:, :, t * P:(t + 1) * P].bitcast(F32), ALU.subtract)\
                    .then_inc(turn_lo, 1)

            def split(n, i, j):
                s = j // GT
                dve.wait_ge(cT_hi_done, n + 1)
                nc.vector.tensor_tensor(cT_lo[:, j], tr_raw[:, s, :, (j % GT) * P:(j % GT + 1) * P],
                                        cT_hi[:, j].bitcast(F32), ALU.subtract).then_inc(cT_lo_done, 1)
                dve.wait_ge(cN_hi_done, n + 1)
                nc.vector.tensor_tensor(cN_lo[:, j], nat_raw[:, s, j % GT],
                                        cN_hi[:, j].bitcast(F32), ALU.subtract).then_inc(cN_lo_done, 1)

            def gelu_low(n, j):
                dve.wait_ge(g_hi_done, n + 1)
                nc.vector.tensor_tensor(g_lo[:, j % GRING], g_full[:, j % GRING],
                                        g_hi[:, j % GRING].bitcast(F32), ALU.subtract).then_inc(g_lo_done, 1)

            def residual(b):
                dve.wait_ge(g_free, (b + 1) * NG * GT + GRING)
                for t in range(TT):
                    nc.vector.tensor_tensor(tok[:, b * TT + t], tok[:, b * TT + t], o_bank[t], ALU.add)\
                        .then_inc(o_read, 1)

            for j in range(AHEAD):
                split(j, 0, j)
            per = NF // RING // B
            for b in range(B):
                with dve.Fori(b * per, (b + 1) * per - b) as i:
                    for j in range(RING):
                        gelu_low(i * RING + j, j)
                        split(i * RING + j + AHEAD, i + (j + AHEAD) // RING, (j + AHEAD) % RING)
                if b == B - 1:
                    for j in range(RING):
                        gelu_low(NF - RING + j, j)
                        if j + AHEAD < RING:
                            split(NF - RING + j + AHEAD, NF // RING - 1, j + AHEAD)
                residual(b)

            for b in range(B):
                layer_stats(b, mv2)
            for b in range(B):
                bs = slice(b * TT, (b + 1) * TT)
                dve.wait_ge(ln_std, B + b + 1)
                link(nc.vector.reciprocal(rstd2[:, bs], rstd2[:, bs]))

            def y_tile(t):
                if t >= 4:
                    dve.wait_ge(norm_turned, NT + t - 3)
                nc.vector.tensor_scalar(ynorm[:, t % 4], tok[:, t], mv2[:, t, 0:1], rstd2[:, t:t + 1],
                                        ALU.subtract, ALU.mult).then_inc(y_normed, 1)

            y_tile(0)
            y_tile(1)

            def w_low(grp):
                dve.wait_ge(w_hi_done, grp * 2 + 1)
                nc.vector.scalar_tensor_tensor(w_lo[:, 0], w_raw[:, 0], fac[:, 0:1], w_hi[:, 0].bitcast(F32),
                                               ALU.mult, ALU.subtract).then_inc(w_lo_done, 1)
                dve.wait_ge(w_hi_done, grp * 2 + 2)
                nc.vector.tensor_tensor(w_lo[:, 1:3], w_raw[:, 1:3], w_hi[:, 1:3].bitcast(F32),
                                        ALU.subtract).then_inc(w_lo_done, 1)

            link(ts(b_all[:, 0], b_all[:, 0], fac[:, 0:1], None, ALU.mult))
            w_low(0)
            for t in range(NT):
                if t + 2 < NT:
                    y_tile(t + 2)
                dve.wait_ge(turn_hi, NT + t + 1)
                nc.vector.tensor_tensor(yT_lo[:, :, t * P:(t + 1) * P],
                                        h_bank[t % 4].rearrange("p (k t) -> p k t", k=KT),
                                        yT_hi[:, :, t * P:(t + 1) * P].bitcast(F32), ALU.subtract)\
                    .then_inc(turn_lo, 1)

            def qk_low(m, grp, pr):
                dve.wait_ge(qk_hi_done, grp * 2 + (m + 1))
                nc.vector.scalar_tensor_tensor(qk_lo[:, m, :], pair[pr].rearrange("p a t -> p (a t)"),
                                               b_all[:, m, bass.ds(grp, 1)], qk_hi[:, m, :].bitcast(F32),
                                               ALU.add, ALU.subtract).then_inc(pair_read[pr], 1)

            def maxima(n, par, p, pr):
                dve.wait_ge(s_done, n * 2 + p + 1)
                nc.vector.tensor_reduce(nmax[:, par, 2 * p:2 * p + 2], pair[pr], AX.X, ALU.max, negate=True)\
                    .then_inc(max_done, 1)

            def turned(n, par, q):
                dve.wait_ge(tr_done, n * 4 + q + 1)
                nc.vector.tensor_copy(probT[:, par, :, q * P:(q + 1) * P],
                                      pt_bank[q % 2].rearrange("p (k t) -> p k t", k=TT))\
                    .then_inc(pt_read[q % 2], 1)

            qk_low(0, 0, 1)
            qk_low(1, 0, 0)
            maxima(0, 0, 0, 0)
            maxima(0, 0, 1, 1)
            maxima(1, 1, 0, 0)
            turned(0, 0, 0)
            maxima(1, 1, 1, 1)
            turned(0, 0, 2)

            def body(grp, last):
                if not last:
                    w_low(grp + 1)
                for s in range(GH):
                    n = grp * GH + s
                    if s == GH - 2:
                        dve.wait_ge(pair_read[slot_of((GH - 1, 1), last)], reads(grp, (GH - 1, 1), last))
                        nc.vector.reciprocal(recip[:, :, :, :], sums[:, :, :, :]).then_inc(r_step, 1)
                        dve.wait_ge(r_step, grp * 3 + 1)
                        ts(recip[:, :, :, :], recip[:, :, :, :], fac[:, 1:2], None, ALU.mult).then_inc(r_step, 1)
                        dve.wait_ge(r_step, grp * 3 + 2)
                        nc.vector.tensor_copy(
                            r_wide[:, :, :].rearrange("p m (j d) -> p m j d", d=DH),
                            recip[:, :, :, :].rearrange("p b q j -> p (b q) j").unsqueeze(3)
                            .to_broadcast([P, B * TT, HG, DH])).then_inc(r_step, 1)
                    for p in range(2):
                        if (s + 2, p) in (LAST_BODY if last else FULL_BODY):
                            maxima(n + 2, s % 2, p, slot_of((s + 2, p), last))
                        if not (last and s == GH - 1):
                            turned(n + 1, (s + 1) % 2, 2 * p)
                    if not last and s in (1, 2):
                        qk_low(s - 1, grp + 1, slot_of("QK"[s - 1]))
                dve.wait_ge(pv_done, grp * GH + GH)
                for b in range(B):
                    dve.wait_ge(pt_read[b], grp * 17 + 17)
                    nc.vector.tensor_tensor(oT[:, bass.ds(grp, 1), b * T:(b + 1) * T].squeeze(1), ot_bank[b], r_all[:, b, :],
                                            ALU.mult).then_inc(ot_free[b], 1)

            with dve.Fori(0, NGRP - 1) as grp:
                body(grp, False)
            dve.wait_ge(wo_hi_done, 1)
            nc.vector.tensor_tensor(wo_lo[:, :, :], wo_raw[:, :, :], wo_hi[:, :, :].bitcast(F32), ALU.subtract)\
                .then_inc(wo_lo_done, 1)
            body(NGRP - 1, True)

            def o_low(t):
                dve.wait_ge(o_hi_done, t + 1)
                nc.vector.tensor_tensor(o_lo[:, t % 2], oT[:, :, t * P:(t + 1) * P], o_hi[:, t % 2].bitcast(F32),
                                        ALU.subtract).then_inc(o_lo_done, 1)

            def attended(t):
                dve.wait_ge(wo_done, t + 1)
                dve.wait_ge(y_bo_done, t + 1)
                nc.vector.tensor_tensor(xa[:, t], bank[t % 4], y_bo[:, t], ALU.add).then_inc(wo_read, 1)
                dve.wait_ge(wo_read, t + 1)

            o_low(0)
            for b in range(B):
                for t in range(b * TT, (b + 1) * TT):
                    if t + 1 < NT:
                        o_low(t + 1)
                    attended(t)
                layer_stats(b, mv3, xa, var3, 0.0)
            for b in range(B):
                bs = slice(b * TT, (b + 1) * TT)
                dve.wait_ge(std3, b + 1)
                link(nc.vector.reciprocal(rstd3[:, bs], rstd3[:, bs]))
                for t in range(b * TT, (b + 1) * TT):
                    ts(xg[:, t], xa[:, t], mv3[:, t, 0:1], rstd3[:, t:t + 1], ALU.subtract, ALU.mult)\
                        .then_inc(n3_done, 1)
            for t in range(NT):
                dve.wait_ge(g3_done, t + 1)
                nc.vector.tensor_tensor(tok[:, t], tok[:, t], xg[:, t], ALU.add).then_inc(x3_done, 1)

            for b in range(B):
                dve.wait_ge(x3_done, (b + 1) * TT)
                layer_stats(b, mv4, tok, var4)
            for b in range(B):
                bs = slice(b * TT, (b + 1) * TT)
                dve.wait_ge(std4, b + 1)
                link(nc.vector.reciprocal(rstd4[:, bs], rstd4[:, bs]))
                for t in range(b * TT, (b + 1) * TT):
                    ts(xg[:, t], tok[:, t], mv4[:, t, 0:1], rstd4[:, t:t + 1], ALU.subtract, ALU.mult)\
                        .then_inc(z_done, 1)
            tt = nc.vector.tensor_tensor
            dec = rcst[:, 0:E].unsqueeze(1).to_broadcast([P, NT, E])
            dve.wait_ge(router_in, 48)
            dve.wait_ge(logit_done, NT)
            link(nc.vector.tensor_copy(logit[:, :, :], bank[0][:, 0:NT * E].rearrange("p (t e) -> p t e", e=E)))
            link(nc.vector.tensor_reduce(best[:, :], logit[:, :, :], AX.X, ALU.max))
            link(tt(hot2[:, :, :], logit[:, :, :], best[:, :].unsqueeze(2).to_broadcast([P, NT, E]), ALU.is_ge))
            link(tt(hot2[:, :, :], hot2[:, :, :], dec, ALU.mult))
            link(nc.vector.tensor_reduce(best[:, :], hot2[:, :, :], AX.X, ALU.max))
            link(tt(hot[:, :, :], dec, best[:, :].unsqueeze(2).to_broadcast([P, NT, E]), ALU.is_equal))
            link(nc.vector.memset(before[:, 0], 0.0))
            for t in range(NT):
                link(tt(before[:, t + 1], before[:, t], hot[:, t], ALU.add))
            nc.vector.memset(base[:, 0:1], 0.0).then_inc(hot_done, 1)
            dve.wait_ge(ranked, 1)
            link(nc.vector.tensor_copy(count[:, :], bank[2][:, 0:E]))
            link(tt(over[:, :, :], count[:, :].unsqueeze(2).to_broadcast([P, E, E]),
                    rcst[:, E:2 * E].unsqueeze(1).to_broadcast([P, E, E]), ALU.is_gt))
            link(nc.vector.tensor_reduce(blocks[:, :], over[:, :, :], AX.X, ALU.add))
            for e in range(1, E):
                link(tt(base[:, e:e + 1], base[:, e - 1:e], blocks[:, e - 1:e], ALU.add))
            link(tt(at_b[:, :, :], base[:, :].unsqueeze(1).to_broadcast([P, NB, E]),
                    rcst[:, 2 * E:].unsqueeze(2).to_broadcast([P, NB, E]), ALU.is_le))
            link(nc.vector.tensor_reduce(blk[:, :], at_b[:, :, :], AX.X, ALU.add))
            ts(blk_i[:, :], blk[:, :], -1.0, None, ALU.add).then_inc(routed, 1)
            link(nc.vector.scalar_tensor_tensor(
                place_f[:, :, :], base[:, :].unsqueeze(1).to_broadcast([P, NT, E]), float(P),
                bank[1][:, 0:NT * E].rearrange("p (t e) -> p t e", e=E), ALU.mult, ALU.add))
            link(tt(place_f[:, :, :], place_f[:, :, :], hot[:, :, :], ALU.mult))
            link(nc.vector.tensor_reduce(slot_f[:, :], place_f[:, :, :], AX.X, ALU.add))
            nc.vector.tensor_copy(slot_i[:, :], slot_f[:, :]).then_inc(routed, 1)
            dve.wait_ge(routed, 2)

            def low(pc, slot, count):
                size = KT * CH[pc[1]] * P
                dve.wait_ge(half_hi_done, count)
                tt(half_lo[pc][:, :], raw[:, slot, 0:size], half_hi[pc][:, :].bitcast(F32), ALU.subtract)\
                    .then_inc(half_lo_done, 1)

            def zb_low(b):
                dve.wait_ge(zb_hi_done, b + 1)
                tt(zbT_lo[:, :, :], turn_bank.rearrange("p (k t) -> p k t", k=KT), zbT_hi[:, :, :].bitcast(F32),
                   ALU.subtract).then_inc(zb_lo_done, 1)

            def hid_low(q, c):
                dve.wait_ge(hT_hi_done, q + 1)
                tt(hT_lo[:, 0:CH[c]], turn_bank[:, 0:CH[c] * P].rearrange("p (i t) -> p i t", t=P),
                   hT_hi[:, 0:CH[c]].bitcast(F32), ALU.subtract).then_inc(hT_lo_done, 1)

            for n, pc in enumerate(EARLY):
                low(pc, (n + 1) % RAW, n + 1)
                if n == 1:
                    zb_low(0)

            def body(b, first=False, last=False):
                for c in range(3):
                    if not (first and c == 0):
                        hid_low(b * 3 + (c - 1), (c - 1) % 3)
                    for n in range(3 * c, 3 * c + 3):
                        pc = PIECES[n]
                        if n == 3 * c + 1:
                            dve.wait_ge(silu_done, b * 3 + (c + 1))
                            dve.wait_ge(up_done, b * 3 + (c + 1))
                            tt(hid[:, 0:CH[c] * P], sil[:, 0:CH[c] * P], u_bank[c][:, 0:CH[c] * P], ALU.mult)\
                                .then_inc(hid_done, 1)
                            if c == 2 and not last:
                                zb_low(b + 1)
                        if not last or pc == ("d", 2):
                            low(pc, n % RAW, b * len(PIECES) + (len(EARLY) + (0 if last else n) + 1))

            body(0, first=True)
            with dve.Fori(1, NB - 1) as b:
                body(b)
            body(NB - 1, last=True)
            hid_low(3 * NB - 1, 2)
            for t in range(NT):
                dve.wait_ge(gathered[t], 16)
                tt(res[:, t], res[:, t], tok[:, t], ALU.add).then_inc(summed, 1)

        @block.tensor
        def _(pe):
            pe.wait_ge(consts_in, 48)
            for t in range(NT):
                pe.wait_ge(normed, t + 1)
                if t >= 4:
                    pe.wait_ge(turn_lo, t - 3)
                for k in range(KT):
                    mm = nc.tensor.transpose(h_bank[t % 4][:, k * P:(k + 1) * P],
                                             norm[:, t % 2, k * P:(k + 1) * P], ident[:, :])
                mm.then_inc(norm_turned, 1)
            pe.sem_inc(g_free, GRING)
            pe.wait_ge(zero_set, 1)

            def first(n, j, b):
                pe.wait_ge(cT_lo_done, n + 1)
                toks = slice(b * T, (b + 1) * T)
                for k in range(KT):
                    for q, (w, v) in enumerate(((cT_hi, xT_hi), (cT_hi, xT_lo), (cT_lo, xT_hi))):
                        mm = nc.tensor.matmul(h_bank[j % 4], w[:, j, k], v[:, k, toks],
                                              start=(k == 0 and q == 0), stop=(k == KT - 1 and q == 2))
                mm.then_inc(h_done, 1)

            def second(n, j, last=False):
                pe.wait_ge(cN_lo_done, n + 1)
                pe.wait_ge(g_lo_done, n + 1)
                for t in range(TT):
                    ts = slice(t * P, (t + 1) * P)
                    for q, (w, v) in enumerate(((g_hi, cN_hi), (g_hi, cN_lo), (g_lo, cN_hi))):
                        mm = nc.tensor.matmul(o_bank[t], w[:, j % GRING, ts], v[:, j],
                                              start=False, stop=(last and q == 2), skip_group_check=True)
                mm.then_inc(g_free, 1)

            pe.wait_ge(turn_lo, NT)
            for j in range(PE_LAG):
                first(j, j, 0)
            per = NF // RING // B
            for b in range(B):
                if b:
                    pe.wait_ge(o_read, b * TT)
                for t in range(TT):
                    nc.tensor.matmul(o_bank[t], zero[:, 0:P], zero[:, :], start=True, stop=False,
                                     skip_group_check=True)
                with pe.Fori(b * per, (b + 1) * per - 1) as i:
                    for j in range(RING):
                        first(i * RING + (j + PE_LAG), (j + PE_LAG) % RING, b)
                        second(i * RING + j, j)
                n0 = ((b + 1) * per - 1) * RING
                for j in range(RING):
                    if n0 + j + PE_LAG < NF:
                        first(n0 + j + PE_LAG, (j + PE_LAG) % RING, (n0 + j + PE_LAG) // (NF // B))
                    second(n0 + j, j, j == RING - 1)


            for t in range(NT):
                pe.wait_ge(y_ready, t + 1)
                if t >= 4:
                    pe.wait_ge(turn_lo, NT + t - 3)
                for k in range(KT):
                    mm = nc.tensor.transpose(h_bank[t % 4][:, k * P:(k + 1) * P],
                                             ynorm[:, t % 4, k * P:(k + 1) * P], ident[:, :])
                mm.then_inc(norm_turned, 1)
            pe.wait_ge(turn_lo, 2 * NT)
            for b in range(B):
                pe.sem_inc(ot_free[b], 1)

            def project(m, grp, pr, before):
                if before is not None:
                    pe.wait_ge(pair_read[pr], before)
                pe.wait_ge(w_lo_done, grp * 2 + 2)
                for b in range(B):
                    toks = slice(b * T, (b + 1) * T)
                    for k in range(KT):
                        for q, (w, v) in enumerate(((w_hi, yT_hi), (w_hi, yT_lo), (w_lo, yT_hi))):
                            mm = nc.tensor.matmul(pair[pr][:, b, :], w[:, m, k], v[:, k, toks],
                                                  start=(k == 0 and q == 0), stop=(k == KT - 1 and q == 2))
                mm.then_inc(proj_done, 1)

            def scores(h, p, pr, before):
                pe.wait_ge(pair_read[pr], before)
                b, j = h % B, h // B
                for q in range(2):
                    at = b * T + (2 * p + q) * P
                    mm = nc.tensor.matmul(pair[pr][:, q, :], q_st[:, j, at:at + P], k_st[:, j, b * T:(b + 1) * T],
                                          start=True, stop=True)
                mm.then_inc(s_done, 1)

            def turn(par, q, pr, probs, before):
                pe.wait_ge(pair_read[pr], probs)
                if before is not None:
                    pe.wait_ge(pt_read[q % 2], before)
                for k in range(TT):
                    mm = nc.tensor.transpose(pt_bank[q % 2][:, k * P:(k + 1) * P],
                                             prob[:, par, q, k * P:(k + 1) * P], ident[:, :])
                mm.then_inc(tr_done, 1)

            for m in range(3):
                u = m + 1
                project(m, 0, u % 2, first_reads(u - 2) if u > 2 else None)
            pe.wait_ge(stack_in[0], 128)
            scores(0, 0, 0, first_reads(2))
            scores(0, 1, 1, first_reads(3))
            scores(1, 0, 0, first_reads(4))
            turn(0, 0, 0, first_reads(4), None)
            turn(0, 1, 0, first_reads(4), None)
            scores(1, 1, 1, first_reads(5))
            turn(0, 2, 1, first_reads(5), 1)
            turn(0, 3, 1, first_reads(5), 1)

            def body(grp, last):
                def before(what):
                    return reads(grp, what, last) - 1
                pr = slot_of("turn", last)
                pe.wait_ge(pair_read[pr], before("turn"))
                pe.wait_ge(pair_read[slot_of("V")], reads(grp - 1, "V"))
                for m in range(NT):
                    mm = nc.tensor.transpose(pair[pr][:, m // TT, (m % TT) * P:(m % TT + 1) * P],
                                             vT[:, m * P:(m + 1) * P], ident[:, :])
                mm.then_inc(v_turned, 1)
                for s in range(GH):
                    pt0 = grp * 17 + (2 + 2 * s + (s == GH - 1))
                    for p in range(2):
                        if (s + 2, p) in (LAST_BODY if last else FULL_BODY):
                            h = (s + 2) % GH
                            if h % B == 0 and p == 0:
                                pe.wait_ge(stack_in[h // B], (grp + (s + 2) // GH) * 128 + 128)
                            scores(h, p, slot_of((s + 2, p), last), before((s + 2, p)))
                        if not (last and s == GH - 1):
                            src = (s + 1, p)
                            for q in (2 * p, 2 * p + 1):
                                turn((s + 1) % 2, q, slot_of(src, last), reads(grp, src, last), pt0 + p)
                    if s == GH - 2:
                        pe.wait_ge(r_step, grp * 3 + 3)
                        for b in range(B):
                            pe.wait_ge(pt_read[b], pt0 + 2)
                            for q in range(TT):
                                mm = nc.tensor.transpose(pt_bank[b][:, q * P:(q + 1) * P], r_wide[:, b * TT + q],
                                                         ident[:, :])
                        mm.then_inc(r_turned, 1)
                    b, j = s % B, s // B
                    for i in range(2):
                        pe.wait_ge(pt_read[i], grp * 17 + (2 + 2 * s))
                    if s == 0:
                        pe.wait_ge(pair_read[slot_of("turn", last)], reads(grp, "turn", last))
                    if s < B:
                        pe.wait_ge(ot_free[b], grp + 1)
                    for k in range(TT):
                        mm = nc.tensor.matmul(ot_bank[b][DH * j:DH * j + DH, :], v_tok[:, b * TT + k, DH * j:DH * j + DH],
                                              probT[:, s % 2, k, :], start=(k == 0), stop=(k == TT - 1))
                    mm.then_inc(pv_done, 1)
                    if not last and s in (1, 2, 3):
                        what = "QKV"[s - 1]
                        project(s - 1, grp + 1, slot_of(what), before(what))

            with pe.Fori(0, NGRP - 1) as grp:
                body(grp, False)
            body(NGRP - 1, True)

            pe.wait_ge(wo_lo_done, 1)
            for t in range(NT):
                pe.wait_ge(o_lo_done, t + 1)
                if t >= 4:
                    pe.wait_ge(wo_read, t - 3)
                for k in range(KT):
                    for q, (w, v) in enumerate(((o_hi, wo_hi), (o_hi, wo_lo), (o_lo, wo_hi))):
                        mm = nc.tensor.matmul(bank[t % 4], w[:, t % 2, k], v[:, k],
                                              start=(k == 0 and q == 0), stop=(k == KT - 1 and q == 2))
                mm.then_inc(wo_done, 1)

            def z_turn(t):
                pe.wait_ge(z_done, t + 1)
                if t >= 4:
                    pe.wait_ge(zT_done, t - 3)
                for k in range(KT):
                    mm = nc.tensor.transpose(h_bank[t % 4][:, k * P:(k + 1) * P], xg[:, t, k * P:(k + 1) * P],
                                             ident[:, :])
                mm.then_inc(z_turned, 1)

            z_turn(0)
            pe.wait_ge(router_in, 48)
            for t in range(NT):
                if t + 1 < NT:
                    z_turn(t + 1)
                pe.wait_ge(zT_done, t + 1)
                for k in range(KT):
                    mm = nc.tensor.matmul(bank[0][:, t * E:(t + 1) * E], zT[:, t % 2, k], rw[:, k],
                                          start=(k == 0), stop=(k == KT - 1))
                mm.then_inc(logit_done, 1)
            pe.wait_ge(hot_done, 1)
            nc.tensor.matmul(bank[1][:, 0:NT * E], tri_one[:, 0], hot[:, :, :], start=True, stop=False)
            nc.tensor.matmul(bank[1][:, 0:NT * E], tri_one[:, 1], before[:, 0:NT, :], start=False, stop=True)
            nc.tensor.matmul(bank[2][:, 0:E], tri_one[:, 1], before[:, NT, :], start=True, stop=True)\
                .then_inc(ranked, 1)

            def zb_turn(b):
                pe.wait_ge(zb_in, b * 16 + 16)
                for k in range(KT):
                    mm = nc.tensor.transpose(turn_bank[:, k * P:(k + 1) * P], zb[:, k * P:(k + 1) * P], ident[:, :])
                mm.then_inc(zb_turned, 1)

            def up(b, what, c, to, done):
                w = CH[c] * P
                pe.wait_ge(half_lo_done, piece_no(b, (what, c)))
                hi, lo = half_hi[what, c], half_lo[what, c]
                for k in range(KT):
                    ks = slice(k * w, (k + 1) * w)
                    for q, (z, v) in enumerate(((zbT_hi, hi), (zbT_hi, lo), (zbT_lo, hi))):
                        mm = nc.tensor.matmul(to[:, 0:w], z[:, k], v[:, ks], start=(k == 0 and q == 0),
                                              stop=(k == KT - 1 and q == 2))
                mm.then_inc(done, 1)

            def hid_turn(q, c):
                pe.wait_ge(hid_done, q + 1)
                for i in range(CH[c]):
                    mm = nc.tensor.transpose(turn_bank[:, i * P:(i + 1) * P], hid[:, i * P:(i + 1) * P], ident[:, :])
                mm.then_inc(hid_turned, 1)

            def down(b, q, c):
                pe.wait_ge(hT_lo_done, q + 1)
                pe.wait_ge(half_lo_done, piece_no(b, ("d", c)))
                hi, lo = half_hi["d", c], half_lo["d", c]
                for i in range(CH[c]):
                    cols = slice(i * D, (i + 1) * D)
                    for n, (h, v) in enumerate(((hT_hi, hi), (hT_hi, lo), (hT_lo, hi))):
                        mm = nc.tensor.matmul(y_bank, h[:, i], v[:, cols], start=(c == 0 and i == 0 and n == 0),
                                              stop=(c == 2 and i == CH[c] - 1 and n == 2))
                mm.then_inc(down_done, 1)

            zb_turn(0)

            def body(b, first=False, last=False):
                for c in range(3):
                    if c == 0:
                        pe.wait_ge(zb_lo_done, b + 1)
                    up(b, "g", c, g_bank[c], gate_done)
                    if not (first and c == 0):
                        hid_turn(b * 3 + (c - 1), (c - 1) % 3)
                    up(b, "u", c, u_bank[c], up_done)
                    if c == 2 and not last:
                        pe.wait_ge(hT_lo_done, b * 3 + 2)
                        zb_turn(b + 1)
                    if c == 1 and not first:
                        pe.wait_ge(y_read, b)
                    if not (first and c == 0):
                        down(b - 1 if c == 0 else b, b * 3 + (c - 1), (c - 1) % 3)

            body(0, first=True)
            with pe.Fori(1, NB - 1) as b:
                body(b)
            body(NB - 1, last=True)
            hid_turn(3 * NB - 1, 2)
            down(NB - 1, 3 * NB - 1, 2)


def kernel(**inputs):
    import concourse.bacc as _bacc
    from concourse.bass_utils import run_bass_kernel_spmd as _run

    a = {k: np.ascontiguousarray(v) for k, v in inputs.items()}
    ctx = a["ctx_1024"].reshape(B * NG, GT * P, D)
    even = np.arange(0, D, 2, dtype=np.float32)
    power = np.power(np.float32(10000.0), (np.float32(2.0) * even / np.float32(D)).astype(np.float32))
    pos = (np.arange(TT)[None, :] * P + np.arange(P)[:, None]).astype(np.float32)
    row = np.concatenate([E - np.arange(E), P * np.arange(E), np.arange(NB)]).astype(np.float32)
    consts = np.concatenate([np.eye(P, dtype=np.float32), pos, np.broadcast_to(power, (P, D // 2)),
                             np.triu(np.ones((P, P), np.float32), 1), np.ones((P, P), np.float32),
                             np.broadcast_to(row, (P, row.size))], axis=1)
    gate, up = (a["L0_ffn_" + w].reshape(E, FF, KT, P).transpose(0, 3, 2, 1) for w in ("gate_w", "up_w"))
    down = a["L0_ffn_down_w"].reshape(E, D, FT, P).transpose(0, 3, 2, 1)
    edges = np.cumsum([0] + CH)
    ffn = [np.stack([gate[..., lo * P:hi * P].reshape(E, P, -1), up[..., lo * P:hi * P].reshape(E, P, -1),
                     down[:, :, lo:hi].reshape(E, P, -1)], axis=1) for lo, hi in zip(edges, edges[1:])]
    att = lambda w: a["L0_attn_" + w]
    w_qkv = np.stack([att(w) for w in ("Wq", "Wk", "Wv")]).reshape(3, NGRP, P, KT, P).transpose(1, 4, 0, 3, 2)
    arrays = {
        "x": a["x"].reshape(B * T, D),
        "ctx_nat": ctx.reshape(B * NG, GT, P, D).transpose(0, 2, 1, 3),
        "ctx_tr": ctx.reshape(B * NG, GT * P, KT, P).transpose(0, 3, 2, 1),
        "consts": consts,
        "rby": att("rby"),
        "w_qkv": w_qkv,
        "b_qkv": np.stack([att(w) for w in ("bq", "bk", "bv")]).reshape(3, NGRP, P).transpose(2, 0, 1),
        "w_o": att("Wo").reshape(D, KT, P).transpose(2, 1, 0),
        "rows": np.stack([att(w) for w in ("bo", "ln_gamma", "ln_beta")]),
        "router": a["L0_ffn_router_w"].reshape(E, KT, P).transpose(2, 1, 0),
        "ffn0": ffn[0],
        "ffn1": ffn[1],
        "ffn2": ffn[2],
    }
    arrays = {k: np.ascontiguousarray(v) for k, v in arrays.items()}
    nc = _bacc.Bacc("TRN2", target_bir_lowering=False, num_devices=1)
    args = [nc.dram_tensor(k, v.shape, mybir.dt.from_np(v.dtype), kind="ExternalInput").ap()
            for k, v in arrays.items()]
    args.append(nc.dram_tensor("y", (B * T, D), F32, kind="ExternalOutput").ap())
    build(nc, *args)
    r = _run(nc, [arrays], core_ids=[0])
    return r.results[0]["y"].reshape(B, T, D)
```

```python
import math
import numpy as np
import concourse.bass as bass
from concourse import mybir
from contextlib import ExitStack

F32 = mybir.dt.float32
F32R = mybir.dt.float32r
I32 = mybir.dt.int32
ALU = mybir.AluOpType
ACT = mybir.ActivationFunctionType
AX = mybir.AxisListType

P = 128
B, T, D = 2, 512, 512
KT = D // P
TT = T // P
NT = B * TT
F = 8192
GT = 4
NG = F // (GT * P)
NF = B * F // P
RING = 8
GRING = 4
AHEAD = 4
PE_LAG = 2
LN_EPS = 1e-5

H, DH = 16, 32
HG = P // DH
NGRP = H // HG
GH = HG * B
PHASE_MOD = 0.1 * math.sin(2.0 * math.pi * 0.25)
EPS_ADAPTIVE = 0.1 * math.sin(2.0 * math.pi * 0.5)
E, FF = 8, 1408
FT = FF // P
CH = [4, 4, 3]
assert sum(CH) == FT
NB = (B * T + E * (P - 1)) // P
PIECES = [("g", 0), ("u", 0), ("d", 2), ("g", 1), ("u", 1), ("d", 0), ("g", 2), ("u", 2), ("d", 1)]
EARLY = [pc for pc in PIECES if pc != ("d", 2)]
SPLITS = [[(("g", 2), 0), (("u", 2), 0), (("d", 1), 0)],
          [(("g", 0), 1), (("u", 0), 1), (("d", 2), 0)],
          [(("g", 1), 1), (("u", 1), 1), (("d", 0), 1)]]
USED = B * T // P
SPLIT_FIRST = [("g", 0), ("u", 0), ("g", 1), ("u", 1), ("d", 0)]
TWO_PI = 2.0 * math.pi
PI_A = 6.28125
PI_B = float(np.float32(0.0019352436065673828))
PI_C = TWO_PI - PI_A - PI_B
ROUND = 1.5 * 2.0 ** 23
C_POS, C_POW, C_TRI = P, P + TT, P + TT + D // 2
C_ONE = C_TRI + P
C_DEC = C_ONE + P
C_END = C_DEC + E + E + NB

FULL_BODY = ["turn"]
for _s in range(GH):
    FULL_BODY += [(_s + 2, 0), (_s + 2, 1)] + {1: ["Q"], 2: ["K"], 3: ["V"]}.get(_s, [])
LAST_BODY = ["turn"] + [(_s + 2, _p) for _s in range(GH - 2) for _p in range(2)]
PER_BODY = len(FULL_BODY)
assert PER_BODY % 2 == 0
FIRST_USES = {"Q": 1, "K": 2, "V": 3}
BODY0 = 2 * 2 + len(FIRST_USES) + 1


def use(grp, what, last=False):
    if isinstance(what, tuple) and what[0] < 2:
        return (grp - 1) * PER_BODY + (BODY0 + FULL_BODY.index((what[0] + GH, what[1])))
    return grp * PER_BODY + (BODY0 + (LAST_BODY if last else FULL_BODY).index(what))


def slot_of(what, last=False):
    if isinstance(what, tuple) and what[0] < 2:
        return (BODY0 + FULL_BODY.index((what[0] + GH, what[1]))) % 2
    return (BODY0 + (LAST_BODY if last else FULL_BODY).index(what)) % 2


def reads(grp, what, last=False):
    prev = isinstance(what, tuple) and what[0] < 2
    order = FULL_BODY if prev or not last else LAST_BODY
    at = BODY0 + order.index((what[0] + GH, what[1]) if prev else what)
    return (grp - 1 if prev else grp) * (PER_BODY // 2) + (at + at % 2) // 2


FAC_STEPS = 10


def first_reads(u):
    return (u + u % 2) // 2


def build(nc, x, ctx_nat, ctx_tr, consts, rby, w_qkv, b_qkv, w_o, rows, router, ffn0, ffn1, ffn2, out):
    ctx = ExitStack()
    with ctx:
        top = [(nc.sbuf_base + 31) // 32 * 32]

        def place(name, shape, dt, at=None):
            size = int(np.prod(shape[1:])) * 4
            if at is None:
                at = top[0]
                top[0] += (size + 31) // 32 * 32
            t = nc.alloc_sbuf_tensor_at(name, shape, dt, offset=at)
            return t

        def sem(name):
            return ctx.enter_context(nc.semaphore(name))

        z_slots = nc.dram_tensor("z_slots", (NB * P, D), F32).ap()
        y_slots = nc.dram_tensor("y_slots", (NB * P, D), F32).ap()

        ident = place("ident", [P, P], F32)
        zero = place("zero", [P, D], F32)
        tok = place("tok", [P, NT, D], F32)
        stats = place("stats", [P, NT, 6], F32)
        mv = place("mv", [P, NT, 2], F32)
        rstd = place("rstd", [P, NT], F32)
        mv2 = place("mv2", [P, NT, 2], F32)
        rstd2 = place("rstd2", [P, NT], F32)
        mv3 = place("mv3", [P, NT, 2], F32)
        rstd3 = place("rstd3", [P, NT], F32)
        mv4 = place("mv4", [P, NT, 2], F32)
        rstd4 = place("rstd4", [P, NT], F32)
        early_c = top[0]
        rby_all = place("rby_all", [P, 3], F32)
        fac = place("fac", [P, 8], F32)
        cst = place("cst", [P, TT + D // 2], F32)
        b_all = place("b_all", [P, 3, NGRP], F32)
        row_in = place("row_in", [P, 3, D], F32)
        w_raw = place("w_raw", [P, 3, KT, P], F32)
        pe_at = top[0]
        pe_tab = place("pe_tab", [P, TT, D], F32)
        wrap = place("wrap", [P, TT, D // 2], F32, pe_at)
        wrap2 = place("wrap2", [P, TT, D // 2], F32, pe_at + 4096)
        phase = top[0]
        late_at = nc.sbuf_usable_end // 32 * 32 - 26 * 1024

        norm = place("norm", [P, 2, D], F32)
        xT_hi = place("xT_hi", [P, KT, NT * P], F32R)
        xT_lo = place("xT_lo", [P, KT, NT * P], F32R)
        nat_raw = place("nat_raw", [P, 2, GT, D], F32)
        tr_raw = place("tr_raw", [P, 2, KT, GT * P], F32)
        cN_hi = place("cN_hi", [P, RING, D], F32R)
        cN_lo = place("cN_lo", [P, RING, D], F32R)
        cT_hi = place("cT_hi", [P, RING, KT, P], F32R)
        cT_lo = place("cT_lo", [P, RING, KT, P], F32R)
        g_full = place("g_full", [P, GRING, T], F32)
        g_hi = place("g_hi", [P, GRING, T], F32R)
        g_lo = place("g_lo", [P, GRING, T], F32R)
        ang = place("ang", [P, TT, D // 2], F32)
        ang2 = place("ang2", [P, TT, D // 2], F32)

        assert top[0] <= nc.sbuf_usable_end, top[0]
        top[0] = phase
        yT_at = top[0]
        yT_hi = place("yT_hi", [P, KT, NT * P], F32R)
        yT_lo = place("yT_lo", [P, KT, NT * P], F32R)
        wo_raw = place("wo_raw", [P, KT, D], F32, yT_at)
        wo_hi = place("wo_hi", [P, KT, D], F32R, yT_at + 8192)
        wo_lo = place("wo_lo", [P, KT, D], F32R, yT_at + 16384)
        w_hi = place("w_hi", [P, 3, KT, P], F32R)
        w_lo = place("w_lo", [P, 3, KT, P], F32R)
        qk_at = top[0]
        qk_hi = place("qk_hi", [P, 2, NT * P], F32R)
        qk_lo = place("qk_lo", [P, 2, NT * P], F32R)
        y_bo = place("y_bo", [P, NT, D], F32, qk_at)
        vT = place("vT", [P, NT * P], F32)
        v_tok = place("v_tok", [P, NT, P], F32)
        stack_at = top[0]
        q_st = place("q_st", [P, HG, NT * P], F32R)
        k_st = place("k_st", [P, HG, NT * P], F32R)
        xa = place("xa", [P, NT, D], F32, stack_at)
        xg = place("xg", [P, NT, D], F32, late_at)
        prob_at = top[0]
        prob = place("prob", [P, 2, TT, T], F32)
        o_hi = place("o_hi", [P, 2, KT, P], F32R, prob_at)
        o_lo = place("o_lo", [P, 2, KT, P], F32R, prob_at + 4096)
        probT = place("probT", [P, 2, TT, T], F32)
        ynorm = place("ynorm", [P, 4, D], F32, prob_at + 16384)
        oT = place("oT", [P, KT, NT * P], F32)
        r_all = place("r_all", [P, B, T], F32)
        r_wide = place("r_wide", [P, B * TT, P], F32)
        sums = place("sums", [P, B, TT, HG], F32)
        recip = place("recip", [P, B, TT, HG], F32)
        nmax = place("nmax", [P, 2, TT], F32)
        assert top[0] <= nc.sbuf_usable_end, top[0]

        rt_at = late_at + 16384
        tri_one = place("tri_one", [P, 2, P], F32, rt_at)
        rcst = place("rcst", [P, 2 * E + NB], F32, rt_at + 1024)
        rw = place("rw", [P, KT, E], F32, rt_at + 1280)
        zT = place("zT", [P, 2, KT, P], F32, rt_at + 2048)
        tmp_at = rt_at + 6144

        def small(name, shape, dt=F32):
            nonlocal tmp_at
            t = place(name, shape, dt, tmp_at)
            tmp_at += (int(np.prod(shape[1:])) * 4 + 31) // 32 * 32
            return t

        logit = small("logit", [P, NT, E])
        best = small("best", [P, NT])
        hot = small("hot", [P, NT, E])
        hot2 = small("hot2", [P, NT, E])
        before = small("before", [P, NT + 1, E])
        count = small("count", [P, E])
        over = small("over", [P, E, E])
        blocks = small("blocks", [P, E])
        base = small("base", [P, E])
        at_b = small("at_b", [P, NB, E])
        blk = small("blk", [P, NB])
        used_f = small("used_f", [P, NB])
        new_f = small("new_f", [P, NB])
        blocks_all = small("blocks_all", [P, 1])
        place_f = small("place_f", [P, NT, E])
        slot_f = small("slot_f", [P, NT])
        assert tmp_at <= nc.sbuf_usable_end
        slot_i = place("slot_i", [P, NT], I32, early_c)
        blk_i = place("blk_i", [P, NB], I32, early_c + 32)
        used_i = place("used_i", [P, NB], I32, early_c + 96)
        new_i = place("new_i", [P, NB], I32, early_c + 160)
        c_at = early_c + 224
        used = [c_at]

        def placec(name, shape, dt):
            t = place(name, shape, dt, used[0])
            used[0] += (int(np.prod(shape[1:])) * 4 + 31) // 32 * 32
            assert used[0] <= late_at, (name, used[0])
            return t

        raw, half_lo = {}, {}
        for pc in sorted(PIECES):
            raw[pc] = place(f"{pc[0]}{pc[1]}_raw", [P, KT * CH[pc[1]] * P], F32, used[0])
            half_lo[pc] = placec(f"{pc[0]}{pc[1]}_lo", [P, KT * CH[pc[1]] * P], F32R)
        half_hi = {pc: placec(f"{pc[0]}{pc[1]}_hi", [P, KT * CH[pc[1]] * P], F32R) for pc in sorted(PIECES)}
        zb = placec("zb", [P, D], F32)
        zbT_hi = placec("zbT_hi", [P, KT, P], F32R)
        zbT_lo = placec("zbT_lo", [P, KT, P], F32R)
        sil = placec("sil", [P, 4 * P], F32)
        hid = placec("hid", [P, 4 * P], F32)
        hT_hi = placec("hT_hi", [P, 4, P], F32R)
        hT_lo = placec("hT_lo", [P, 4, P], F32R)
        yb = placec("yb", [P, D], F32)
        res = place("res", [P, NT, D], F32, c_at)

        psum = ctx.enter_context(nc.psum_tensor("psum", [P, 8, 512], F32))
        bank = [psum[:, i, :] for i in range(8)]
        o_bank, h_bank = bank[0:4], bank[4:8]
        pair = [psum[:, 0:2, :], psum[:, 2:4, :]]
        pt_bank, ot_bank = bank[4:6], bank[6:8]
        g_bank, u_bank, turn_bank, y_bank = bank[0:3], bank[3:6], bank[6], bank[7]

        consts_in = sem("consts_in")
        x_in = [sem(f"x_in{b}") for b in range(B)]
        zero_set = sem("zero_set")
        ln_step = sem("ln_step")
        ln_var = sem("ln_var")
        ln_std = sem("ln_std")
        normed = sem("normed")
        norm_turned = sem("norm_turned")
        turn_hi = sem("turn_hi")
        turn_lo = sem("turn_lo")
        nat_in = [sem(f"nat_in{s}") for s in range(2)]
        tr_in = [sem(f"tr_in{s}") for s in range(2)]
        cT_hi_done = sem("cT_hi_done")
        cT_lo_done = sem("cT_lo_done")
        cN_hi_done = sem("cN_hi_done")
        cN_lo_done = sem("cN_lo_done")
        h_done = sem("h_done")
        g_hi_done = sem("g_hi_done")
        g_lo_done = sem("g_lo_done")
        g_free = sem("g_free")
        o_read = sem("o_read")
        stored = sem("stored")
        row_in_done = sem("row_in_done")
        fac_step = sem("fac_step")
        pool_step = sem("pool_step")
        angles = sem("angles")
        wrapped = sem("wrapped")
        encoded = sem("encoded")
        y_ready = sem("y_ready")
        y_normed = sem("y_normed")
        act_step = sem("act_step")
        w_in = sem("w_in")
        w_hi_done = sem("w_hi_done")
        w_lo_done = sem("w_lo_done")
        proj_done = sem("proj_done")
        qk_hi_done = sem("qk_hi_done")
        pair_read = [sem(f"pair_read{i}") for i in range(2)]
        stack_in = [sem(f"stack_in{j}") for j in range(HG)]
        v_turned = sem("v_turned")
        s_done = sem("s_done")
        max_done = sem("max_done")
        tr_done = sem("tr_done")
        pt_read = [sem(f"pt_read{i}") for i in range(2)]
        pv_done = sem("pv_done")
        ot_free = [sem(f"ot_free{b}") for b in range(B)]
        r_step = sem("r_step")
        r_turned = sem("r_turned")
        wo_in = sem("wo_in")
        wo_hi_done = sem("wo_hi_done")
        wo_lo_done = sem("wo_lo_done")
        y_bo_done = sem("y_bo_done")
        o_hi_done = sem("o_hi_done")
        o_lo_done = sem("o_lo_done")
        wo_done = sem("wo_done")
        wo_read = sem("wo_read")
        var3 = sem("var3")
        std3 = sem("std3")
        n3_done = sem("n3_done")
        g3_done = sem("g3_done")
        x3_done = sem("x3_done")
        zeroed = sem("zeroed")
        router_in = sem("router_in")
        var4 = sem("var4")
        std4 = sem("std4")
        z_done = sem("z_done")
        z_turned = sem("z_turned")
        zT_done = sem("zT_done")
        logit_done = sem("logit_done")
        hot_done = sem("hot_done")
        ranked = sem("ranked")
        route_step = sem("route_step")
        routed = sem("routed")
        scattered = sem("scattered")
        piece_in = {pc: sem(f"{pc[0]}{pc[1]}_in") for pc in PIECES}
        half_hi_done = sem("half_hi_done")
        half_lo_done = sem("half_lo_done")
        zb_in = sem("zb_in")
        zb_turned = sem("zb_turned")
        zb_hi_done = sem("zb_hi_done")
        zb_lo_done = sem("zb_lo_done")
        gate_done = sem("gate_done")
        up_done = sem("up_done")
        silu_done = sem("silu_done")
        hid_done = sem("hid_done")
        hid_turned = sem("hid_turned")
        hT_hi_done = sem("hT_hi_done")
        hT_lo_done = sem("hT_lo_done")
        down_done = sem("down_done")
        y_read = sem("y_read")
        y_stored = sem("y_stored")
        gathered = [sem(f"gathered{t}") for t in range(NT)]
        summed = sem("summed")

        block = ctx.enter_context(nc.Block())

        def piece_no(b, pc):
            for stage in SPLITS:
                for n, (piece, ahead) in enumerate(stage):
                    if piece == pc:
                        at = SPLITS.index(stage) * 3 + n + 1
                        if ahead and isinstance(b, int) and b == 0:
                            return SPLIT_FIRST.index(pc) + 1
                        if pc == ("d", 2) and isinstance(b, int) and b == NB - 1:
                            at -= 2
                        return b * len(PIECES) + (len(SPLIT_FIRST) + at - ahead * len(PIECES))

        def flag(eng, flags, b):
            return eng.value_load(flags[0:1, bass.ds(b, 1)], min_val=0, max_val=1)

        def count_on(eng, sem_, now, by):
            eng.wait_ge(sem_, now)
            eng.sem_inc(sem_, by)

        @block.sync
        def _(sp):
            sp.dma_start(ident[:, :], consts[:, 0:P]).then_inc(consts_in, 16)
            xt = x.rearrange("(t p) d -> p t d", p=P)
            sp.dma_start(cst[:, :], consts[:, C_POS:C_TRI]).then_inc(consts_in, 16)
            sp.dma_start(rby_all[:, :], rby.partition_broadcast(P)).then_inc(consts_in, 16)
            for b in range(B):
                sp.dma_start(tok[:, b * TT:(b + 1) * TT, :], xt[:, b * TT:(b + 1) * TT, :]).then_inc(x_in[b], 16)

            def load_group(g, s):
                sp.dma_start(tr_raw[:, s], ctx_tr[g]).then_inc(tr_in[s], 16)
                sp.dma_start(nat_raw[:, s], ctx_nat[g]).then_inc(nat_in[s], 16)

            for s in range(2):
                load_group(s, s)
            sp.dma_start(w_raw[:, :, :, :], w_qkv[0]).then_inc(w_in, 16)
            sp.dma_start(row_in[:, :, :], rows.partition_broadcast(P)).then_inc(row_in_done, 16)
            sp.dma_start(b_all[:, :, :], b_qkv).then_inc(row_in_done, 16)
            sp.wait_ge(zero_set, 1)
            sp.dma_start(z_slots.rearrange("(b p) d -> p b d", p=P),
                         zero[:, :].unsqueeze(1).to_broadcast([P, NB, D])).then_inc(zeroed, 16)
            with sp.Fori(1, B * NG // 2) as i:
                for s in range(2):
                    sp.wait_ge(cT_lo_done, i * (2 * GT) + (s - 1) * GT)
                    sp.wait_ge(cN_lo_done, i * (2 * GT) + (s - 1) * GT)
                    load_group(i * 2 + s, s)

            def stack(grp, j, seen):
                rows_j = slice(DH * j, DH * j + DH)
                for st, m, halves in ((q_st, 0, (qk_hi, qk_hi, qk_lo, qk_lo)), (k_st, 1, (qk_hi, qk_lo, qk_hi, qk_lo))):
                    for c, half in enumerate(halves):
                        sp.dma_start(st[DH * c:DH * c + DH, j, :].bitcast(F32), half[rows_j, m, :].bitcast(F32)).then_inc(stack_in[j], 16)

            for u in (FIRST_USES["Q"], FIRST_USES["K"]):
                sp.wait_ge(pair_read[u % 2], first_reads(u))
            for j in range(HG):
                stack(0, j, None)
            with sp.Fori(0, NGRP - 1) as grp:
                sp.wait_ge(w_lo_done, grp * 2 + 2)
                sp.dma_start(w_raw[:, :, :, :], w_qkv[grp + 1]).then_inc(w_in, 16)
                sp.wait_ge(pair_read[slot_of("K")], reads(grp, "K"))
                for j in range(HG):
                    sp.wait_ge(s_done, grp * (2 * GH) + (4 * j + 4))
                    stack(grp + 1, j, None)
            sp.wait_ge(proj_done, 3 * NGRP)
            sp.dma_start(wo_raw[:, :, :], w_o).then_inc(wo_in, 16)


            sp.wait_ge(wo_done, NT)
            sp.dma_start(tri_one[:, :, :], consts[:, C_TRI:C_DEC].rearrange("p (a c) -> p a c", a=2))\
                .then_inc(router_in, 16)
            sp.dma_start(rcst[:, :], consts[:, C_DEC:C_END]).then_inc(router_in, 16)
            sp.dma_start(rw[:, :, :], router).then_inc(router_in, 16)

            def load_piece(pc, e):
                sp.dma_start(raw[pc][:, :], (ffn0, ffn1, ffn2)[pc[1]][e, "gud".index(pc[0])])\
                    .then_inc(piece_in[pc], 16)

            sp.wait_ge(routed, 1)
            e0 = sp.value_load(blk_i[0:1, 0:1], min_val=0, max_val=E - 1)
            for n, pc in enumerate(EARLY):
                load_piece(pc, e0)
                if n == 2:
                    sp.wait_ge(scattered, 16 * NT)
                    sp.dma_start(zb[:, :], z_slots[0:P, :]).then_inc(zb_in, 16)

            def load_next(b, pieces, e, new):
                with sp.If(new):
                    for pc in pieces:
                        sp.wait_ge({"g": gate_done, "u": up_done, "d": down_done}[pc[0]], b * 3 + (pc[1] + 1))
                        load_piece(pc, e)
                with sp.Else():
                    for pc in pieces:
                        count_on(sp, piece_in[pc], b * 16 + 16, 16)

            def load_tokens(b):
                sp.wait_ge(zb_turned, b)
                sp.dma_start(zb[:, :], z_slots[bass.ds(b * P, P), :]).then_inc(zb_in, 16)

            def store(b):
                sp.wait_ge(y_read, b + 1)
                sp.dma_start(y_slots[bass.ds(b * P, P), :], yb[:, :]).then_inc(y_stored, 16)

            def body(b, first=False, last=False):
                e_now = sp.value_load(blk_i[0:1, bass.ds(b, 1)], min_val=0, max_val=E - 1)
                if not last:
                    e_next = sp.value_load(blk_i[0:1, bass.ds(b + 1, 1)], min_val=0, max_val=E - 1)
                    new_next = flag(sp, new_i, b + 1)
                    load_tokens(b + 1)
                    load_next(b, PIECES[0:2], e_next, new_next)
                if first:
                    load_piece(("d", 2), e_now)
                else:
                    new_now = flag(sp, new_i, b)
                    with sp.If(new_now):
                        sp.wait_ge(down_done, b * 3)
                        load_piece(("d", 2), e_now)
                    with sp.Else():
                        count_on(sp, piece_in["d", 2], b * 16, 16)
                if not last:
                    load_next(b, PIECES[3:5], e_next, new_next)
                if not first:
                    store(b - 1)
                if not last:
                    load_next(b, PIECES[5:], e_next, new_next)

            def tail_body(b, last=False):
                with sp.If(flag(sp, used_i, b)):
                    body(b, last=last)
                    sp.wait_ge(routed, 2)
                with sp.Else():
                    if not last:
                        count_on(sp, zb_in, b * 16 + 16, 16)
                        for pc in PIECES:
                            count_on(sp, piece_in[pc], b * 16 + (0 if pc == ("d", 2) else 16), 16)
                    store(b - 1)

            body(0, first=True)
            with sp.Fori(1, USED) as b:
                body(b)
            with sp.Fori(USED, NB - 1) as b:
                tail_body(b)
            tail_body(NB - 1, last=True)
            store(NB - 1)
            for t in range(NT):
                sp.wait_ge(summed, t + 1)
                sp.dma_start(out[t * P:(t + 1) * P, :], res[:, t]).then_inc(stored, 16)
            sp.wait_ge(stored, 16 * NT)

        @block.scalar
        def _(act):
            for b in range(B):
                act.wait_ge(ln_var, (b + 1))
                act.activation(rstd[:, b * TT:(b + 1) * TT], mv[:, b * TT:(b + 1) * TT, 1], ACT.Sqrt)\
                   .then_inc(ln_std, 1)
            for t in range(NT):
                act.wait_ge(norm_turned, t + 1)
                act.activation(xT_hi[:, :, t * P:(t + 1) * P],
                               h_bank[t % 4].rearrange("p (k t) -> p k t", k=KT), ACT.Copy)\
                   .then_inc(turn_hi, 1)

            def split(n, i, j):
                s = j // GT
                act.wait_ge(tr_in[s], i * 16 + 16)
                act.activation(cT_hi[:, j], tr_raw[:, s, :, (j % GT) * P:(j % GT + 1) * P], ACT.Copy)\
                   .then_inc(cT_hi_done, 1)
                act.wait_ge(nat_in[s], i * 16 + 16)
                act.activation(cN_hi[:, j], nat_raw[:, s, j % GT], ACT.Copy).then_inc(cN_hi_done, 1)

            def gelu(n, j):
                act.wait_ge(h_done, n + 1)
                act.wait_ge(g_free, n + 1)
                act.activation(g_full[:, j % GRING], h_bank[j % 4], ACT.Gelu_apprx_tanh)
                act.activation(g_hi[:, j % GRING], h_bank[j % 4], ACT.Gelu_apprx_tanh).then_inc(g_hi_done, 1)

            for j in range(AHEAD):
                split(j, 0, j)
            with act.Fori(0, NF // RING - 1) as i:
                for j in range(RING):
                    gelu(i * RING + j, j)
                    split(None, i + (j + AHEAD) // RING, (j + AHEAD) % RING)
            for j in range(RING):
                gelu(NF - RING + j, j)
                if j + AHEAD < RING:
                    split(None, NF // RING - 1, j + AHEAD)

            for q in range(2):
                act.wait_ge(wrapped, q + 1)
                act.activation(pe_tab[:, :, q::2], (ang, ang2)[q][:, :, :], ACT.Sin).then_inc(encoded, 1)
            sq = [0]

            def root(to, mv_x, b, ready, n, done, bias=0.0):
                act.wait_ge(ready, n)
                act.activation(to[:, b * TT:(b + 1) * TT], mv_x[:, b * TT:(b + 1) * TT, 1], ACT.Sqrt)\
                   .then_inc(done, 1)

            for b in range(B):
                root(rstd2, mv2, b, ln_var, B + b + 1, ln_std)

            def w_high(grp):
                act.wait_ge(w_in, grp * 16 + 16)
                act.activation(w_hi[:, 0], w_raw[:, 0], ACT.Copy, scale=fac[:, 0:1]).then_inc(w_hi_done, 1)
                act.activation(w_hi[:, 1:3], w_raw[:, 1:3], ACT.Copy).then_inc(w_hi_done, 1)

            act.wait_ge(fac_step, FAC_STEPS)
            w_high(0)
            for t in range(NT):
                act.wait_ge(norm_turned, NT + t + 1)
                act.activation(yT_hi[:, :, t * P:(t + 1) * P],
                               h_bank[t % 4].rearrange("p (k t) -> p k t", k=KT), ACT.Copy)\
                   .then_inc(turn_hi, 1)

            def qk_high(m, grp, pr):
                act.wait_ge(proj_done, grp * 3 + (m + 1))
                for j in range(HG):
                    if not isinstance(grp, int) or grp:
                        act.wait_ge(stack_in[j], grp * 128)
                act.activation(qk_hi[:, m, :], pair[pr].rearrange("p a t -> p (a t)"), ACT.Identity,
                               bias=b_all[:, m, bass.ds(grp, 1)]).then_inc(qk_hi_done, 1)

            def v_out(grp, pr):
                act.wait_ge(proj_done, grp * 3 + 3)
                act.activation(vT[:, :], pair[pr].rearrange("p a t -> p (a t)"), ACT.Identity,
                               bias=b_all[:, 2, bass.ds(grp, 1)]).then_inc(pair_read[pr], 1)

            def exps(n, par, h, p, pr):
                act.wait_ge(max_done, n * 2 + p + 1)
                b, j = h % B, h // B
                for q in (2 * p, 2 * p + 1):
                    e = act.activation(prob[:, par, q, :], pair[pr][:, q % 2, :], ACT.Exp,
                                       bias=nmax[:, par, q:q + 1], accum_out=sums[:, b, q, j:j + 1])
                e.then_inc(pair_read[pr], 1)

            def turned(n, par, q):
                act.wait_ge(tr_done, n * 4 + q + 1)
                act.activation(probT[:, par, :, q * P:(q + 1) * P],
                               pt_bank[q % 2].rearrange("p (k t) -> p k t", k=TT), ACT.Copy)\
                   .then_inc(pt_read[q % 2], 1)

            qk_high(0, 0, 1)
            qk_high(1, 0, 0)
            v_out(0, 1)
            exps(0, 0, 0, 0, 0)
            exps(0, 0, 0, 1, 1)
            exps(1, 1, 1, 0, 0)
            turned(0, 0, 1)
            exps(1, 1, 1, 1, 1)
            turned(0, 0, 3)

            def body(grp, last):
                if not last:
                    w_high(grp + 1)
                act.wait_ge(v_turned, grp + 1)
                pr = slot_of("turn", last)
                act.activation(v_tok[:, :, :], pair[pr].rearrange("p a (k d) -> p (a k) d", d=P), ACT.Copy)\
                   .then_inc(pair_read[pr], 1)
                for s in range(GH):
                    n = grp * GH + s
                    for p in range(2):
                        if (s + 2, p) in (LAST_BODY if last else FULL_BODY):
                            exps(n + 2, s % 2, (s + 2) % GH, p, slot_of((s + 2, p), last))
                        if s == GH - 1 and p == 0:
                            act.wait_ge(r_turned, grp + 1)
                            for b in range(B):
                                act.activation(r_all[:, b, :], pt_bank[b], ACT.Copy).then_inc(pt_read[b], 1)
                        if not (last and s == GH - 1):
                            turned(n + 1, (s + 1) % 2, 2 * p + 1)
                    if not last and s in (1, 2):
                        qk_high(s - 1, grp + 1, slot_of("QK"[s - 1]))
                    if not last and s == 3:
                        v_out(grp + 1, slot_of("V"))

            with act.Fori(0, NGRP - 1) as grp:
                body(grp, False)
            act.wait_ge(wo_in, 16)
            act.activation(wo_hi[:, :, :], wo_raw[:, :, :], ACT.Copy).then_inc(wo_hi_done, 1)
            body(NGRP - 1, True)

            for t in range(NT):
                if t == 0:
                    for b in range(B):
                        act.wait_ge(ot_free[b], NGRP + 1)
                if t >= 2:
                    act.wait_ge(wo_done, t - 1)
                act.activation(o_hi[:, t % 2], oT[:, :, t * P:(t + 1) * P], ACT.Copy).then_inc(o_hi_done, 1)
            for b in range(B):
                act.wait_ge(var3, b + 1)
                act.activation(rstd3[:, b * TT:(b + 1) * TT], mv3[:, b * TT:(b + 1) * TT, 1], ACT.Sqrt,
                               bias=fac[:, 2:3]).then_inc(std3, 1)

            for b in range(B):
                root(rstd4, mv4, b, var4, b + 1, std4)
            for t in range(NT):
                act.wait_ge(z_turned, t + 1)
                if t >= 2:
                    act.wait_ge(logit_done, t - 1)
                act.activation(zT[:, t % 2], h_bank[t % 4].rearrange("p (k t) -> p k t", k=KT), ACT.Copy)\
                   .then_inc(zT_done, 1)
            act.sem_inc(y_stored, 16)

            def high(b, pc):
                act.wait_ge(piece_in[pc], b * 16 + 16)
                act.activation(half_hi[pc][:, :], raw[pc][:, :], ACT.Copy).then_inc(half_hi_done, 1)

            def high_if(b, pc, new):
                if new is None:
                    return high(b, pc)
                with act.If(new):
                    high(b, pc)
                with act.Else():
                    count_on(act, half_hi_done, piece_no(b, pc) - 1, 1)

            def zb_high(b):
                act.wait_ge(zb_turned, b + 1)
                act.activation(zbT_hi[:, :, :], turn_bank.rearrange("p (k t) -> p k t", k=KT), ACT.Copy)\
                   .then_inc(zb_hi_done, 1)

            def hid_high(q, c):
                act.wait_ge(hid_turned, q + 1)
                act.activation(hT_hi[:, 0:CH[c]], turn_bank[:, 0:CH[c] * P].rearrange("p (i t) -> p i t", t=P),
                               ACT.Copy).then_inc(hT_hi_done, 1)

            def y_out(b):
                act.wait_ge(down_done, b * 3 + 3)
                act.wait_ge(y_stored, b * 16 + 16)
                act.activation(yb[:, :], y_bank, ACT.Copy).then_inc(y_read, 1)

            act.wait_ge(scattered, 16 * NT)
            for pc in SPLIT_FIRST[:2]:
                high(0, pc)
            zb_high(0)
            for pc in SPLIT_FIRST[2:]:
                high(0, pc)

            def body(b, first=False, last=False):
                new_now = None if first else flag(act, new_i, b)
                new_next = None if last else flag(act, new_i, b + 1)
                for c in range(3):
                    act.wait_ge(gate_done, b * 3 + (c + 1))
                    if not (first and c == 0):
                        act.wait_ge(hid_done, b * 3 + c)
                    act.activation(sil[:, 0:CH[c] * P], g_bank[c][:, 0:CH[c] * P], ACT.Silu).then_inc(silu_done, 1)
                    if not (first and c == 0):
                        hid_high(b * 3 + (c - 1), (c - 1) % 3)
                    for n, (pc, ahead) in enumerate(SPLITS[c]):
                        if not (last and ahead):
                            high_if(b + ahead, pc, (new_now, new_next)[ahead])
                        if n == 1 and c == 2 and not last:
                            zb_high(b + 1)
                    if c == 0 and not first:
                        y_out(b - 1)

            def tail_body(b, last=False):
                with act.If(flag(act, used_i, b)):
                    body(b, last=last)
                    act.wait_ge(routed, 2)
                with act.Else():
                    hid_high(b * 3 - 1, 2)
                    y_out(b - 1)
                    if not last:
                        count_on(act, silu_done, b * 3, 3)
                        count_on(act, hT_hi_done, b * 3, 2)
                        count_on(act, half_hi_done, piece_no(b, SPLITS[0][0][0]) - 1, len(PIECES))
                        count_on(act, zb_hi_done, b + 1, 1)
                    else:
                        count_on(act, hT_hi_done, b * 3, 2)

            body(0, first=True)
            with act.Fori(1, USED) as b:
                body(b)
            with act.Fori(USED, NB - 1) as b:
                tail_body(b)
            tail_body(NB - 1, last=True)
            hid_high(3 * NB - 1, 2)
            y_out(NB - 1)

        @block.gpsimd
        def _(pool):
            steps = [0]

            def link(ins):
                steps[0] += 1
                ins.then_inc(pool_step, 1)
                pool.wait_ge(pool_step, steps[0])

            pool.wait_ge(angles, 1)
            for q, (to, turn) in enumerate(((ang2, 0.25), (ang, 0.0))):
                link(nc.gpsimd.tensor_scalar(wrap[:, :, :], ang[:, :, :], 1.0 / TWO_PI, turn, ALU.mult, ALU.add))
                link(nc.gpsimd.tensor_scalar(wrap[:, :, :], wrap[:, :, :], ROUND, None, ALU.add))
                link(nc.gpsimd.tensor_scalar(wrap[:, :, :], wrap[:, :, :], ROUND, None, ALU.subtract))
                for n, part in enumerate((PI_A, PI_B, PI_C)):
                    link(nc.gpsimd.tensor_scalar(wrap2[:, :, :], wrap[:, :, :], part, None, ALU.mult))
                    link(nc.gpsimd.tensor_tensor(to[:, :, :], (ang if n == 0 else to)[:, :, :], wrap2[:, :, :],
                                                 ALU.subtract))
                if turn:
                    link(nc.gpsimd.tensor_scalar(to[:, :, :], to[:, :, :], turn * TWO_PI, None, ALU.add))
                lim = float(np.nextafter(np.float32(math.pi), np.float32(0)))
                link(nc.gpsimd.tensor_scalar(to[:, :, :], to[:, :, :], lim, -lim, ALU.min, ALU.max))
            nc.gpsimd.tensor_scalar(to[:, 0, 0:1], to[:, 0, 0:1], 1.0, None, ALU.mult).then_inc(wrapped, 2)

            pool.wait_ge(row_in_done, 32)
            pool.wait_ge(fac_step, FAC_STEPS)
            link(nc.gpsimd.tensor_scalar(row_in[:, 1], row_in[:, 1], fac[:, 3:4], None, ALU.mult))

            pool.wait_ge(encoded, 2)
            for t in range(NT):
                pool.wait_ge(y_normed, t + 1)
                nc.gpsimd.tensor_tensor(ynorm[:, t % 4], ynorm[:, t % 4], pe_tab[:, t % TT], ALU.add)\
                    .then_inc(y_ready, 1)
            pool.wait_ge(proj_done, 3 * NGRP)
            for j in range(HG):
                pool.wait_ge(stack_in[j], 128 * NGRP)
            for t in range(NT):
                link(nc.gpsimd.tensor_scalar(y_bo[:, t], tok[:, t], mv2[:, t, 0:1], rstd2[:, t:t + 1],
                                             ALU.subtract, ALU.mult))
                link(nc.gpsimd.tensor_tensor(y_bo[:, t], y_bo[:, t], pe_tab[:, t % TT], ALU.add))
                nc.gpsimd.tensor_tensor(tok[:, t], tok[:, t], row_in[:, 2], ALU.add)
                nc.gpsimd.tensor_tensor(y_bo[:, t], y_bo[:, t], row_in[:, 0], ALU.add).then_inc(y_bo_done, 1)
            for t in range(NT):
                pool.wait_ge(n3_done, t + 1)
                nc.gpsimd.tensor_tensor(xg[:, t], xg[:, t], row_in[:, 1], ALU.mult).then_inc(g3_done, 1)

            pool.wait_ge(zeroed, 16)
            pool.wait_ge(routed, 2)
            pool.wait_ge(z_done, NT)
            for t in range(NT):
                nc.gpsimd.indirect_dma_start(
                    out=z_slots, out_offset=bass.IndirectOffsetOnAxis(ap=slot_i[:, t:t + 1], axis=0),
                    in_=xg[:, t], in_offset=None).then_inc(scattered, 16)
            pool.wait_ge(y_stored, 16 * NB + 16)
            for t in range(NT):
                nc.gpsimd.indirect_dma_start(
                    out=res[:, t], out_offset=None, in_=y_slots,
                    in_offset=bass.IndirectOffsetOnAxis(ap=slot_i[:, t:t + 1], axis=0)).then_inc(gathered[t], 16)

        @block.vector
        def _(dve):
            steps = [0]

            def link(ins):
                steps[0] += 1
                ins.then_inc(ln_step, 1)
                dve.wait_ge(ln_step, steps[0])

            nc.vector.memset(zero[:, :], 0.0).then_inc(zero_set, 1)

            dve.wait_ge(consts_in, 48)
            facs = [0]

            def fac_link(ins):
                facs[0] += 1
                ins.then_inc(fac_step, 1)
                dve.wait_ge(fac_step, facs[0])

            red, blue, yellow = (rby_all[:, c:c + 1] for c in range(3))
            ts = nc.vector.tensor_scalar
            fac_link(ts(fac[:, 5:6], red, 0.1, 1.0, ALU.mult, ALU.add))
            fac_link(nc.vector.scalar_tensor_tensor(fac[:, 0:1], blue, 0.05, fac[:, 5:6], ALU.mult, ALU.add))
            fac_link(nc.vector.scalar_tensor_tensor(fac[:, 6:7], yellow, 0.15, fac[:, 0:1], ALU.mult, ALU.add))
            fac_link(ts(fac[:, 0:1], fac[:, 6:7], DH ** -0.5, None, ALU.mult))
            fac_link(ts(fac[:, 1:2], yellow, EPS_ADAPTIVE, 1.0, ALU.mult, ALU.add))
            fac_link(ts(fac[:, 2:3], blue, 0.1 * LN_EPS, LN_EPS, ALU.mult, ALU.add))
            fac_link(nc.vector.scalar_tensor_tensor(fac[:, 3:4], yellow, 0.05, fac[:, 5:6], ALU.mult, ALU.add))
            fac_link(ts(fac[:, 4:5], yellow, PHASE_MOD, 1.0, ALU.mult, ALU.add))
            fac_link(ts(cst[:, TT:], cst[:, TT:], fac[:, 4:5], None, ALU.mult))
            fac_link(nc.vector.reciprocal(cst[:, TT:], cst[:, TT:]))
            assert facs[0] == FAC_STEPS
            nc.vector.tensor_tensor(ang[:, :, :], cst[:, 0:TT].unsqueeze(2).to_broadcast([P, TT, D // 2]),
                                    cst[:, TT:].unsqueeze(1).to_broadcast([P, TT, D // 2]), ALU.mult)\
                .then_inc(angles, 1)

            def layer_stats(b, mv=mv, src=tok, done=ln_var, eps=LN_EPS):
                for t in range(b * TT, (b + 1) * TT):
                    link(nc.vector.bn_stats(stats[:, t], src[:, t]))
                    link(nc.vector.bn_aggr(mv[:, t], stats[:, t]))
                nc.vector.tensor_scalar(mv[:, b * TT:(b + 1) * TT, 1], mv[:, b * TT:(b + 1) * TT, 1],
                                        eps, None, ALU.add).then_inc(done, 1)

            def layer_scale(b, n_std):
                dve.wait_ge(ln_std, n_std)
                link(nc.vector.reciprocal(rstd[:, b * TT:(b + 1) * TT], rstd[:, b * TT:(b + 1) * TT]))

            for b in range(B):
                dve.wait_ge(x_in[b], 16)
                layer_stats(b)
            for b in range(B):
                layer_scale(b, b + 1)
            for t in range(NT):
                if t >= 2:
                    dve.wait_ge(norm_turned, t - 1)
                nc.vector.tensor_scalar(norm[:, t % 2], tok[:, t], mv[:, t, 0:1], rstd[:, t:t + 1],
                                        ALU.subtract, ALU.mult).then_inc(normed, 1)
                dve.wait_ge(turn_hi, t + 1)
                nc.vector.tensor_tensor(xT_lo[:, :, t * P:(t + 1) * P],
                                        h_bank[t % 4].rearrange("p (k t) -> p k t", k=KT),
                                        xT_hi[:, :, t * P:(t + 1) * P].bitcast(F32), ALU.subtract)\
                    .then_inc(turn_lo, 1)

            def split(n, i, j):
                s = j // GT
                dve.wait_ge(cT_hi_done, n + 1)
                nc.vector.tensor_tensor(cT_lo[:, j], tr_raw[:, s, :, (j % GT) * P:(j % GT + 1) * P],
                                        cT_hi[:, j].bitcast(F32), ALU.subtract).then_inc(cT_lo_done, 1)
                dve.wait_ge(cN_hi_done, n + 1)
                nc.vector.tensor_tensor(cN_lo[:, j], nat_raw[:, s, j % GT],
                                        cN_hi[:, j].bitcast(F32), ALU.subtract).then_inc(cN_lo_done, 1)

            def gelu_low(n, j):
                dve.wait_ge(g_hi_done, n + 1)
                nc.vector.tensor_tensor(g_lo[:, j % GRING], g_full[:, j % GRING],
                                        g_hi[:, j % GRING].bitcast(F32), ALU.subtract).then_inc(g_lo_done, 1)

            def residual(b):
                dve.wait_ge(g_free, (b + 1) * NG * GT + GRING)
                for t in range(TT):
                    nc.vector.tensor_tensor(tok[:, b * TT + t], tok[:, b * TT + t], o_bank[t], ALU.add)\
                        .then_inc(o_read, 1)

            for j in range(AHEAD):
                split(j, 0, j)
            per = NF // RING // B
            for b in range(B):
                with dve.Fori(b * per, (b + 1) * per - b) as i:
                    for j in range(RING):
                        gelu_low(i * RING + j, j)
                        split(i * RING + j + AHEAD, i + (j + AHEAD) // RING, (j + AHEAD) % RING)
                if b == B - 1:
                    for j in range(RING):
                        gelu_low(NF - RING + j, j)
                        if j + AHEAD < RING:
                            split(NF - RING + j + AHEAD, NF // RING - 1, j + AHEAD)
                residual(b)

            for b in range(B):
                layer_stats(b, mv2)
            for b in range(B):
                bs = slice(b * TT, (b + 1) * TT)
                dve.wait_ge(ln_std, B + b + 1)
                link(nc.vector.reciprocal(rstd2[:, bs], rstd2[:, bs]))

            def y_tile(t):
                if t >= 4:
                    dve.wait_ge(norm_turned, NT + t - 3)
                nc.vector.tensor_scalar(ynorm[:, t % 4], tok[:, t], mv2[:, t, 0:1], rstd2[:, t:t + 1],
                                        ALU.subtract, ALU.mult).then_inc(y_normed, 1)

            y_tile(0)
            y_tile(1)

            def w_low(grp):
                dve.wait_ge(w_hi_done, grp * 2 + 1)
                nc.vector.scalar_tensor_tensor(w_lo[:, 0], w_raw[:, 0], fac[:, 0:1], w_hi[:, 0].bitcast(F32),
                                               ALU.mult, ALU.subtract).then_inc(w_lo_done, 1)
                dve.wait_ge(w_hi_done, grp * 2 + 2)
                nc.vector.tensor_tensor(w_lo[:, 1:3], w_raw[:, 1:3], w_hi[:, 1:3].bitcast(F32),
                                        ALU.subtract).then_inc(w_lo_done, 1)

            link(ts(b_all[:, 0], b_all[:, 0], fac[:, 0:1], None, ALU.mult))
            w_low(0)
            for t in range(NT):
                if t + 2 < NT:
                    y_tile(t + 2)
                dve.wait_ge(turn_hi, NT + t + 1)
                nc.vector.tensor_tensor(yT_lo[:, :, t * P:(t + 1) * P],
                                        h_bank[t % 4].rearrange("p (k t) -> p k t", k=KT),
                                        yT_hi[:, :, t * P:(t + 1) * P].bitcast(F32), ALU.subtract)\
                    .then_inc(turn_lo, 1)

            def qk_low(m, grp, pr):
                dve.wait_ge(qk_hi_done, grp * 2 + (m + 1))
                nc.vector.scalar_tensor_tensor(qk_lo[:, m, :], pair[pr].rearrange("p a t -> p (a t)"),
                                               b_all[:, m, bass.ds(grp, 1)], qk_hi[:, m, :].bitcast(F32),
                                               ALU.add, ALU.subtract).then_inc(pair_read[pr], 1)

            def maxima(n, par, p, pr):
                dve.wait_ge(s_done, n * 2 + p + 1)
                nc.vector.tensor_reduce(nmax[:, par, 2 * p:2 * p + 2], pair[pr], AX.X, ALU.max, negate=True)\
                    .then_inc(max_done, 1)

            def turned(n, par, q):
                dve.wait_ge(tr_done, n * 4 + q + 1)
                nc.vector.tensor_copy(probT[:, par, :, q * P:(q + 1) * P],
                                      pt_bank[q % 2].rearrange("p (k t) -> p k t", k=TT))\
                    .then_inc(pt_read[q % 2], 1)

            qk_low(0, 0, 1)
            qk_low(1, 0, 0)
            maxima(0, 0, 0, 0)
            maxima(0, 0, 1, 1)
            maxima(1, 1, 0, 0)
            turned(0, 0, 0)
            maxima(1, 1, 1, 1)
            turned(0, 0, 2)

            def body(grp, last):
                if not last:
                    w_low(grp + 1)
                for s in range(GH):
                    n = grp * GH + s
                    if s == GH - 2:
                        dve.wait_ge(pair_read[slot_of((GH - 1, 1), last)], reads(grp, (GH - 1, 1), last))
                        nc.vector.reciprocal(recip[:, :, :, :], sums[:, :, :, :]).then_inc(r_step, 1)
                        dve.wait_ge(r_step, grp * 3 + 1)
                        ts(recip[:, :, :, :], recip[:, :, :, :], fac[:, 1:2], None, ALU.mult).then_inc(r_step, 1)
                        dve.wait_ge(r_step, grp * 3 + 2)
                        nc.vector.tensor_copy(
                            r_wide[:, :, :].rearrange("p m (j d) -> p m j d", d=DH),
                            recip[:, :, :, :].rearrange("p b q j -> p (b q) j").unsqueeze(3)
                            .to_broadcast([P, B * TT, HG, DH])).then_inc(r_step, 1)
                    for p in range(2):
                        if (s + 2, p) in (LAST_BODY if last else FULL_BODY):
                            maxima(n + 2, s % 2, p, slot_of((s + 2, p), last))
                        if not (last and s == GH - 1):
                            turned(n + 1, (s + 1) % 2, 2 * p)
                    if not last and s in (1, 2):
                        qk_low(s - 1, grp + 1, slot_of("QK"[s - 1]))
                dve.wait_ge(pv_done, grp * GH + GH)
                for b in range(B):
                    dve.wait_ge(pt_read[b], grp * 17 + 17)
                    nc.vector.tensor_tensor(oT[:, bass.ds(grp, 1), b * T:(b + 1) * T].squeeze(1), ot_bank[b], r_all[:, b, :],
                                            ALU.mult).then_inc(ot_free[b], 1)

            with dve.Fori(0, NGRP - 1) as grp:
                body(grp, False)
            dve.wait_ge(wo_hi_done, 1)
            nc.vector.tensor_tensor(wo_lo[:, :, :], wo_raw[:, :, :], wo_hi[:, :, :].bitcast(F32), ALU.subtract)\
                .then_inc(wo_lo_done, 1)
            body(NGRP - 1, True)

            def o_low(t):
                dve.wait_ge(o_hi_done, t + 1)
                nc.vector.tensor_tensor(o_lo[:, t % 2], oT[:, :, t * P:(t + 1) * P], o_hi[:, t % 2].bitcast(F32),
                                        ALU.subtract).then_inc(o_lo_done, 1)

            def attended(t):
                dve.wait_ge(wo_done, t + 1)
                dve.wait_ge(y_bo_done, t + 1)
                nc.vector.tensor_tensor(xa[:, t], bank[t % 4], y_bo[:, t], ALU.add).then_inc(wo_read, 1)
                dve.wait_ge(wo_read, t + 1)

            o_low(0)
            for b in range(B):
                for t in range(b * TT, (b + 1) * TT):
                    if t + 1 < NT:
                        o_low(t + 1)
                    attended(t)
                layer_stats(b, mv3, xa, var3, 0.0)
            for b in range(B):
                bs = slice(b * TT, (b + 1) * TT)
                dve.wait_ge(std3, b + 1)
                link(nc.vector.reciprocal(rstd3[:, bs], rstd3[:, bs]))
                for t in range(b * TT, (b + 1) * TT):
                    ts(xg[:, t], xa[:, t], mv3[:, t, 0:1], rstd3[:, t:t + 1], ALU.subtract, ALU.mult)\
                        .then_inc(n3_done, 1)
            for t in range(NT):
                dve.wait_ge(g3_done, t + 1)
                nc.vector.tensor_tensor(tok[:, t], tok[:, t], xg[:, t], ALU.add).then_inc(x3_done, 1)

            for b in range(B):
                dve.wait_ge(x3_done, (b + 1) * TT)
                layer_stats(b, mv4, tok, var4)
            for b in range(B):
                bs = slice(b * TT, (b + 1) * TT)
                dve.wait_ge(std4, b + 1)
                link(nc.vector.reciprocal(rstd4[:, bs], rstd4[:, bs]))
                for t in range(b * TT, (b + 1) * TT):
                    ts(xg[:, t], tok[:, t], mv4[:, t, 0:1], rstd4[:, t:t + 1], ALU.subtract, ALU.mult)\
                        .then_inc(z_done, 1)
            tt = nc.vector.tensor_tensor
            dec = rcst[:, 0:E].unsqueeze(1).to_broadcast([P, NT, E])
            dve.wait_ge(router_in, 48)
            dve.wait_ge(logit_done, NT)
            link(nc.vector.tensor_copy(logit[:, :, :], bank[0][:, 0:NT * E].rearrange("p (t e) -> p t e", e=E)))
            link(nc.vector.tensor_reduce(best[:, :], logit[:, :, :], AX.X, ALU.max))
            link(tt(hot2[:, :, :], logit[:, :, :], best[:, :].unsqueeze(2).to_broadcast([P, NT, E]), ALU.is_ge))
            link(tt(hot2[:, :, :], hot2[:, :, :], dec, ALU.mult))
            link(nc.vector.tensor_reduce(best[:, :], hot2[:, :, :], AX.X, ALU.max))
            link(tt(hot[:, :, :], dec, best[:, :].unsqueeze(2).to_broadcast([P, NT, E]), ALU.is_equal))
            link(nc.vector.memset(before[:, 0], 0.0))
            for t in range(NT):
                link(tt(before[:, t + 1], before[:, t], hot[:, t], ALU.add))
            nc.vector.memset(base[:, 0:1], 0.0).then_inc(hot_done, 1)
            dve.wait_ge(ranked, 1)
            link(nc.vector.tensor_copy(count[:, :], bank[2][:, 0:E]))
            link(tt(over[:, :, :], count[:, :].unsqueeze(2).to_broadcast([P, E, E]),
                    rcst[:, E:2 * E].unsqueeze(1).to_broadcast([P, E, E]), ALU.is_gt))
            link(nc.vector.tensor_reduce(blocks[:, :], over[:, :, :], AX.X, ALU.add))
            for e in range(1, E):
                link(tt(base[:, e:e + 1], base[:, e - 1:e], blocks[:, e - 1:e], ALU.add))
            link(tt(at_b[:, :, :], base[:, :].unsqueeze(1).to_broadcast([P, NB, E]),
                    rcst[:, 2 * E:].unsqueeze(2).to_broadcast([P, NB, E]), ALU.is_le))
            link(nc.vector.tensor_reduce(blk[:, :], at_b[:, :, :], AX.X, ALU.add))
            link(tt(blocks_all[:, :], base[:, E - 1:E], blocks[:, E - 1:E], ALU.add))
            link(ts(used_f[:, :], rcst[:, 2 * E:], blocks_all[:, :], None, ALU.is_lt))
            link(nc.vector.memset(new_f[:, 0:1], 1.0))
            link(tt(new_f[:, 1:], blk[:, 1:], blk[:, :NB - 1], ALU.not_equal))
            link(nc.vector.tensor_copy(used_i[:, :], used_f[:, :]))
            link(tt(new_i[:, :], new_f[:, :], used_f[:, :], ALU.mult))
            ts(blk_i[:, :], blk[:, :], -1.0, None, ALU.add).then_inc(routed, 1)
            link(nc.vector.scalar_tensor_tensor(
                place_f[:, :, :], base[:, :].unsqueeze(1).to_broadcast([P, NT, E]), float(P),
                bank[1][:, 0:NT * E].rearrange("p (t e) -> p t e", e=E), ALU.mult, ALU.add))
            link(tt(place_f[:, :, :], place_f[:, :, :], hot[:, :, :], ALU.mult))
            link(nc.vector.tensor_reduce(slot_f[:, :], place_f[:, :, :], AX.X, ALU.add))
            nc.vector.tensor_copy(slot_i[:, :], slot_f[:, :]).then_inc(routed, 1)
            dve.wait_ge(routed, 2)

            def low(b, pc):
                dve.wait_ge(half_hi_done, piece_no(b, pc))
                tt(half_lo[pc][:, :], raw[pc][:, :], half_hi[pc][:, :].bitcast(F32), ALU.subtract)\
                    .then_inc(half_lo_done, 1)

            def low_if(b, pc, new):
                if new is None:
                    return low(b, pc)
                with dve.If(new):
                    low(b, pc)
                with dve.Else():
                    count_on(dve, half_lo_done, piece_no(b, pc) - 1, 1)

            def zb_low(b):
                dve.wait_ge(zb_hi_done, b + 1)
                tt(zbT_lo[:, :, :], turn_bank.rearrange("p (k t) -> p k t", k=KT), zbT_hi[:, :, :].bitcast(F32),
                   ALU.subtract).then_inc(zb_lo_done, 1)

            def hid_low(q, c):
                dve.wait_ge(hT_hi_done, q + 1)
                tt(hT_lo[:, 0:CH[c]], turn_bank[:, 0:CH[c] * P].rearrange("p (i t) -> p i t", t=P),
                   hT_hi[:, 0:CH[c]].bitcast(F32), ALU.subtract).then_inc(hT_lo_done, 1)

            for pc in SPLIT_FIRST[:2]:
                low(0, pc)
            zb_low(0)
            for pc in SPLIT_FIRST[2:]:
                low(0, pc)

            def body(b, first=False, last=False):
                new_now = None if first else flag(dve, new_i, b)
                new_next = None if last else flag(dve, new_i, b + 1)
                for c in range(3):
                    if not (first and c == 0):
                        hid_low(b * 3 + (c - 1), (c - 1) % 3)
                    for n, (pc, ahead) in enumerate(SPLITS[c]):
                        if n == 1:
                            dve.wait_ge(silu_done, b * 3 + (c + 1))
                            dve.wait_ge(up_done, b * 3 + (c + 1))
                            tt(hid[:, 0:CH[c] * P], sil[:, 0:CH[c] * P], u_bank[c][:, 0:CH[c] * P], ALU.mult)\
                                .then_inc(hid_done, 1)
                        if n == 2 and c == 2 and not last:
                            zb_low(b + 1)
                        if not (last and ahead):
                            low_if(b + ahead, pc, (new_now, new_next)[ahead])

            def tail_body(b, last=False):
                with dve.If(flag(dve, used_i, b)):
                    body(b, last=last)
                    dve.wait_ge(routed, 2)
                with dve.Else():
                    hid_low(b * 3 - 1, 2)
                    count_on(dve, hid_done, b * 3, 3)
                    count_on(dve, hT_lo_done, b * 3, 2)
                    count_on(dve, half_lo_done, piece_no(b, SPLITS[0][0][0]) - 1, 4 if last else len(PIECES))
                    if not last:
                        count_on(dve, zb_lo_done, b + 1, 1)

            body(0, first=True)
            with dve.Fori(1, USED) as b:
                body(b)
            with dve.Fori(USED, NB - 1) as b:
                tail_body(b)
            tail_body(NB - 1, last=True)
            hid_low(3 * NB - 1, 2)
            for t in range(NT):
                dve.wait_ge(gathered[t], 16)
                tt(res[:, t], res[:, t], tok[:, t], ALU.add).then_inc(summed, 1)

        @block.tensor
        def _(pe):
            pe.wait_ge(consts_in, 48)
            for t in range(NT):
                pe.wait_ge(normed, t + 1)
                if t >= 4:
                    pe.wait_ge(turn_lo, t - 3)
                for k in range(KT):
                    mm = nc.tensor.transpose(h_bank[t % 4][:, k * P:(k + 1) * P],
                                             norm[:, t % 2, k * P:(k + 1) * P], ident[:, :])
                mm.then_inc(norm_turned, 1)
            pe.sem_inc(g_free, GRING)
            pe.wait_ge(zero_set, 1)

            def first(n, j, b):
                pe.wait_ge(cT_lo_done, n + 1)
                toks = slice(b * T, (b + 1) * T)
                for k in range(KT):
                    for q, (w, v) in enumerate(((cT_hi, xT_hi), (cT_hi, xT_lo), (cT_lo, xT_hi))):
                        mm = nc.tensor.matmul(h_bank[j % 4], w[:, j, k], v[:, k, toks],
                                              start=(k == 0 and q == 0), stop=(k == KT - 1 and q == 2))
                mm.then_inc(h_done, 1)

            def second(n, j, last=False):
                pe.wait_ge(cN_lo_done, n + 1)
                pe.wait_ge(g_lo_done, n + 1)
                for t in range(TT):
                    ts = slice(t * P, (t + 1) * P)
                    for q, (w, v) in enumerate(((g_hi, cN_hi), (g_hi, cN_lo), (g_lo, cN_hi))):
                        mm = nc.tensor.matmul(o_bank[t], w[:, j % GRING, ts], v[:, j],
                                              start=False, stop=(last and q == 2), skip_group_check=True)
                mm.then_inc(g_free, 1)

            pe.wait_ge(turn_lo, NT)
            for j in range(PE_LAG):
                first(j, j, 0)
            per = NF // RING // B
            for b in range(B):
                if b:
                    pe.wait_ge(o_read, b * TT)
                for t in range(TT):
                    nc.tensor.matmul(o_bank[t], zero[:, 0:P], zero[:, :], start=True, stop=False,
                                     skip_group_check=True)
                with pe.Fori(b * per, (b + 1) * per - 1) as i:
                    for j in range(RING):
                        first(i * RING + (j + PE_LAG), (j + PE_LAG) % RING, b)
                        second(i * RING + j, j)
                n0 = ((b + 1) * per - 1) * RING
                for j in range(RING):
                    if n0 + j + PE_LAG < NF:
                        first(n0 + j + PE_LAG, (j + PE_LAG) % RING, (n0 + j + PE_LAG) // (NF // B))
                    second(n0 + j, j, j == RING - 1)


            for t in range(NT):
                pe.wait_ge(y_ready, t + 1)
                if t >= 4:
                    pe.wait_ge(turn_lo, NT + t - 3)
                for k in range(KT):
                    mm = nc.tensor.transpose(h_bank[t % 4][:, k * P:(k + 1) * P],
                                             ynorm[:, t % 4, k * P:(k + 1) * P], ident[:, :])
                mm.then_inc(norm_turned, 1)
            pe.wait_ge(turn_lo, 2 * NT)
            for b in range(B):
                pe.sem_inc(ot_free[b], 1)

            def project(m, grp, pr, before):
                if before is not None:
                    pe.wait_ge(pair_read[pr], before)
                pe.wait_ge(w_lo_done, grp * 2 + 2)
                for b in range(B):
                    toks = slice(b * T, (b + 1) * T)
                    for k in range(KT):
                        for q, (w, v) in enumerate(((w_hi, yT_hi), (w_hi, yT_lo), (w_lo, yT_hi))):
                            mm = nc.tensor.matmul(pair[pr][:, b, :], w[:, m, k], v[:, k, toks],
                                                  start=(k == 0 and q == 0), stop=(k == KT - 1 and q == 2))
                mm.then_inc(proj_done, 1)

            def scores(h, p, pr, before):
                pe.wait_ge(pair_read[pr], before)
                b, j = h % B, h // B
                for q in range(2):
                    at = b * T + (2 * p + q) * P
                    mm = nc.tensor.matmul(pair[pr][:, q, :], q_st[:, j, at:at + P], k_st[:, j, b * T:(b + 1) * T],
                                          start=True, stop=True)
                mm.then_inc(s_done, 1)

            def turn(par, q, pr, probs, before):
                pe.wait_ge(pair_read[pr], probs)
                if before is not None:
                    pe.wait_ge(pt_read[q % 2], before)
                for k in range(TT):
                    mm = nc.tensor.transpose(pt_bank[q % 2][:, k * P:(k + 1) * P],
                                             prob[:, par, q, k * P:(k + 1) * P], ident[:, :])
                mm.then_inc(tr_done, 1)

            for m in range(3):
                u = m + 1
                project(m, 0, u % 2, first_reads(u - 2) if u > 2 else None)
            pe.wait_ge(stack_in[0], 128)
            scores(0, 0, 0, first_reads(2))
            scores(0, 1, 1, first_reads(3))
            scores(1, 0, 0, first_reads(4))
            turn(0, 0, 0, first_reads(4), None)
            turn(0, 1, 0, first_reads(4), None)
            scores(1, 1, 1, first_reads(5))
            turn(0, 2, 1, first_reads(5), 1)
            turn(0, 3, 1, first_reads(5), 1)

            def body(grp, last):
                def before(what):
                    return reads(grp, what, last) - 1
                pr = slot_of("turn", last)
                pe.wait_ge(pair_read[pr], before("turn"))
                pe.wait_ge(pair_read[slot_of("V")], reads(grp - 1, "V"))
                for m in range(NT):
                    mm = nc.tensor.transpose(pair[pr][:, m // TT, (m % TT) * P:(m % TT + 1) * P],
                                             vT[:, m * P:(m + 1) * P], ident[:, :])
                mm.then_inc(v_turned, 1)
                for s in range(GH):
                    pt0 = grp * 17 + (2 + 2 * s + (s == GH - 1))
                    for p in range(2):
                        if (s + 2, p) in (LAST_BODY if last else FULL_BODY):
                            h = (s + 2) % GH
                            if h % B == 0 and p == 0:
                                pe.wait_ge(stack_in[h // B], (grp + (s + 2) // GH) * 128 + 128)
                            scores(h, p, slot_of((s + 2, p), last), before((s + 2, p)))
                        if not (last and s == GH - 1):
                            src = (s + 1, p)
                            for q in (2 * p, 2 * p + 1):
                                turn((s + 1) % 2, q, slot_of(src, last), reads(grp, src, last), pt0 + p)
                    if s == GH - 2:
                        pe.wait_ge(r_step, grp * 3 + 3)
                        for b in range(B):
                            pe.wait_ge(pt_read[b], pt0 + 2)
                            for q in range(TT):
                                mm = nc.tensor.transpose(pt_bank[b][:, q * P:(q + 1) * P], r_wide[:, b * TT + q],
                                                         ident[:, :])
                        mm.then_inc(r_turned, 1)
                    b, j = s % B, s // B
                    for i in range(2):
                        pe.wait_ge(pt_read[i], grp * 17 + (2 + 2 * s))
                    if s == 0:
                        pe.wait_ge(pair_read[slot_of("turn", last)], reads(grp, "turn", last))
                    if s < B:
                        pe.wait_ge(ot_free[b], grp + 1)
                    for k in range(TT):
                        mm = nc.tensor.matmul(ot_bank[b][DH * j:DH * j + DH, :], v_tok[:, b * TT + k, DH * j:DH * j + DH],
                                              probT[:, s % 2, k, :], start=(k == 0), stop=(k == TT - 1))
                    mm.then_inc(pv_done, 1)
                    if not last and s in (1, 2, 3):
                        what = "QKV"[s - 1]
                        project(s - 1, grp + 1, slot_of(what), before(what))

            with pe.Fori(0, NGRP - 1) as grp:
                body(grp, False)
            body(NGRP - 1, True)

            pe.wait_ge(wo_lo_done, 1)
            for t in range(NT):
                pe.wait_ge(o_lo_done, t + 1)
                if t >= 4:
                    pe.wait_ge(wo_read, t - 3)
                for k in range(KT):
                    for q, (w, v) in enumerate(((o_hi, wo_hi), (o_hi, wo_lo), (o_lo, wo_hi))):
                        mm = nc.tensor.matmul(bank[t % 4], w[:, t % 2, k], v[:, k],
                                              start=(k == 0 and q == 0), stop=(k == KT - 1 and q == 2))
                mm.then_inc(wo_done, 1)

            def z_turn(t):
                pe.wait_ge(z_done, t + 1)
                if t >= 4:
                    pe.wait_ge(zT_done, t - 3)
                for k in range(KT):
                    mm = nc.tensor.transpose(h_bank[t % 4][:, k * P:(k + 1) * P], xg[:, t, k * P:(k + 1) * P],
                                             ident[:, :])
                mm.then_inc(z_turned, 1)

            z_turn(0)
            pe.wait_ge(router_in, 48)
            for t in range(NT):
                if t + 1 < NT:
                    z_turn(t + 1)
                pe.wait_ge(zT_done, t + 1)
                for k in range(KT):
                    mm = nc.tensor.matmul(bank[0][:, t * E:(t + 1) * E], zT[:, t % 2, k], rw[:, k],
                                          start=(k == 0), stop=(k == KT - 1))
                mm.then_inc(logit_done, 1)
            pe.wait_ge(hot_done, 1)
            nc.tensor.matmul(bank[1][:, 0:NT * E], tri_one[:, 0], hot[:, :, :], start=True, stop=False)
            nc.tensor.matmul(bank[1][:, 0:NT * E], tri_one[:, 1], before[:, 0:NT, :], start=False, stop=True)
            nc.tensor.matmul(bank[2][:, 0:E], tri_one[:, 1], before[:, NT, :], start=True, stop=True)\
                .then_inc(ranked, 1)

            def zb_turn(b):
                pe.wait_ge(zb_in, b * 16 + 16)
                for k in range(KT):
                    mm = nc.tensor.transpose(turn_bank[:, k * P:(k + 1) * P], zb[:, k * P:(k + 1) * P], ident[:, :])
                mm.then_inc(zb_turned, 1)

            def up(b, what, c, to, done):
                w = CH[c] * P
                pe.wait_ge(half_lo_done, piece_no(b, (what, c)))
                hi, lo = half_hi[what, c], half_lo[what, c]
                for k in range(KT):
                    ks = slice(k * w, (k + 1) * w)
                    for q, (z, v) in enumerate(((zbT_hi, hi), (zbT_hi, lo), (zbT_lo, hi))):
                        mm = nc.tensor.matmul(to[:, 0:w], z[:, k], v[:, ks], start=(k == 0 and q == 0),
                                              stop=(k == KT - 1 and q == 2))
                mm.then_inc(done, 1)

            def hid_turn(q, c):
                pe.wait_ge(hid_done, q + 1)
                for i in range(CH[c]):
                    mm = nc.tensor.transpose(turn_bank[:, i * P:(i + 1) * P], hid[:, i * P:(i + 1) * P], ident[:, :])
                mm.then_inc(hid_turned, 1)

            def down(b, q, c):
                pe.wait_ge(hT_lo_done, q + 1)
                pe.wait_ge(half_lo_done, piece_no(b, ("d", c)))
                hi, lo = half_hi["d", c], half_lo["d", c]
                for i in range(CH[c]):
                    cols = slice(i * D, (i + 1) * D)
                    for n, (h, v) in enumerate(((hT_hi, hi), (hT_hi, lo), (hT_lo, hi))):
                        mm = nc.tensor.matmul(y_bank, h[:, i], v[:, cols], start=(c == 0 and i == 0 and n == 0),
                                              stop=(c == 2 and i == CH[c] - 1 and n == 2), skip_group_check=True)
                mm.then_inc(down_done, 1)

            zb_turn(0)

            def body(b, first=False, last=False):
                for c in range(3):
                    if c == 0:
                        pe.wait_ge(zb_lo_done, b + 1)
                    up(b, "g", c, g_bank[c], gate_done)
                    if not (first and c == 0):
                        hid_turn(b * 3 + (c - 1), (c - 1) % 3)
                    up(b, "u", c, u_bank[c], up_done)
                    if c == 2 and not last:
                        pe.wait_ge(hT_lo_done, b * 3 + 2)
                        zb_turn(b + 1)
                    if c == 1 and not first:
                        pe.wait_ge(y_read, b)
                    if not (first and c == 0):
                        down(b - 1 if c == 0 else b, b * 3 + (c - 1), (c - 1) % 3)

            def tail_body(b, last=False):
                with pe.If(flag(pe, used_i, b)):
                    body(b, last=last)
                with pe.Else():
                    pe.wait_ge(zb_lo_done, b + 1)
                    pe.wait_ge(y_read, b - 1)
                    hid_turn(b * 3 - 1, 2)
                    down(b - 1, b * 3 - 1, 2)
                    count_on(pe, hid_turned, b * 3, 2)
                    count_on(pe, down_done, b * 3, 2)
                    if not last:
                        count_on(pe, gate_done, b * 3, 3)
                        count_on(pe, up_done, b * 3, 3)
                        count_on(pe, zb_turned, b + 1, 1)

            body(0, first=True)
            with pe.Fori(1, USED) as b:
                body(b)
            with pe.Fori(USED, NB - 1) as b:
                tail_body(b)
            tail_body(NB - 1, last=True)
            hid_turn(3 * NB - 1, 2)
            down(NB - 1, 3 * NB - 1, 2)


def kernel(**inputs):
    import concourse.bacc as _bacc
    from concourse.bass_utils import run_bass_kernel_spmd as _run

    a = {k: np.ascontiguousarray(v) for k, v in inputs.items()}
    ctx = a["ctx_1024"].reshape(B * NG, GT * P, D)
    even = np.arange(0, D, 2, dtype=np.float32)
    power = np.power(np.float32(10000.0), (np.float32(2.0) * even / np.float32(D)).astype(np.float32))
    pos = (np.arange(TT)[None, :] * P + np.arange(P)[:, None]).astype(np.float32)
    row = np.concatenate([E - np.arange(E), P * np.arange(E), np.arange(NB)]).astype(np.float32)
    consts = np.concatenate([np.eye(P, dtype=np.float32), pos, np.broadcast_to(power, (P, D // 2)),
                             np.triu(np.ones((P, P), np.float32), 1), np.ones((P, P), np.float32),
                             np.broadcast_to(row, (P, row.size))], axis=1)
    gate, up = (a["L0_ffn_" + w].reshape(E, FF, KT, P).transpose(0, 3, 2, 1) for w in ("gate_w", "up_w"))
    down = a["L0_ffn_down_w"].reshape(E, D, FT, P).transpose(0, 3, 2, 1)
    edges = np.cumsum([0] + CH)
    ffn = [np.stack([gate[..., lo * P:hi * P].reshape(E, P, -1), up[..., lo * P:hi * P].reshape(E, P, -1),
                     down[:, :, lo:hi].reshape(E, P, -1)], axis=1) for lo, hi in zip(edges, edges[1:])]
    att = lambda w: a["L0_attn_" + w]
    w_qkv = np.stack([att(w) for w in ("Wq", "Wk", "Wv")]).reshape(3, NGRP, P, KT, P).transpose(1, 4, 0, 3, 2)
    arrays = {
        "x": a["x"].reshape(B * T, D),
        "ctx_nat": ctx.reshape(B * NG, GT, P, D).transpose(0, 2, 1, 3),
        "ctx_tr": ctx.reshape(B * NG, GT * P, KT, P).transpose(0, 3, 2, 1),
        "consts": consts,
        "rby": att("rby"),
        "w_qkv": w_qkv,
        "b_qkv": np.stack([att(w) for w in ("bq", "bk", "bv")]).reshape(3, NGRP, P).transpose(2, 0, 1),
        "w_o": att("Wo").reshape(D, KT, P).transpose(2, 1, 0),
        "rows": np.stack([att(w) for w in ("bo", "ln_gamma", "ln_beta")]),
        "router": a["L0_ffn_router_w"].reshape(E, KT, P).transpose(2, 1, 0),
        "ffn0": ffn[0],
        "ffn1": ffn[1],
        "ffn2": ffn[2],
    }
    arrays = {k: np.ascontiguousarray(v) for k, v in arrays.items()}
    nc = _bacc.Bacc("TRN2", target_bir_lowering=False, num_devices=1)
    args = [nc.dram_tensor(k, v.shape, mybir.dt.from_np(v.dtype), kind="ExternalInput").ap()
            for k, v in arrays.items()]
    args.append(nc.dram_tensor("y", (B * T, D), F32, kind="ExternalOutput").ap())
    build(nc, *args)
    r = _run(nc, [arrays], core_ids=[0])
    return r.results[0]["y"].reshape(B, T, D)
```

```python
import math
import numpy as np
import concourse.bass as bass
from concourse import mybir
from contextlib import ExitStack

F32 = mybir.dt.float32
F32R = mybir.dt.float32r
I32 = mybir.dt.int32
ALU = mybir.AluOpType
ACT = mybir.ActivationFunctionType
AX = mybir.AxisListType

P = 128
B, T, D = 2, 512, 512
KT = D // P
TT = T // P
NT = B * TT
F = 8192
GT = 4
NG = F // (GT * P)
NF = B * F // P
RING = 8
GRING = 4
AHEAD = 4
PE_LAG = 2
LN_EPS = 1e-5

H, DH = 16, 32
HG = P // DH
NGRP = H // HG
GH = HG * B
PHASE_MOD = 0.1 * math.sin(2.0 * math.pi * 0.25)
EPS_ADAPTIVE = 0.1 * math.sin(2.0 * math.pi * 0.5)
E, FF = 8, 1408
FT = FF // P
CH = [4, 4, 3]
assert sum(CH) == FT
NB = (B * T + E * (P - 1)) // P
PIECES = [("g", 0), ("u", 0), ("d", 2), ("g", 1), ("u", 1), ("d", 0), ("g", 2), ("u", 2), ("d", 1)]
EARLY = [pc for pc in PIECES if pc != ("d", 2)]
SPLITS = [[(("g", 2), 0), (("u", 2), 0), (("d", 1), 0)],
          [(("g", 0), 1), (("u", 0), 1), (("d", 2), 0)],
          [(("g", 1), 1), (("u", 1), 1), (("d", 0), 1)]]
USED = B * T // P
SPLIT_FIRST = [("g", 0), ("u", 0), ("g", 1), ("u", 1), ("d", 0)]
TWO_PI = 2.0 * math.pi
PI_A = 6.28125
PI_B = float(np.float32(0.0019352436065673828))
PI_C = TWO_PI - PI_A - PI_B
ROUND = 1.5 * 2.0 ** 23
C_POS = P
C_TRI = P + TT + D // 2
C_ONE = C_TRI + P
C_DEC = C_ONE + P
C_END = C_DEC + E + E + NB

S_AHEAD, T_AHEAD = 3, 1


def body_uses(part):
    uses, pos = [], 0
    for s in range(GH):
        for what in ["turn"] * (s == 0) + [(kind, s + ahead, p) for kind, ahead in (("T", T_AHEAD), ("S", S_AHEAD))
                                           for p in range(2)] + {1: ["Q"], 2: ["K"], 3: ["V"]}.get(s, []):
            ahead = what in ("Q", "K", "V") or (isinstance(what, tuple) and what[1] >= GH)
            if part == "mid" or ahead == (part == "first"):
                uses.append((what, pos % 3))
            pos += 1
    assert pos % 3 == 0
    return uses


USES = {part: body_uses(part) for part in ("first", "mid", "last")}
PAIR = dict(USES["mid"])


def uses_of(part, pr):
    return [what for what, p in USES[part] if p == pr]


def nth(grp, what, part):
    pr = PAIR[what]
    at = uses_of(part, pr).index(what) + 1
    if part == "first":
        return at
    return grp * len(uses_of("mid", pr)) + (len(uses_of("first", pr)) + at)


def nth_last_t(grp):
    pr = PAIR["T", GH, 1]
    return grp * len(uses_of("mid", pr)) + len(uses_of("first", pr))


def has(part, h=None):
    return part == "mid" or (part == "first") == (h is None or h >= GH)


FAC_STEPS = 10


def build(nc, x, ctx_nat, ctx_tr, consts, rby, w_qkv, b_qkv, w_o, rows, router, ffn0, ffn1, ffn2, out):
    ctx = ExitStack()
    with ctx:
        top = [(nc.sbuf_base + 31) // 32 * 32]

        def place(name, shape, dt, at=None):
            size = int(np.prod(shape[1:])) * 4
            if at is None:
                at = top[0]
                top[0] += (size + 31) // 32 * 32
            return nc.alloc_sbuf_tensor_at(name, shape, dt, offset=at)

        def sem(name):
            return ctx.enter_context(nc.semaphore(name))

        z_slots = nc.dram_tensor("z_slots", (NB * P, D), F32).ap()
        y_slots = nc.dram_tensor("y_slots", (NB * P, D), F32).ap()

        ident = place("ident", [P, P], F32)
        zero = place("zero", [P, D], F32)
        tok = place("tok", [P, NT, D], F32)
        stats = place("stats", [P, NT, 6], F32)
        mv = place("mv", [P, NT, 2], F32)
        rstd = place("rstd", [P, NT], F32)
        mv2 = place("mv2", [P, NT, 2], F32)
        rstd2 = place("rstd2", [P, NT], F32)
        mv3 = place("mv3", [P, NT, 2], F32)
        rstd3 = place("rstd3", [P, NT], F32)
        mv4 = place("mv4", [P, NT, 2], F32)
        rstd4 = place("rstd4", [P, NT], F32)
        early_c = top[0]
        rby_all = place("rby_all", [P, 3], F32)
        fac = place("fac", [P, 8], F32)
        cst = place("cst", [P, TT + D // 2], F32)
        b_all = place("b_all", [P, 3, NGRP], F32)
        row_in = place("row_in", [P, 3, D], F32)
        w_raw = place("w_raw", [P, 3, KT, P], F32)
        pe_at = top[0]
        pe_tab = place("pe_tab", [P, TT, D], F32)
        wrap = place("wrap", [P, TT, D // 2], F32, pe_at)
        wrap2 = place("wrap2", [P, TT, D // 2], F32, pe_at + 4096)
        phase = top[0]
        late_at = nc.sbuf_usable_end // 32 * 32 - 26 * 1024

        norm = place("norm", [P, 2, D], F32)
        xT_hi = place("xT_hi", [P, KT, NT * P], F32R)
        xT_lo = place("xT_lo", [P, KT, NT * P], F32R)
        nat_raw = place("nat_raw", [P, 2, GT, D], F32)
        ynorm_at = top[0] + 4096
        tr_raw = place("tr_raw", [P, 2, KT, GT * P], F32)
        cN_hi = place("cN_hi", [P, RING, D], F32R)
        cN_lo = place("cN_lo", [P, RING, D], F32R)
        cT_hi = place("cT_hi", [P, RING, KT, P], F32R)
        cT_lo = place("cT_lo", [P, RING, KT, P], F32R)
        g_full = place("g_full", [P, GRING, T], F32)
        g_hi = place("g_hi", [P, GRING, T], F32R)
        g_lo = place("g_lo", [P, GRING, T], F32R)
        ang = place("ang", [P, TT, D // 2], F32)
        ang2 = place("ang2", [P, TT, D // 2], F32)

        assert top[0] <= nc.sbuf_usable_end, top[0]
        top[0] = phase
        yT_at = top[0]
        yT_hi = place("yT_hi", [P, KT, NT * P], F32R)
        yT_lo = place("yT_lo", [P, KT, NT * P], F32R)
        wo_raw = place("wo_raw", [P, KT, D], F32, yT_at)
        wo_hi = place("wo_hi", [P, KT, D], F32R, yT_at + 8192)
        wo_lo = place("wo_lo", [P, KT, D], F32R, yT_at + 16384)
        w_hi = place("w_hi", [P, 3, KT, P], F32R)
        w_lo = place("w_lo", [P, 3, KT, P], F32R)
        qk_at = top[0]
        qk_hi = place("qk_hi", [P, 2, NT * P], F32R)
        qk_lo = place("qk_lo", [P, 2, NT * P], F32R)
        y_bo = place("y_bo", [P, NT, D], F32, qk_at)
        vT = place("vT", [P, NT * P], F32)
        v_one = place("v_one", [P, NT, HG, 2 * DH], F32)
        stack_at = top[0]
        q_st = place("q_st", [P, HG, NT * P], F32R)
        k_st = place("k_st", [P, HG, NT * P], F32R)
        xa = place("xa", [P, NT, D], F32, stack_at)
        xg = place("xg", [P, NT, D], F32, late_at)
        prob_at = top[0]
        o_hi = place("o_hi", [P, 2, KT, P], F32R, prob_at)
        o_lo = place("o_lo", [P, 2, KT, P], F32R, prob_at + 4096)
        ynorm = place("ynorm", [P, 4, D], F32, ynorm_at)
        probT = place("probT", [P, 2, TT, T], F32)
        oT_all = place("oT_all", [P, 1 + KT, NT * P], F32)
        oT = oT_all[:, 1:, :]
        o_half = place("o_half", [P, 2, T], F32)
        sums = place("sums", [P, B, T], F32)
        nmax = place("nmax", [P, 2, TT], F32)
        nmax_hi = place("nmax_hi", [P, 2, TT], F32R)
        lead = place("lead", [P, 2, TT, DH], F32)
        two_one = place("two_one", [P, 1], F32)
        assert top[0] <= nc.sbuf_usable_end, top[0]

        rt_at = late_at + 16384
        tri_one = place("tri_one", [P, 2, P], F32, rt_at)
        rcst = place("rcst", [P, 2 * E + NB], F32, rt_at + 1024)
        rw = place("rw", [P, KT, E], F32, rt_at + 1280)
        zT = place("zT", [P, 2, KT, P], F32, rt_at + 2048)
        tmp_at = rt_at + 6144

        def small(name, shape, dt=F32):
            nonlocal tmp_at
            t = place(name, shape, dt, tmp_at)
            tmp_at += (int(np.prod(shape[1:])) * 4 + 31) // 32 * 32
            return t

        logit = small("logit", [P, NT, E])
        best = small("best", [P, NT])
        hot = small("hot", [P, NT, E])
        hot2 = small("hot2", [P, NT, E])
        before = small("before", [P, NT + 1, E])
        count = small("count", [P, E])
        over = small("over", [P, E, E])
        blocks = small("blocks", [P, E])
        base = small("base", [P, E])
        at_b = small("at_b", [P, NB, E])
        blk = small("blk", [P, NB])
        used_f = small("used_f", [P, NB])
        new_f = small("new_f", [P, NB])
        blocks_all = small("blocks_all", [P, 1])
        place_f = small("place_f", [P, NT, E])
        slot_f = small("slot_f", [P, NT])
        assert tmp_at <= nc.sbuf_usable_end
        slot_i = place("slot_i", [P, NT], I32, early_c)
        blk_i = place("blk_i", [P, NB], I32, early_c + 32)
        used_i = place("used_i", [P, NB], I32, early_c + 96)
        new_i = place("new_i", [P, NB], I32, early_c + 160)
        c_at = early_c + 224
        used = [c_at]

        def placec(name, shape, dt):
            t = place(name, shape, dt, used[0])
            used[0] += (int(np.prod(shape[1:])) * 4 + 31) // 32 * 32
            assert used[0] <= late_at, (name, used[0])
            return t

        raw, half_lo = {}, {}
        for pc in sorted(PIECES):
            raw[pc] = place(f"{pc[0]}{pc[1]}_raw", [P, KT * CH[pc[1]] * P], F32, used[0])
            half_lo[pc] = placec(f"{pc[0]}{pc[1]}_lo", [P, KT * CH[pc[1]] * P], F32R)
        half_hi = {pc: placec(f"{pc[0]}{pc[1]}_hi", [P, KT * CH[pc[1]] * P], F32R) for pc in sorted(PIECES)}
        zb = placec("zb", [P, D], F32)
        zbT_hi = placec("zbT_hi", [P, KT, P], F32R)
        zbT_lo = placec("zbT_lo", [P, KT, P], F32R)
        sil = placec("sil", [P, 4 * P], F32)
        hid = placec("hid", [P, 4 * P], F32)
        hT_hi = placec("hT_hi", [P, 4, P], F32R)
        hT_lo = placec("hT_lo", [P, 4, P], F32R)
        yb = placec("yb", [P, D], F32)
        res = place("res", [P, NT, D], F32, c_at)

        psum = ctx.enter_context(nc.psum_tensor("psum", [P, 8, 512], F32))
        bank = [psum[:, i, :] for i in range(8)]
        o_bank, h_bank = bank[0:4], bank[4:8]
        input_bank = h_bank + [bank[6], bank[7], bank[1], bank[3]]
        norm_bank = h_bank + o_bank
        pair = [psum[:, 2 * i:2 * i + 2, :] for i in range(3)]
        lead_bank = bank[6]
        ROW0 = 3 * DH
        pv_bank = bank[7]
        g_bank, u_bank, turn_bank, y_bank = bank[0:3], bank[3:6], bank[6], bank[7]

        consts_in = sem("consts_in")
        x_in = [sem(f"x_in{b}") for b in range(B)]
        zero_set = sem("zero_set")
        ln_step = sem("ln_step")
        ln_var = sem("ln_var")
        ln_std = sem("ln_std")
        normed = sem("normed")
        norm_turned = sem("norm_turned")
        turn_hi = sem("turn_hi")
        turn_lo = sem("turn_lo")
        nat_in = [sem(f"nat_in{s}") for s in range(2)]
        tr_in = [sem(f"tr_in{s}") for s in range(2)]
        cT_hi_done = sem("cT_hi_done")
        cT_lo_done = sem("cT_lo_done")
        cN_hi_done = sem("cN_hi_done")
        cN_lo_done = sem("cN_lo_done")
        h_done = sem("h_done")
        g_hi_done = sem("g_hi_done")
        g_lo_done = sem("g_lo_done")
        g_free = sem("g_free")
        o_read = sem("o_read")
        stored = sem("stored")
        tables_in = sem("tables_in")
        fac_step = sem("fac_step")
        pool_step = sem("pool_step")
        angles = sem("angles")
        wrapped = sem("wrapped")
        encoded = sem("encoded")
        y_ready = sem("y_ready")
        y_normed = sem("y_normed")
        w_in = sem("w_in")
        w_hi_done = sem("w_hi_done")
        w_lo_done = sem("w_lo_done")
        proj_done = sem("proj_done")
        qk_hi_done = sem("qk_hi_done")
        pair_read = [sem(f"pair_read{i}") for i in range(3)]
        stack_in = [sem(f"stack_in{j}") for j in range(HG)]
        v_turned = sem("v_turned")
        s_done = sem("s_done")
        nmax_hi_done = sem("nmax_hi_done")
        recip_done = sem("recip_done")
        o_half_done = sem("o_half_done")
        lead_done = sem("lead_done")
        lead_turned = sem("lead_turned")
        shift_done = sem("shift_done")
        ones_done = sem("ones_done")
        t_done = sem("t_done")
        pv_done = sem("pv_done")
        pv_read = sem("pv_read")
        oT_done = sem("oT_done")
        wo_in = sem("wo_in")
        wo_hi_done = sem("wo_hi_done")
        wo_lo_done = sem("wo_lo_done")
        y_bo_done = sem("y_bo_done")
        o_hi_done = sem("o_hi_done")
        o_lo_done = sem("o_lo_done")
        wo_done = sem("wo_done")
        wo_read = sem("wo_read")
        var3 = sem("var3")
        std3 = sem("std3")
        gamma_done = sem("gamma_done")
        zeroed = sem("zeroed")
        router_in = sem("router_in")
        var4 = sem("var4")
        std4 = sem("std4")
        z_done = sem("z_done")
        z_turned = sem("z_turned")
        zT_done = sem("zT_done")
        logit_done = sem("logit_done")
        hot_done = sem("hot_done")
        ranked = sem("ranked")
        routed = sem("routed")
        scattered = sem("scattered")
        piece_in = {pc: sem(f"{pc[0]}{pc[1]}_in") for pc in PIECES}
        half_hi_done = sem("half_hi_done")
        half_lo_done = sem("half_lo_done")
        zb_in = sem("zb_in")
        zb_turned = sem("zb_turned")
        zb_hi_done = sem("zb_hi_done")
        zb_lo_done = sem("zb_lo_done")
        gate_done = sem("gate_done")
        up_done = sem("up_done")
        silu_done = sem("silu_done")
        hid_done = sem("hid_done")
        hid_turned = sem("hid_turned")
        hT_hi_done = sem("hT_hi_done")
        hT_lo_done = sem("hT_lo_done")
        down_done = sem("down_done")
        y_read = sem("y_read")
        y_stored = sem("y_stored")
        gathered = [sem(f"gathered{t}") for t in range(NT)]
        summed = sem("summed")

        block = ctx.enter_context(nc.Block())

        def piece_no(b, pc):
            for stage in SPLITS:
                for n, (piece, ahead) in enumerate(stage):
                    if piece == pc:
                        at = SPLITS.index(stage) * 3 + n + 1
                        if ahead and isinstance(b, int) and b == 0:
                            return SPLIT_FIRST.index(pc) + 1
                        if pc == ("d", 2) and isinstance(b, int) and b == NB - 1:
                            at -= 2
                        return b * len(PIECES) + (len(SPLIT_FIRST) + at - ahead * len(PIECES))

        def flag(eng, flags, b):
            return eng.value_load(flags[0:1, bass.ds(b, 1)], min_val=0, max_val=1)

        def count_on(eng, sem_, now, by):
            eng.wait_ge(sem_, now)
            eng.sem_inc(sem_, by)

        @block.sync
        def _(sp):
            sp.dma_start(ident[:, :], consts[:, 0:P]).then_inc(consts_in, 16)
            xt = x.rearrange("(t p) d -> p t d", p=P)
            sp.dma_start(tok[:, 0:TT, :], xt[:, 0:TT, :]).then_inc(x_in[0], 16)

            def load_group(g, s):
                sp.dma_start(tr_raw[:, s], ctx_tr[g]).then_inc(tr_in[s], 16)
                sp.dma_start(nat_raw[:, s], ctx_nat[g]).then_inc(nat_in[s], 16)

            load_group(0, 0)
            sp.dma_start(tok[:, TT:NT, :], xt[:, TT:NT, :]).then_inc(x_in[1], 16)
            load_group(1, 1)
            sp.dma_start(cst[:, :], consts[:, C_POS:C_TRI]).then_inc(tables_in, 16)
            sp.dma_start(rby_all[:, :], rby.partition_broadcast(P)).then_inc(tables_in, 16)
            sp.dma_start(w_raw[:, :, :, :], w_qkv[0]).then_inc(w_in, 16)
            sp.dma_start(row_in[:, :, :], rows.partition_broadcast(P)).then_inc(tables_in, 16)
            sp.dma_start(b_all[:, :, :], b_qkv).then_inc(tables_in, 16)
            sp.wait_ge(zero_set, 1)
            sp.dma_start(z_slots.rearrange("(b p) d -> p b d", p=P),
                         zero[:, :].unsqueeze(1).to_broadcast([P, NB, D])).then_inc(zeroed, 16)
            with sp.Fori(1, B * NG // 2) as i:
                for s in range(2):
                    sp.wait_ge(cT_lo_done, i * (2 * GT) + (s - 1) * GT)
                    sp.wait_ge(cN_lo_done, i * (2 * GT) + (s - 1) * GT)
                    load_group(i * 2 + s, s)

            def stack(grp, j):
                rows_j = slice(DH * j, DH * j + DH)
                for st, m, halves in ((q_st, 0, (qk_hi, qk_hi, qk_lo)), (k_st, 1, (qk_hi, qk_lo, qk_hi))):
                    for c, half in enumerate(halves):
                        sp.dma_start(st[DH * c:DH * c + DH, j, :].bitcast(F32), half[rows_j, m, :].bitcast(F32))\
                            .then_inc(stack_in[j], 16)

            sp.wait_ge(pair_read[PAIR["K"]], nth(-1, "K", "first"))
            for j in range(HG):
                stack(0, j)
            with sp.Fori(0, NGRP - 1) as grp:
                sp.wait_ge(w_lo_done, grp * 2 + 2)
                sp.dma_start(w_raw[:, :, :, :], w_qkv[grp + 1]).then_inc(w_in, 16)
                sp.wait_ge(pair_read[PAIR["K"]], nth(grp, "K", "mid"))
                for j in range(HG):
                    sp.wait_ge(t_done, grp * (2 * GH) + 2 * (HG + j + 1))
                    stack(grp + 1, j)
            sp.wait_ge(proj_done, 3 * NGRP)
            sp.dma_start(wo_raw[:, :, :], w_o).then_inc(wo_in, 16)

            sp.wait_ge(wo_done, NT)
            sp.dma_start(tri_one[:, :, :], consts[:, C_TRI:C_DEC].rearrange("p (a c) -> p a c", a=2))\
                .then_inc(router_in, 16)
            sp.dma_start(rcst[:, :], consts[:, C_DEC:C_END]).then_inc(router_in, 16)
            sp.dma_start(rw[:, :, :], router).then_inc(router_in, 16)

            def load_piece(pc, e):
                sp.dma_start(raw[pc][:, :], (ffn0, ffn1, ffn2)[pc[1]][e, "gud".index(pc[0])])\
                    .then_inc(piece_in[pc], 16)

            sp.wait_ge(routed, 2)
            e0 = sp.value_load(blk_i[0:1, 0:1], min_val=0, max_val=E - 1)
            for n, pc in enumerate(EARLY):
                load_piece(pc, e0)
                if n == 1:
                    sp.wait_ge(scattered, 16 * NT)
                    sp.dma_start(zb[:, :], z_slots[0:P, :]).then_inc(zb_in, 16)

            def load_next(b, pieces, e, new):
                with sp.If(new):
                    for pc in pieces:
                        sp.wait_ge({"g": gate_done, "u": up_done, "d": down_done}[pc[0]], b * 3 + (pc[1] + 1))
                        load_piece(pc, e)
                with sp.Else():
                    for pc in pieces:
                        count_on(sp, piece_in[pc], b * 16 + 16, 16)

            def load_tokens(b):
                sp.wait_ge(zb_turned, b)
                sp.dma_start(zb[:, :], z_slots[bass.ds(b * P, P), :]).then_inc(zb_in, 16)

            def store(b):
                sp.wait_ge(y_read, b + 1)
                sp.dma_start(y_slots[bass.ds(b * P, P), :], yb[:, :]).then_inc(y_stored, 16)

            def body(b, first=False, last=False):
                e_now = sp.value_load(blk_i[0:1, bass.ds(b, 1)], min_val=0, max_val=E - 1)
                if not last:
                    e_next = sp.value_load(blk_i[0:1, bass.ds(b + 1, 1)], min_val=0, max_val=E - 1)
                    new_next = flag(sp, new_i, b + 1)
                    load_tokens(b + 1)
                    load_next(b, PIECES[0:2], e_next, new_next)
                if first:
                    load_piece(("d", 2), e_now)
                else:
                    new_now = flag(sp, new_i, b)
                    with sp.If(new_now):
                        sp.wait_ge(down_done, b * 3)
                        load_piece(("d", 2), e_now)
                    with sp.Else():
                        count_on(sp, piece_in["d", 2], b * 16, 16)
                if not last:
                    load_next(b, PIECES[3:5], e_next, new_next)
                if not first:
                    store(b - 1)
                if not last:
                    load_next(b, PIECES[5:], e_next, new_next)

            def tail_body(b, last=False):
                with sp.If(flag(sp, used_i, b)):
                    body(b, last=last)
                    sp.wait_ge(routed, 2)
                with sp.Else():
                    store(b - 1)

            body(0, first=True)
            with sp.Fori(1, USED) as b:
                body(b)
            with sp.Fori(USED, NB - 1) as b:
                tail_body(b)
            tail_body(NB - 1, last=True)
            store(NB - 1)
            for t in range(NT):
                sp.wait_ge(summed, t + 1)
                sp.dma_start(out[t * P:(t + 1) * P, :], res[:, t]).then_inc(stored, 16)
            sp.wait_ge(stored, 16 * NT)

        @block.scalar
        def _(act):
            def normalised(b):
                act.wait_ge(ln_var, (b + 1))
                act.activation(rstd[:, b * TT:(b + 1) * TT], mv[:, b * TT:(b + 1) * TT, 1], ACT.Sqrt)\
                   .then_inc(ln_std, 1)
                for t in range(b * TT, (b + 1) * TT):
                    act.wait_ge(norm_turned, t + 1)
                    act.activation(xT_hi[:, :, t * P:(t + 1) * P],
                                   norm_bank[t].rearrange("p (k t) -> p k t", k=KT), ACT.Copy)\
                       .then_inc(turn_hi, 1)

            normalised(0)

            def split(i, j):
                s = j // GT
                act.wait_ge(tr_in[s], i * 16 + 16)
                act.activation(cT_hi[:, j], tr_raw[:, s, :, (j % GT) * P:(j % GT + 1) * P], ACT.Copy)\
                   .then_inc(cT_hi_done, 1)
                act.wait_ge(nat_in[s], i * 16 + 16)
                act.activation(cN_hi[:, j], nat_raw[:, s, j % GT], ACT.Copy).then_inc(cN_hi_done, 1)

            def gelu(n, j):
                act.wait_ge(h_done, n + 1)
                act.wait_ge(g_free, n + 1)
                act.activation(g_full[:, j % GRING], h_bank[j % 4], ACT.Gelu_apprx_tanh)
                act.activation(g_hi[:, j % GRING], h_bank[j % 4], ACT.Gelu_apprx_tanh).then_inc(g_hi_done, 1)

            for j in range(AHEAD):
                split(0, j)
            normalised(1)
            with act.Fori(0, NF // RING - 1) as i:
                for j in range(RING):
                    gelu(i * RING + j, j)
                    split(i + (j + AHEAD) // RING, (j + AHEAD) % RING)
            for j in range(RING):
                gelu(NF - RING + j, j)
                if j + AHEAD < RING:
                    split(NF // RING - 1, j + AHEAD)

            for q in range(2):
                act.wait_ge(wrapped, q + 1)
                act.activation(pe_tab[:, :, q::2], (ang, ang2)[q][:, :, :], ACT.Sin).then_inc(encoded, 1)

            def root(to, mv_x, b, ready, n, done, bias=0.0):
                act.wait_ge(ready, n)
                act.activation(to[:, b * TT:(b + 1) * TT], mv_x[:, b * TT:(b + 1) * TT, 1], ACT.Sqrt)\
                   .then_inc(done, 1)

            root(rstd2, mv2, 0, ln_var, B + 1, ln_std)

            def w_high(grp):
                act.wait_ge(w_in, grp * 16 + 16)
                act.activation(w_hi[:, 0], w_raw[:, 0], ACT.Copy, scale=fac[:, 0:1]).then_inc(w_hi_done, 1)
                act.activation(w_hi[:, 1:3], w_raw[:, 1:3], ACT.Copy).then_inc(w_hi_done, 1)

            for t in range(NT):
                if t == TT:
                    act.wait_ge(fac_step, FAC_STEPS)
                    w_high(0)
                    root(rstd2, mv2, 1, ln_var, B + 2, ln_std)
                act.wait_ge(norm_turned, NT + t + 1)
                act.activation(yT_hi[:, :, t * P:(t + 1) * P],
                               input_bank[t].rearrange("p (k t) -> p k t", k=KT), ACT.Copy)\
                   .then_inc(turn_hi, 1)

            def ones():
                act.wait_ge(zero_set, 2)
                for j in range(HG):
                    for b in range(B):
                        o = act.activation(k_st[ROW0:P, j, b * T:(b + 1) * T], zero[ROW0:P, :], ACT.Identity,
                                           bias=two_one[ROW0:P, :])
                o.then_inc(ones_done, 1)

            def qk_high(m, grp):
                act.wait_ge(proj_done, grp * 3 + (m + 1))
                if not isinstance(grp, int):
                    for j in range(HG):
                        act.wait_ge(stack_in[j], grp * 96)
                act.activation(qk_hi[:, m, :], pair[PAIR["QK"[m]]].rearrange("p a t -> p (a t)"), ACT.Identity,
                               bias=b_all[:, m, bass.ds(grp, 1)]).then_inc(qk_hi_done, 1)

            def v_out(grp):
                act.wait_ge(proj_done, grp * 3 + 3)
                pr = PAIR["V"]
                act.activation(vT[:, :], pair[pr].rearrange("p a t -> p (a t)"), ACT.Identity,
                               bias=b_all[:, 2, bass.ds(grp, 1)]).then_inc(pair_read[pr], 1)

            def shift(grp, h):
                act.wait_ge(lead_turned, grp * GH + (h + 1))
                b, j = h % GH // HG, h % HG
                act.activation(q_st[ROW0:P, j, b * T:(b + 1) * T], lead_bank[ROW0:P, :], ACT.Copy)\
                   .then_inc(shift_done, 1)

            def exps(grp, h, p):
                n = grp * GH + h
                act.wait_ge(t_done, n * 2 + (p + 1))
                if p == 0 and not (isinstance(n, int) and n == 0):
                    act.wait_ge(pv_done, n)
                pr = PAIR["T", h, p]
                act.activation(probT[:, h % 2, 2 * p:2 * p + 2, :], pair[pr], ACT.Exp).then_inc(pair_read[pr], 1)

            def body(grp, part):
                if part != "first":
                    act.wait_ge(v_turned, grp + 1)
                    pr = PAIR["turn"]
                    act.activation(v_one[:, :, :, 0:DH],
                                   pair[pr].rearrange("p a (k j d) -> p (a k) j d", j=HG, d=DH), ACT.Copy,
                                   scale=fac[:, 1:2]).then_inc(pair_read[pr], 1)
                for s in range(GH):
                    if has(part, s + T_AHEAD):
                        for p in range(2):
                            exps(grp, s + T_AHEAD, p)
                    if has(part, s + S_AHEAD - 1):
                        shift(grp, s + S_AHEAD - 1)
                    if has(part, s):
                        act.wait_ge(pv_done, grp * GH + (s + 2))
                        act.wait_ge(pv_read, grp * GH + (s + 1))
                        act.activation(o_half[0:2 * DH, s % 2], pv_bank[0:2 * DH, :], ACT.Copy)\
                           .then_inc(o_half_done, 1)
                    if has(part):
                        if s == 0 and part == "mid":
                            w_high(grp + 1)
                        if s in (1, 2):
                            qk_high(s - 1, grp + 1)
                        if s == 3:
                            v_out(grp + 1)
                        if s == 3 and part == "first":
                            ones()

            body(-1, "first")
            with act.Fori(0, NGRP - 1) as grp:
                body(grp, "mid")
            act.wait_ge(wo_in, 16)
            act.activation(wo_hi[:, :, :], wo_raw[:, :, :], ACT.Copy).then_inc(wo_hi_done, 1)
            body(NGRP - 1, "last")

            def root3(b):
                act.wait_ge(var3, b + 1)
                act.activation(rstd3[:, b * TT:(b + 1) * TT], mv3[:, b * TT:(b + 1) * TT, 1], ACT.Sqrt,
                               bias=fac[:, 2:3]).then_inc(std3, 1)

            act.wait_ge(oT_done, NGRP * 4)
            for t in range(NT):
                if t == TT:
                    act.wait_ge(oT_done, NGRP * 4 + 2)
                if t >= 2:
                    act.wait_ge(wo_done, t - 1)
                act.activation(o_hi[:, t % 2], oT[:, :, t * P:(t + 1) * P], ACT.Copy).then_inc(o_hi_done, 1)
                if t == TT + 1:
                    root3(0)

            root(rstd4, mv4, 0, var4, 1, std4)
            root3(1)
            root(rstd4, mv4, 1, var4, 2, std4)
            for t in range(NT):
                act.wait_ge(z_turned, t + 1)
                if t >= 2:
                    act.wait_ge(logit_done, t - 1)
                act.activation(zT[:, t % 2], h_bank[t % 4].rearrange("p (k t) -> p k t", k=KT), ACT.Copy)\
                   .then_inc(zT_done, 1)
            act.sem_inc(y_stored, 16)

            def high(b, pc):
                act.wait_ge(piece_in[pc], b * 16 + 16)
                act.activation(half_hi[pc][:, :], raw[pc][:, :], ACT.Copy).then_inc(half_hi_done, 1)

            def high_if(b, pc, new):
                if new is None:
                    return high(b, pc)
                with act.If(new):
                    high(b, pc)
                with act.Else():
                    count_on(act, half_hi_done, piece_no(b, pc) - 1, 1)

            def zb_high(b):
                act.wait_ge(zb_turned, b + 1)
                act.activation(zbT_hi[:, :, :], turn_bank.rearrange("p (k t) -> p k t", k=KT), ACT.Copy)\
                   .then_inc(zb_hi_done, 1)

            def hid_high(q, c):
                act.wait_ge(hid_turned, q + 1)
                act.activation(hT_hi[:, 0:CH[c]], turn_bank[:, 0:CH[c] * P].rearrange("p (i t) -> p i t", t=P),
                               ACT.Copy).then_inc(hT_hi_done, 1)

            def y_out(b):
                act.wait_ge(down_done, b * 3 + 3)
                act.wait_ge(y_stored, b * 16 + 16)
                act.activation(yb[:, :], y_bank, ACT.Copy).then_inc(y_read, 1)

            for pc in SPLIT_FIRST[:2]:
                high(0, pc)
            zb_high(0)
            for pc in SPLIT_FIRST[2:]:
                high(0, pc)

            def body(b, first=False, last=False):
                new_now = None if first else flag(act, new_i, b)
                new_next = None if last else flag(act, new_i, b + 1)
                for c in range(3):
                    act.wait_ge(gate_done, b * 3 + (c + 1))
                    if not (first and c == 0):
                        act.wait_ge(hid_done, b * 3 + c)
                    act.activation(sil[:, 0:CH[c] * P], g_bank[c][:, 0:CH[c] * P], ACT.Silu).then_inc(silu_done, 1)
                    if not (first and c == 0):
                        hid_high(b * 3 + (c - 1), (c - 1) % 3)
                    for n, (pc, ahead) in enumerate(SPLITS[c]):
                        if not (last and ahead):
                            high_if(b + ahead, pc, (new_now, new_next)[ahead])
                        if n == 1 and c == 2 and not last:
                            zb_high(b + 1)
                    if c == 0 and not first:
                        y_out(b - 1)

            def end(b):
                with act.If(flag(act, used_i, b)):
                    hid_high(b * 3 + 2, 2)
                    y_out(b)
                with act.Else():
                    count_on(act, y_read, b, 1)

            def tail_body(b, last=False):
                with act.If(flag(act, used_i, b)):
                    body(b, last=last)
                    act.wait_ge(routed, 2)
                with act.Else():
                    end(b - 1)
                    act.wait_ge(routed, 2)

            body(0, first=True)
            with act.Fori(1, USED) as b:
                body(b)
            with act.Fori(USED, NB - 1) as b:
                tail_body(b)
            tail_body(NB - 1, last=True)
            end(NB - 1)

        @block.gpsimd
        def _(pool):
            steps = [0]

            def link(ins):
                steps[0] += 1
                ins.then_inc(pool_step, 1)
                pool.wait_ge(pool_step, steps[0])

            pool.wait_ge(angles, 1)
            for q, (to, turn) in enumerate(((ang2, 0.25), (ang, 0.0))):
                link(nc.gpsimd.tensor_scalar(wrap[:, :, :], ang[:, :, :], 1.0 / TWO_PI, turn, ALU.mult, ALU.add))
                link(nc.gpsimd.tensor_scalar(wrap[:, :, :], wrap[:, :, :], ROUND, None, ALU.add))
                link(nc.gpsimd.tensor_scalar(wrap[:, :, :], wrap[:, :, :], ROUND, None, ALU.subtract))
                for n, part in enumerate((PI_A, PI_B, PI_C)):
                    link(nc.gpsimd.tensor_scalar(wrap2[:, :, :], wrap[:, :, :], part, None, ALU.mult))
                    link(nc.gpsimd.tensor_tensor(to[:, :, :], (ang if n == 0 else to)[:, :, :], wrap2[:, :, :],
                                                 ALU.subtract))
                if turn:
                    link(nc.gpsimd.tensor_scalar(to[:, :, :], to[:, :, :], turn * TWO_PI, None, ALU.add))
                lim = float(np.nextafter(np.float32(math.pi), np.float32(0)))
                link(nc.gpsimd.tensor_scalar(to[:, :, :], to[:, :, :], lim, -lim, ALU.min, ALU.max))
            nc.gpsimd.tensor_scalar(to[:, 0, 0:1], to[:, 0, 0:1], 1.0, None, ALU.mult).then_inc(wrapped, 2)

            pool.wait_ge(tables_in, 64)
            pool.wait_ge(fac_step, FAC_STEPS)
            nc.gpsimd.tensor_scalar(row_in[:, 1], row_in[:, 1], fac[:, 3:4], None, ALU.mult).then_inc(gamma_done, 1)

            pool.wait_ge(encoded, 2)
            for t in range(NT):
                pool.wait_ge(y_normed, t + 1)
                nc.gpsimd.tensor_tensor(ynorm[:, t % 4], ynorm[:, t % 4], pe_tab[:, t % TT], ALU.add)\
                    .then_inc(y_ready, 1)
            pool.wait_ge(proj_done, 3 * NGRP)
            for j in range(HG):
                pool.wait_ge(stack_in[j], 96 * NGRP)
            for t in range(NT):
                link(nc.gpsimd.tensor_scalar(y_bo[:, t], tok[:, t], mv2[:, t, 0:1], rstd2[:, t:t + 1],
                                             ALU.subtract, ALU.mult))
                link(nc.gpsimd.tensor_tensor(y_bo[:, t], y_bo[:, t], pe_tab[:, t % TT], ALU.add))
                nc.gpsimd.tensor_tensor(tok[:, t], tok[:, t], row_in[:, 2], ALU.add)
                nc.gpsimd.tensor_tensor(y_bo[:, t], y_bo[:, t], row_in[:, 0], ALU.add).then_inc(y_bo_done, 1)

            pool.wait_ge(zeroed, 16)
            pool.wait_ge(routed, 1)
            pool.wait_ge(z_done, NT)
            for t in range(NT):
                nc.gpsimd.indirect_dma_start(
                    out=z_slots, out_offset=bass.IndirectOffsetOnAxis(ap=slot_i[:, t:t + 1], axis=0),
                    in_=xg[:, t], in_offset=None).then_inc(scattered, 16)
            pool.wait_ge(y_stored, 16 * NB + 16)
            for t in range(NT):
                nc.gpsimd.indirect_dma_start(
                    out=res[:, t], out_offset=None, in_=y_slots,
                    in_offset=bass.IndirectOffsetOnAxis(ap=slot_i[:, t:t + 1], axis=0)).then_inc(gathered[t], 16)

        @block.vector
        def _(dve):
            steps = [0]

            def link(ins):
                steps[0] += 1
                ins.then_inc(ln_step, 1)
                dve.wait_ge(ln_step, steps[0])

            nc.vector.memset(zero[:, :], 0.0).then_inc(zero_set, 1)

            def layer_stats(b, mv=mv, src=tok, done=ln_var, eps=LN_EPS):
                tiles = range(b * TT, (b + 1) * TT)
                link([nc.vector.bn_stats(stats[:, t], src[:, t]) for t in tiles][-1])
                link([nc.vector.bn_aggr(mv[:, t], stats[:, t]) for t in tiles][-1])
                nc.vector.tensor_scalar(mv[:, b * TT:(b + 1) * TT, 1], mv[:, b * TT:(b + 1) * TT, 1],
                                        eps, None, ALU.add).then_inc(done, 1)

            def layer_scale(b, n_std):
                dve.wait_ge(ln_std, n_std)
                link(nc.vector.reciprocal(rstd[:, b * TT:(b + 1) * TT], rstd[:, b * TT:(b + 1) * TT]))

            def normalised(b):
                dve.wait_ge(x_in[b], 16)
                layer_stats(b)
                layer_scale(b, b + 1)
                for t in range(b * TT, (b + 1) * TT):
                    if t >= 2:
                        dve.wait_ge(norm_turned, t - 1)
                    nc.vector.tensor_scalar(norm[:, t % 2], tok[:, t], mv[:, t, 0:1], rstd[:, t:t + 1],
                                            ALU.subtract, ALU.mult).then_inc(normed, 1)
                    if t > b * TT:
                        turned_low(t - 1)
                turned_low((b + 1) * TT - 1)

            def turned_low(t):
                dve.wait_ge(turn_hi, t + 1)
                nc.vector.tensor_tensor(xT_lo[:, :, t * P:(t + 1) * P],
                                        norm_bank[t].rearrange("p (k t) -> p k t", k=KT),
                                        xT_hi[:, :, t * P:(t + 1) * P].bitcast(F32), ALU.subtract)\
                    .then_inc(turn_lo, 1)

            normalised(0)

            def split(n, i, j):
                s = j // GT
                dve.wait_ge(cT_hi_done, n + 1)
                nc.vector.tensor_tensor(cT_lo[:, j], tr_raw[:, s, :, (j % GT) * P:(j % GT + 1) * P],
                                        cT_hi[:, j].bitcast(F32), ALU.subtract).then_inc(cT_lo_done, 1)
                dve.wait_ge(cN_hi_done, n + 1)
                nc.vector.tensor_tensor(cN_lo[:, j], nat_raw[:, s, j % GT],
                                        cN_hi[:, j].bitcast(F32), ALU.subtract).then_inc(cN_lo_done, 1)

            def gelu_low(n, j):
                dve.wait_ge(g_hi_done, n + 1)
                nc.vector.tensor_tensor(g_lo[:, j % GRING], g_full[:, j % GRING],
                                        g_hi[:, j % GRING].bitcast(F32), ALU.subtract).then_inc(g_lo_done, 1)

            def residual(b):
                dve.wait_ge(g_free, (b + 1) * NG * GT + GRING)
                for t in range(TT):
                    nc.vector.tensor_tensor(tok[:, b * TT + t], tok[:, b * TT + t], o_bank[t], ALU.add)\
                        .then_inc(o_read, 1)
                dve.wait_ge(o_read, (b + 1) * TT)

            for j in range(AHEAD):
                split(j, 0, j)
            normalised(1)
            per = NF // RING // B
            for b in range(B):
                with dve.Fori(b * per, (b + 1) * per - b) as i:
                    for j in range(RING):
                        gelu_low(i * RING + j, j)
                        split(i * RING + j + AHEAD, i + (j + AHEAD) // RING, (j + AHEAD) % RING)
                if b == B - 1:
                    for j in range(RING):
                        gelu_low(NF - RING + j, j)
                        if j + AHEAD < RING:
                            split(NF - RING + j + AHEAD, NF // RING - 1, j + AHEAD)
                if b == 0:
                    residual(0)
                    layer_stats(0, mv2)
                    dve.wait_ge(tables_in, 64)
                    facs = [0]

                    def fac_link(ins):
                        facs[0] += 1
                        ins.then_inc(fac_step, 1)
                        dve.wait_ge(fac_step, facs[0])

                    red, blue, yellow = (rby_all[:, c:c + 1] for c in range(3))
                    ts = nc.vector.tensor_scalar
                    fac_link(ts(fac[:, 5:6], red, 0.1, 1.0, ALU.mult, ALU.add))
                    fac_link(nc.vector.scalar_tensor_tensor(fac[:, 0:1], blue, 0.05, fac[:, 5:6], ALU.mult, ALU.add))
                    fac_link(nc.vector.scalar_tensor_tensor(fac[:, 6:7], yellow, 0.15, fac[:, 0:1], ALU.mult, ALU.add))
                    fac_link(ts(fac[:, 0:1], fac[:, 6:7], DH ** -0.5, None, ALU.mult))
                    fac_link(ts(fac[:, 1:2], yellow, EPS_ADAPTIVE, 1.0, ALU.mult, ALU.add))
                    fac_link(ts(fac[:, 2:3], blue, 0.1 * LN_EPS, LN_EPS, ALU.mult, ALU.add))
                    fac_link(nc.vector.scalar_tensor_tensor(fac[:, 3:4], yellow, 0.05, fac[:, 5:6], ALU.mult, ALU.add))
                    fac_link(ts(fac[:, 4:5], yellow, PHASE_MOD, 1.0, ALU.mult, ALU.add))
                    fac_link(ts(cst[:, TT:], cst[:, TT:], fac[:, 4:5], None, ALU.mult))
                    fac_link(nc.vector.reciprocal(cst[:, TT:], cst[:, TT:]))
                    assert facs[0] == FAC_STEPS
                    nc.vector.tensor_tensor(ang[:, :, :], cst[:, 0:TT].unsqueeze(2).to_broadcast([P, TT, D // 2]),
                                            cst[:, TT:].unsqueeze(1).to_broadcast([P, TT, D // 2]), ALU.mult)\
                        .then_inc(angles, 1)

            def scale(rstd_x, b, std, n):
                dve.wait_ge(std, n)
                bs = slice(b * TT, (b + 1) * TT)
                link(nc.vector.reciprocal(rstd_x[:, bs], rstd_x[:, bs]))

            def y_tile(t):
                if t >= 4:
                    dve.wait_ge(norm_turned, NT + t - 3)
                nc.vector.tensor_scalar(ynorm[:, t % 4], tok[:, t], mv2[:, t, 0:1], rstd2[:, t:t + 1],
                                        ALU.subtract, ALU.mult).then_inc(y_normed, 1)

            def w_low(grp):
                dve.wait_ge(w_hi_done, grp * 2 + 1)
                nc.vector.scalar_tensor_tensor(w_lo[:, 0], w_raw[:, 0], fac[:, 0:1], w_hi[:, 0].bitcast(F32),
                                               ALU.mult, ALU.subtract).then_inc(w_lo_done, 1)
                dve.wait_ge(w_hi_done, grp * 2 + 2)
                nc.vector.tensor_tensor(w_lo[:, 1:3], w_raw[:, 1:3], w_hi[:, 1:3].bitcast(F32),
                                        ALU.subtract).then_inc(w_lo_done, 1)

            link(ts(b_all[:, 0], b_all[:, 0], fac[:, 0:1], None, ALU.mult))
            scale(rstd2, 0, ln_std, B + 1)
            for t in range(TT):
                y_tile(t)
            residual(1)

            def y_low(t):
                dve.wait_ge(turn_hi, NT + t + 1)
                nc.vector.tensor_tensor(yT_lo[:, :, t * P:(t + 1) * P],
                                        input_bank[t].rearrange("p (k t) -> p k t", k=KT),
                                        yT_hi[:, :, t * P:(t + 1) * P].bitcast(F32), ALU.subtract)\
                    .then_inc(turn_lo, 1)

            for t in range(TT):
                y_low(t)
            w_low(0)
            layer_stats(1, mv2)
            scale(rstd2, 1, ln_std, B + 2)
            for t in range(TT, NT):
                y_tile(t)
            for t in range(TT, NT):
                y_low(t)

            tt = nc.vector.tensor_tensor
            tt(two_one[:, :], ident[:, ROW0:ROW0 + 1], ident[:, ROW0 + 1:ROW0 + 2], ALU.add).then_inc(zero_set, 1)
            nc.vector.tensor_copy(lead[:, :, :, :], zero[:, 0:2 * TT * DH]
                                  .rearrange("p (a q d) -> p a q d", a=2, q=TT))

            def qk_low(m, grp):
                dve.wait_ge(qk_hi_done, grp * 2 + (m + 1))
                pr = PAIR["QK"[m]]
                nc.vector.scalar_tensor_tensor(qk_lo[:, m, :], pair[pr].rearrange("p a t -> p (a t)"),
                                               b_all[:, m, bass.ds(grp, 1)], qk_hi[:, m, :].bitcast(F32),
                                               ALU.add, ALU.subtract).then_inc(pair_read[pr], 1)

            def maxima(grp, h, p):
                dve.wait_ge(s_done, (grp * GH + h) * 2 + (p + 1))
                pr = PAIR["S", h, p]
                nc.vector.tensor_reduce(nmax[:, h % 2, 2 * p:2 * p + 2], pair[pr], AX.X, ALU.max, negate=True)\
                    .then_inc(pair_read[pr], 1)

            def halve(grp, h, part):
                par = h % 2
                dve.wait_ge(pair_read[PAIR["S", h, 1]], nth(grp, ("S", h, 1), part))
                nc.vector.tensor_copy(nmax_hi[:, par], nmax[:, par]).then_inc(nmax_hi_done, 1)
                dve.wait_ge(nmax_hi_done, grp * GH + (h + 1))
                nc.vector.tensor_copy(lead[:, par, :, 0], nmax_hi[:, par].bitcast(F32))
                tt(lead[:, par, :, 1], nmax[:, par], nmax_hi[:, par].bitcast(F32), ALU.subtract)\
                    .then_inc(lead_done, 1)

            def collect(grp, h):
                n = grp * GH + h
                b, j = h // HG, h % HG
                rows_j, cols = slice(DH * j, DH * j + DH), slice(b * T, (b + 1) * T)
                dve.wait_ge(o_half_done, n + 1)
                tt(oT_all[rows_j, bass.ds(grp + 1, 1), cols].squeeze(1), o_half[0:DH, h % 2], pv_bank[2 * DH:3 * DH, :],
                   ALU.add)
                tt(sums[rows_j, b, :], o_half[DH:2 * DH, h % 2], pv_bank[3 * DH:P, :], ALU.add).then_inc(pv_read, 1)

            def divide(grp, part4, body_grp):
                w = B * T // 4
                cols = slice(part4 * w, (part4 + 1) * w)
                den = sums[:, :, :].rearrange("p b t -> p (b t)")[:, cols]
                dve.wait_ge(pv_read, grp * GH + (GH // B * (part4 // 2 + 1) + 2))
                nc.vector.reciprocal(den, den).then_inc(recip_done, 1)
                dve.wait_ge(recip_done, body_grp * 4 + ((part4 + 2) % 4 + 1))
                to = oT_all[:, bass.ds(grp + 1, 1), cols].squeeze(1)
                tt(to, to, den, ALU.mult).then_inc(oT_done, 1)

            def body(grp, part):
                for s in range(GH):
                    if has(part, s + S_AHEAD):
                        maxima(grp, s + S_AHEAD, 0)
                    if has(part, s):
                        collect(grp, s)
                    if has(part, s + S_AHEAD):
                        maxima(grp, s + S_AHEAD, 1)
                        halve(grp, s + S_AHEAD, part)
                    if part != "first" and s == 1:
                        divide(grp - 1, 2, grp)
                        divide(grp - 1, 3, grp)
                    if part != "first" and s == 3:
                        divide(grp, 0, grp)
                        divide(grp, 1, grp)
                    if has(part):
                        if s == 0 and part == "mid":
                            w_low(grp + 1)
                        if s in (1, 2):
                            qk_low(s - 1, grp + 1)
                        if s == 3 and part == "first":
                            nc.vector.memset(v_one[:, :, :, DH:], 1.0)
                            nc.vector.memset(sums[:, :, :], 1.0)
                            nc.vector.memset(oT_all[:, 0, :], 1.0)

            body(-1, "first")
            with dve.Fori(0, NGRP - 1) as grp:
                body(grp, "mid")
            dve.wait_ge(wo_hi_done, 1)
            nc.vector.tensor_tensor(wo_lo[:, :, :], wo_raw[:, :, :], wo_hi[:, :, :].bitcast(F32), ALU.subtract)\
                .then_inc(wo_lo_done, 1)
            body(NGRP - 1, "last")
            def o_low(t):
                dve.wait_ge(o_hi_done, t + 1)
                nc.vector.tensor_tensor(o_lo[:, t % 2], oT[:, :, t * P:(t + 1) * P], o_hi[:, t % 2].bitcast(F32),
                                        ALU.subtract).then_inc(o_lo_done, 1)

            def attended(t):
                dve.wait_ge(wo_done, t + 1)
                dve.wait_ge(y_bo_done, t + 1)
                nc.vector.tensor_tensor(xa[:, t], bank[t % 4], y_bo[:, t], ALU.add).then_inc(wo_read, 1)
                dve.wait_ge(wo_read, t + 1)

            def residual3(tiles):
                stt = nc.vector.scalar_tensor_tensor
                link([stt(xa[:, t], xa[:, t], mv3[:, t, 0:1], row_in[:, 1], ALU.subtract, ALU.mult)
                      for t in tiles][-1])
                link([stt(tok[:, t], xa[:, t], rstd3[:, t:t + 1], tok[:, t], ALU.mult, ALU.add)
                      for t in tiles][-1])

            def normal4(b):
                scale(rstd4, b, std4, b + 1)
                for t in range(b * TT, (b + 1) * TT):
                    ts(xg[:, t], tok[:, t], mv4[:, t, 0:1], rstd4[:, t:t + 1], ALU.subtract, ALU.mult)\
                        .then_inc(z_done, 1)

            dve.wait_ge(gamma_done, 1)
            o_low(0)
            for t in range(NT):
                if t + 1 < NT:
                    o_low(t + 1)
                attended(t)
                if t < 2:
                    divide(NGRP - 1, t + 2, NGRP)
                if t == TT:
                    layer_stats(0, mv3, xa, var3, 0.0)
                if t == NT - 2:
                    scale(rstd3, 0, std3, 1)
                if t >= NT - 2:
                    residual3((2 * (t - NT + 2), 2 * (t - NT + 2) + 1))
            layer_stats(0, mv4, tok, var4)
            layer_stats(1, mv3, xa, var3, 0.0)
            normal4(0)
            scale(rstd3, 1, std3, 2)
            residual3(range(TT, NT))
            layer_stats(1, mv4, tok, var4)
            normal4(1)

            dec = rcst[:, 0:E].unsqueeze(1).to_broadcast([P, NT, E])
            dve.wait_ge(router_in, 48)
            dve.wait_ge(logit_done, NT)
            link(nc.vector.tensor_copy(logit[:, :, :], bank[0][:, 0:NT * E].rearrange("p (t e) -> p t e", e=E)))
            link(nc.vector.tensor_reduce(best[:, :], logit[:, :, :], AX.X, ALU.max))
            link(tt(hot2[:, :, :], logit[:, :, :], best[:, :].unsqueeze(2).to_broadcast([P, NT, E]), ALU.is_ge))
            link(tt(hot2[:, :, :], hot2[:, :, :], dec, ALU.mult))
            link(nc.vector.tensor_reduce(best[:, :], hot2[:, :, :], AX.X, ALU.max))
            link(tt(hot[:, :, :], dec, best[:, :].unsqueeze(2).to_broadcast([P, NT, E]), ALU.is_equal))
            link(nc.vector.memset(before[:, 0], 0.0))
            for t in range(NT):
                link(tt(before[:, t + 1], before[:, t], hot[:, t], ALU.add))
            nc.vector.memset(base[:, 0:1], 0.0).then_inc(hot_done, 1)
            dve.wait_ge(ranked, 1)
            link(nc.vector.tensor_copy(count[:, :], bank[2][:, 0:E]))
            link(tt(over[:, :, :], count[:, :].unsqueeze(2).to_broadcast([P, E, E]),
                    rcst[:, E:2 * E].unsqueeze(1).to_broadcast([P, E, E]), ALU.is_gt))
            link(nc.vector.tensor_reduce(blocks[:, :], over[:, :, :], AX.X, ALU.add))
            for e in range(1, E):
                link(tt(base[:, e:e + 1], base[:, e - 1:e], blocks[:, e - 1:e], ALU.add))
            link(nc.vector.scalar_tensor_tensor(
                place_f[:, :, :], base[:, :].unsqueeze(1).to_broadcast([P, NT, E]), float(P),
                bank[1][:, 0:NT * E].rearrange("p (t e) -> p t e", e=E), ALU.mult, ALU.add))
            link(tt(place_f[:, :, :], place_f[:, :, :], hot[:, :, :], ALU.mult))
            link(nc.vector.tensor_reduce(slot_f[:, :], place_f[:, :, :], AX.X, ALU.add))
            nc.vector.tensor_copy(slot_i[:, :], slot_f[:, :]).then_inc(routed, 1)
            link(tt(at_b[:, :, :], base[:, :].unsqueeze(1).to_broadcast([P, NB, E]),
                    rcst[:, 2 * E:].unsqueeze(2).to_broadcast([P, NB, E]), ALU.is_le))
            link(nc.vector.tensor_reduce(blk[:, :], at_b[:, :, :], AX.X, ALU.add))
            link(tt(blocks_all[:, :], base[:, E - 1:E], blocks[:, E - 1:E], ALU.add))
            link(ts(used_f[:, :], rcst[:, 2 * E:], blocks_all[:, :], None, ALU.is_lt))
            link(nc.vector.memset(new_f[:, 0:1], 1.0))
            link(tt(new_f[:, 1:], blk[:, 1:], blk[:, :NB - 1], ALU.not_equal))
            link(nc.vector.tensor_copy(used_i[:, :], used_f[:, :]))
            link(tt(new_i[:, :], new_f[:, :], used_f[:, :], ALU.mult))
            ts(blk_i[:, :], blk[:, :], -1.0, None, ALU.add).then_inc(routed, 1)
            dve.wait_ge(routed, 2)

            def low(b, pc):
                dve.wait_ge(half_hi_done, piece_no(b, pc))
                tt(half_lo[pc][:, :], raw[pc][:, :], half_hi[pc][:, :].bitcast(F32), ALU.subtract)\
                    .then_inc(half_lo_done, 1)

            def low_if(b, pc, new):
                if new is None:
                    return low(b, pc)
                with dve.If(new):
                    low(b, pc)
                with dve.Else():
                    count_on(dve, half_lo_done, piece_no(b, pc) - 1, 1)

            def zb_low(b):
                dve.wait_ge(zb_hi_done, b + 1)
                tt(zbT_lo[:, :, :], turn_bank.rearrange("p (k t) -> p k t", k=KT), zbT_hi[:, :, :].bitcast(F32),
                   ALU.subtract).then_inc(zb_lo_done, 1)

            def hid_low(q, c):
                dve.wait_ge(hT_hi_done, q + 1)
                tt(hT_lo[:, 0:CH[c]], turn_bank[:, 0:CH[c] * P].rearrange("p (i t) -> p i t", t=P),
                   hT_hi[:, 0:CH[c]].bitcast(F32), ALU.subtract).then_inc(hT_lo_done, 1)

            for pc in SPLIT_FIRST[:2]:
                low(0, pc)
            zb_low(0)
            for pc in SPLIT_FIRST[2:]:
                low(0, pc)

            def body(b, first=False, last=False):
                new_now = None if first else flag(dve, new_i, b)
                new_next = None if last else flag(dve, new_i, b + 1)
                for c in range(3):
                    if not (first and c == 0):
                        hid_low(b * 3 + (c - 1), (c - 1) % 3)
                    for n, (pc, ahead) in enumerate(SPLITS[c]):
                        if n == 1:
                            dve.wait_ge(silu_done, b * 3 + (c + 1))
                            dve.wait_ge(up_done, b * 3 + (c + 1))
                            tt(hid[:, 0:CH[c] * P], sil[:, 0:CH[c] * P], u_bank[c][:, 0:CH[c] * P], ALU.mult)\
                                .then_inc(hid_done, 1)
                        if n == 2 and c == 2 and not last:
                            zb_low(b + 1)
                        if not (last and ahead):
                            low_if(b + ahead, pc, (new_now, new_next)[ahead])

            def end(b):
                with dve.If(flag(dve, used_i, b)):
                    hid_low(b * 3 + 2, 2)

            def tail_body(b, last=False):
                with dve.If(flag(dve, used_i, b)):
                    body(b, last=last)
                    dve.wait_ge(routed, 2)
                with dve.Else():
                    end(b - 1)
                    dve.wait_ge(routed, 2)

            body(0, first=True)
            with dve.Fori(1, USED) as b:
                body(b)
            with dve.Fori(USED, NB - 1) as b:
                tail_body(b)
            tail_body(NB - 1, last=True)
            end(NB - 1)
            for t in range(NT):
                dve.wait_ge(gathered[t], 16)
                tt(res[:, t], res[:, t], tok[:, t], ALU.add).then_inc(summed, 1)

        @block.tensor
        def _(pe):
            pe.wait_ge(consts_in, 16)

            def norm_turn(t):
                pe.wait_ge(normed, t + 1)
                for k in range(KT):
                    mm = nc.tensor.transpose(norm_bank[t][:, k * P:(k + 1) * P],
                                             norm[:, t % 2, k * P:(k + 1) * P], ident[:, :])
                mm.then_inc(norm_turned, 1)

            for t in range(TT):
                norm_turn(t)
            pe.sem_inc(g_free, GRING)
            pe.wait_ge(zero_set, 1)

            def first(n, j, b):
                pe.wait_ge(cT_lo_done, n + 1)
                toks = slice(b * T, (b + 1) * T)
                for k in range(KT):
                    for q, (w, v) in enumerate(((cT_hi, xT_hi), (cT_hi, xT_lo), (cT_lo, xT_hi))):
                        mm = nc.tensor.matmul(h_bank[j % 4], w[:, j, k], v[:, k, toks],
                                              start=(k == 0 and q == 0), stop=(k == KT - 1 and q == 2))
                mm.then_inc(h_done, 1)

            def second(n, j, last=False):
                pe.wait_ge(cN_lo_done, n + 1)
                pe.wait_ge(g_lo_done, n + 1)
                for t in range(TT):
                    ts = slice(t * P, (t + 1) * P)
                    for q, (w, v) in enumerate(((g_hi, cN_hi), (g_hi, cN_lo), (g_lo, cN_hi))):
                        mm = nc.tensor.matmul(o_bank[t], w[:, j % GRING, ts], v[:, j],
                                              start=False, stop=(last and q == 2), skip_group_check=True)
                mm.then_inc(g_free, 1)

            pe.wait_ge(turn_lo, TT)
            for j in range(PE_LAG):
                first(j, j, 0)
            for t in range(TT, NT):
                norm_turn(t)
            pe.wait_ge(turn_lo, NT)
            per = NF // RING // B
            for b in range(B):
                if b:
                    pe.wait_ge(o_read, b * TT)
                for t in range(TT):
                    nc.tensor.matmul(o_bank[t], zero[:, 0:P], zero[:, :], start=True, stop=False,
                                     skip_group_check=True)
                with pe.Fori(b * per, (b + 1) * per - 1) as i:
                    for j in range(RING):
                        first(i * RING + (j + PE_LAG), (j + PE_LAG) % RING, b)
                        second(i * RING + j, j)
                n0 = ((b + 1) * per - 1) * RING
                for j in range(RING):
                    if n0 + j + PE_LAG < NF:
                        first(n0 + j + PE_LAG, (j + PE_LAG) % RING, (n0 + j + PE_LAG) // (NF // B))
                    second(n0 + j, j, j == RING - 1)

            def y_turn(t):
                pe.wait_ge(y_ready, t + 1)
                for k in range(KT):
                    mm = nc.tensor.transpose(input_bank[t][:, k * P:(k + 1) * P],
                                             ynorm[:, t % 4, k * P:(k + 1) * P], ident[:, :])
                mm.then_inc(norm_turned, 1)

            pe.sem_inc(pv_done, 1)
            pe.sem_inc(pv_read, 2)

            def pair_free(grp, what, part):
                before = nth(grp, what, part) - 1
                if not (isinstance(before, int) and before == 0):
                    pe.wait_ge(pair_read[PAIR[what]], before)

            def project(m, grp, part, batches=range(B)):
                what = "QKV"[m]
                pair_free(grp, what, part)
                pe.wait_ge(w_lo_done, (grp + 1) * 2 + 2)
                for b in batches:
                    toks = slice(b * T, (b + 1) * T)
                    for k in range(KT):
                        for q, (w, v) in enumerate(((w_hi, yT_hi), (w_hi, yT_lo), (w_lo, yT_hi))):
                            mm = nc.tensor.matmul(pair[PAIR[what]][:, b, :], w[:, m, k], v[:, k, toks],
                                                  start=(k == 0 and q == 0), stop=(k == KT - 1 and q == 2))
                if b == B - 1:
                    mm.then_inc(proj_done, 1)

            def scores(grp, h, p, part):
                b, j = h % GH // HG, h % HG
                if b == 0 and p == 0:
                    pe.wait_ge(stack_in[j], (grp + h // GH) * 96 + 96)
                pair_free(grp, ("S", h, p), part)
                for q in range(2):
                    at = b * T + (2 * p + q) * P
                    mm = nc.tensor.matmul(pair[PAIR["S", h, p]][:, q, :], q_st[0:ROW0, j, at:at + P],
                                          k_st[0:ROW0, j, b * T:(b + 1) * T], start=True, stop=True)
                mm.then_inc(s_done, 1)

            def lead_turn(grp, h):
                n = grp * GH + h
                pe.wait_ge(lead_done, n + 1)
                if not (isinstance(n, int) and n == 0):
                    pe.wait_ge(shift_done, n)
                for q in range(TT):
                    mm = nc.tensor.matmul(lead_bank[ROW0:P, q * P:(q + 1) * P], lead[:, h % 2, q, :], ident[:, :],
                                          start=True, stop=True)
                mm.then_inc(lead_turned, 1)

            def scores_by_keys(grp, h, part):
                b, j = h % GH // HG, h % HG
                pe.wait_ge(shift_done, grp * GH + (h + 1))
                if part == "first":
                    pe.wait_ge(ones_done, 1)
                for p in range(2):
                    pair_free(grp, ("T", h, p), part)
                    for k in range(2):
                        at = b * T + (2 * p + k) * P
                        mm = nc.tensor.matmul(pair[PAIR["T", h, p]][:, k, :], k_st[:, j, at:at + P],
                                              q_st[:, j, b * T:(b + 1) * T], start=True, stop=True)
                    mm.then_inc(t_done, 1)

            def output(grp, h, part):
                n = grp * GH + h
                b, j = h // HG, h % HG
                if h == 0:
                    pe.wait_ge(pair_read[PAIR["T", GH, 1]], nth_last_t(grp))
                    pe.wait_ge(pair_read[PAIR["turn"]], nth(grp, "turn", part))
                else:
                    pe.wait_ge(pair_read[PAIR["T", h, 1]], nth(grp, ("T", h, 1), part))
                pe.wait_ge(pv_read, n + 2)
                for k in range(TT):
                    half = slice(k % 2 * 2 * DH, k % 2 * 2 * DH + 2 * DH)
                    mm = nc.tensor.matmul(pv_bank[half, :], v_one[:, b * TT + k, j], probT[:, h % 2, k, :],
                                          start=(k < 2), stop=(k >= TT - 2))
                mm.then_inc(pv_done, 1)

            def v_turn(grp, part):
                pair_free(grp, "turn", part)
                for m in range(NT):
                    mm = nc.tensor.transpose(pair[PAIR["turn"]][:, m // TT, (m % TT) * P:(m % TT + 1) * P],
                                             vT[:, m * P:(m + 1) * P], ident[:, :])
                mm.then_inc(v_turned, 1)

            def body(grp, part):
                for s in range(GH):
                    if s == 0 and part != "first":
                        v_turn(grp, part)
                    if has(part, s + T_AHEAD):
                        scores_by_keys(grp, s + T_AHEAD, part)
                    if has(part, s):
                        output(grp, s, part)
                    if has(part, s + S_AHEAD - 1):
                        lead_turn(grp, s + S_AHEAD - 1)
                    if has(part, s + S_AHEAD):
                        for p in range(2):
                            scores(grp, s + S_AHEAD, p, part)
                    if part == "mid" and s in (1, 2, 3):
                        project(s - 1, grp, part)
                if has(part):
                    pe.wait_ge(pair_read[PAIR["V"]], nth(grp, "V", part))

            for b in range(B):
                for t in range(b * TT, (b + 1) * TT):
                    y_turn(t)
                pe.wait_ge(turn_lo, NT + (b + 1) * TT)
                for m in range(3):
                    project(m, -1, "first", [b])
            body(-1, "first")
            with pe.Fori(0, NGRP - 1) as grp:
                body(grp, "mid")
            body(NGRP - 1, "last")

            pe.wait_ge(wo_lo_done, 1)
            for t in range(NT):
                pe.wait_ge(o_lo_done, t + 1)
                if t >= 4:
                    pe.wait_ge(wo_read, t - 3)
                for k in range(KT):
                    for q, (w, v) in enumerate(((o_hi, wo_hi), (o_hi, wo_lo), (o_lo, wo_hi))):
                        mm = nc.tensor.matmul(bank[t % 4], w[:, t % 2, k], v[:, k],
                                              start=(k == 0 and q == 0), stop=(k == KT - 1 and q == 2))
                mm.then_inc(wo_done, 1)

            def z_turn(t):
                pe.wait_ge(z_done, t + 1)
                if t >= 4:
                    pe.wait_ge(zT_done, t - 3)
                for k in range(KT):
                    mm = nc.tensor.transpose(h_bank[t % 4][:, k * P:(k + 1) * P], xg[:, t, k * P:(k + 1) * P],
                                             ident[:, :])
                mm.then_inc(z_turned, 1)

            z_turn(0)
            pe.wait_ge(router_in, 48)
            for t in range(NT):
                if t + 1 < NT:
                    z_turn(t + 1)
                pe.wait_ge(zT_done, t + 1)
                for k in range(KT):
                    mm = nc.tensor.matmul(bank[0][:, t * E:(t + 1) * E], zT[:, t % 2, k], rw[:, k],
                                          start=(k == 0), stop=(k == KT - 1))
                mm.then_inc(logit_done, 1)
            pe.wait_ge(hot_done, 1)
            nc.tensor.matmul(bank[1][:, 0:NT * E], tri_one[:, 0], hot[:, :, :], start=True, stop=False)
            nc.tensor.matmul(bank[1][:, 0:NT * E], tri_one[:, 1], before[:, 0:NT, :], start=False, stop=True)
            nc.tensor.matmul(bank[2][:, 0:E], tri_one[:, 1], before[:, NT, :], start=True, stop=True)\
                .then_inc(ranked, 1)

            def zb_turn(b):
                pe.wait_ge(zb_in, b * 16 + 16)
                for k in range(KT):
                    mm = nc.tensor.transpose(turn_bank[:, k * P:(k + 1) * P], zb[:, k * P:(k + 1) * P], ident[:, :])
                mm.then_inc(zb_turned, 1)

            def up(b, what, c, to, done):
                w = CH[c] * P
                pe.wait_ge(half_lo_done, piece_no(b, (what, c)))
                hi, lo = half_hi[what, c], half_lo[what, c]
                for k in range(KT):
                    ks = slice(k * w, (k + 1) * w)
                    for q, (z, v) in enumerate(((zbT_hi, hi), (zbT_hi, lo), (zbT_lo, hi))):
                        mm = nc.tensor.matmul(to[:, 0:w], z[:, k], v[:, ks], start=(k == 0 and q == 0),
                                              stop=(k == KT - 1 and q == 2))
                mm.then_inc(done, 1)

            def hid_turn(q, c):
                pe.wait_ge(hid_done, q + 1)
                for i in range(CH[c]):
                    mm = nc.tensor.transpose(turn_bank[:, i * P:(i + 1) * P], hid[:, i * P:(i + 1) * P], ident[:, :])
                mm.then_inc(hid_turned, 1)

            def down(b, q, c):
                pe.wait_ge(hT_lo_done, q + 1)
                pe.wait_ge(half_lo_done, piece_no(b, ("d", c)))
                hi, lo = half_hi["d", c], half_lo["d", c]
                for i in range(CH[c]):
                    cols = slice(i * D, (i + 1) * D)
                    for n, (h, v) in enumerate(((hT_hi, hi), (hT_hi, lo), (hT_lo, hi))):
                        mm = nc.tensor.matmul(y_bank, h[:, i], v[:, cols], start=(c == 0 and i == 0 and n == 0),
                                              stop=(c == 2 and i == CH[c] - 1 and n == 2), skip_group_check=True)
                mm.then_inc(down_done, 1)

            zb_turn(0)

            def body(b, first=False, last=False):
                for c in range(3):
                    if c == 0:
                        pe.wait_ge(zb_lo_done, b + 1)
                    up(b, "g", c, g_bank[c], gate_done)
                    if not (first and c == 0):
                        hid_turn(b * 3 + (c - 1), (c - 1) % 3)
                    up(b, "u", c, u_bank[c], up_done)
                    if c == 2 and not last:
                        pe.wait_ge(hT_lo_done, b * 3 + 2)
                        zb_turn(b + 1)
                    if c == 1 and not first:
                        pe.wait_ge(y_read, b)
                    if not (first and c == 0):
                        down(b - 1 if c == 0 else b, b * 3 + (c - 1), (c - 1) % 3)

            def end(b, last=False):
                with pe.If(flag(pe, used_i, b)):
                    if not last:
                        pe.wait_ge(zb_lo_done, b + 2)
                    hid_turn(b * 3 + 2, 2)
                    down(b, b * 3 + 2, 2)

            def tail_body(b, last=False):
                with pe.If(flag(pe, used_i, b)):
                    body(b, last=last)
                with pe.Else():
                    end(b - 1)
                    pe.wait_ge(routed, 2)

            body(0, first=True)
            with pe.Fori(1, USED) as b:
                body(b)
            with pe.Fori(USED, NB - 1) as b:
                tail_body(b)
            tail_body(NB - 1, last=True)
            end(NB - 1, last=True)


def kernel(**inputs):
    import concourse.bacc as _bacc
    from concourse.bass_utils import run_bass_kernel_spmd as _run

    a = {k: np.ascontiguousarray(v) for k, v in inputs.items()}
    ctx = a["ctx_1024"].reshape(B * NG, GT * P, D)
    even = np.arange(0, D, 2, dtype=np.float32)
    power = np.power(np.float32(10000.0), (np.float32(2.0) * even / np.float32(D)).astype(np.float32))
    pos = (np.arange(TT)[None, :] * P + np.arange(P)[:, None]).astype(np.float32)
    row = np.concatenate([E - np.arange(E), P * np.arange(E), np.arange(NB)]).astype(np.float32)
    consts = np.concatenate([np.eye(P, dtype=np.float32), pos, np.broadcast_to(power, (P, D // 2)),
                             np.triu(np.ones((P, P), np.float32), 1), np.ones((P, P), np.float32),
                             np.broadcast_to(row, (P, row.size))], axis=1)
    gate, up = (a["L0_ffn_" + w].reshape(E, FF, KT, P).transpose(0, 3, 2, 1) for w in ("gate_w", "up_w"))
    down = a["L0_ffn_down_w"].reshape(E, D, FT, P).transpose(0, 3, 2, 1)
    edges = np.cumsum([0] + CH)
    ffn = [np.stack([gate[..., lo * P:hi * P].reshape(E, P, -1), up[..., lo * P:hi * P].reshape(E, P, -1),
                     down[:, :, lo:hi].reshape(E, P, -1)], axis=1) for lo, hi in zip(edges, edges[1:])]
    att = lambda w: a["L0_attn_" + w]
    w_qkv = np.stack([att(w) for w in ("Wq", "Wk", "Wv")]).reshape(3, NGRP, P, KT, P).transpose(1, 4, 0, 3, 2)
    arrays = {
        "x": a["x"].reshape(B * T, D),
        "ctx_nat": ctx.reshape(B * NG, GT, P, D).transpose(0, 2, 1, 3),
        "ctx_tr": ctx.reshape(B * NG, GT * P, KT, P).transpose(0, 3, 2, 1),
        "consts": consts,
        "rby": att("rby"),
        "w_qkv": w_qkv,
        "b_qkv": np.stack([att(w) for w in ("bq", "bk", "bv")]).reshape(3, NGRP, P).transpose(2, 0, 1),
        "w_o": att("Wo").reshape(D, KT, P).transpose(2, 1, 0),
        "rows": np.stack([att(w) for w in ("bo", "ln_gamma", "ln_beta")]),
        "router": a["L0_ffn_router_w"].reshape(E, KT, P).transpose(2, 1, 0),
        "ffn0": ffn[0],
        "ffn1": ffn[1],
        "ffn2": ffn[2],
    }
    arrays = {k: np.ascontiguousarray(v) for k, v in arrays.items()}
    nc = _bacc.Bacc("TRN2", target_bir_lowering=False, num_devices=1)
    args = [nc.dram_tensor(k, v.shape, mybir.dt.from_np(v.dtype), kind="ExternalInput").ap()
            for k, v in arrays.items()]
    args.append(nc.dram_tensor("y", (B * T, D), F32, kind="ExternalOutput").ap())
    build(nc, *args)
    r = _run(nc, [arrays], core_ids=[0])
    return r.results[0]["y"].reshape(B, T, D)
```
